# Optimizing a Trainium2 kernel written in Bass

```python
import numpy as np
import jax
import jax.numpy as jnp

def _softmax(x, axis=-1):
    return jax.nn.softmax(x, axis=axis)

def _gelu(x):
    return jax.nn.gelu(x, approximate=True)

def _silu(x):
    return jax.nn.silu(x)

def _sigmoid(x):
    return jax.nn.sigmoid(x)

def _layernorm(x, axis=-1, eps=1e-05):
    m = jnp.mean(x, axis=axis, keepdims=True)
    v = jnp.var(x, axis=axis, keepdims=True)
    return (x - m) / jnp.sqrt(v + eps)

def _scatter_add(tgt, idx, src, axis=0):
    return tgt.at[idx].add(src)

def _segment_sum(src, seg, n):
    return jax.ops.segment_sum(src, seg, n)
kernel_name = 'mk_flamingo_gated_d4_seqx_r4_7f4ec8'

def setup_inputs(seed: int=0):
    np.random.seed(seed)
    _w = jnp.asarray

    def _rec_inputs():
        import jax
        import jax.numpy as jnp
        _rk = jax.random.key(seed)
        x = -0.0002928 + 1 * jax.random.normal(jax.random.fold_in(_rk, 1), (4, 512, 256), jnp.float32)
        _lenS = 512 - jax.random.randint(jax.random.fold_in(_rk, 7), (4,), 0, max(1, 512 // 4) + 1, jnp.int32)
        _lenS2 = 1601 - jax.random.randint(jax.random.fold_in(_rk, 8), (4,), 0, max(1, 1601 // 4) + 1, jnp.int32)
        _ctx_1024P = jax.random.normal(jax.random.fold_in(_rk, 11), (4, 16, 256), jnp.float32)
        _ctx_1024c = jax.random.dirichlet(jax.random.fold_in(_rk, 511), 0.3 * jnp.ones((16,), jnp.float32), (4, 1601))
        _ctx_1024t = jnp.einsum('bsk,bkd->bsd', _ctx_1024c, _ctx_1024P)
        _ctx_1024t = _ctx_1024t * jax.lax.rsqrt(jnp.mean(jnp.square(_ctx_1024t)) + 1e-12) * 0.953939
        ctx_1024 = -0.000191848 + 0.999787 * (_ctx_1024t + 0.3 * jax.random.normal(jax.random.fold_in(_rk, 611), (4, 1601, 256), jnp.float32))
        _validS = jnp.arange(512)[None, :] < _lenS[:, None]
        _validS2 = jnp.arange(1601)[None, :] < _lenS2[:, None]
        _causal = jnp.tril(jnp.ones((512, 512), dtype=bool))
        mask_Bx1x1xS2_if1 = jnp.where(jnp.ones((4, 1, 1, 1601), dtype=bool), 1, 0).astype(jnp.int32)
        _g = jax.random.normal(jax.random.fold_in(_rk, 9001), (2, 4), jnp.float32)
        _g = jnp.sign(_g) * jnp.maximum(jnp.abs(_g), 1.0) + (_g == 0) * 1.0
        g_xattn = _g[0]
        g_ffn = _g[1]
        return (x, ctx_1024, mask_Bx1x1xS2_if1, g_xattn, g_ffn)
    x, ctx_1024, mask_Bx1x1xS2_if1, g_xattn, g_ffn = _rec_inputs()

    def _L0_xattn_setup():
        import jax, jax.numpy as jnp
        import numpy as np
        D_MODEL = 256
        NUM_HEADS = 16
        DEPTH = D_MODEL // NUM_HEADS
        key = jax.random.key(seed)
        ks = jax.random.split(key, 10)
        B, T, C = (2, 512, 768)
        s = 1.0 / np.sqrt(D_MODEL)
        inp = {'x': jax.random.normal(ks[0], (B, T, D_MODEL), dtype=jnp.float32), 'context': jax.random.normal(ks[1], (B, C, D_MODEL), dtype=jnp.float32), 'Wq': jax.random.normal(ks[2], (D_MODEL, D_MODEL), dtype=jnp.float32) * s, 'bq': jnp.zeros((D_MODEL,), dtype=jnp.float32), 'Wk': jax.random.normal(ks[3], (D_MODEL, D_MODEL), dtype=jnp.float32) * s, 'bk': jnp.zeros((D_MODEL,), dtype=jnp.float32), 'Wv': jax.random.normal(ks[4], (D_MODEL, D_MODEL), dtype=jnp.float32) * s, 'bv': jnp.zeros((D_MODEL,), dtype=jnp.float32), 'Wo': jax.random.normal(ks[5], (D_MODEL, D_MODEL), dtype=jnp.float32) * s, 'bo': jnp.zeros((D_MODEL,), dtype=jnp.float32)}
        return inp
    _L0_xattn_all = _L0_xattn_setup()
    _L0_xattn_in = {k: v for k, v in _L0_xattn_all.items() if k in ('Wq', 'bq', 'Wk', 'bk', 'Wv', 'bv', 'Wo', 'bo')}
    del _L0_xattn_all

    def _L0_ffn_setup():
        import jax, jax.numpy as jnp
        import numpy as np
        IN_FEATURES = 256
        ACT_BITS = 4

        def _hadamard(size: int) -> np.ndarray:
            h = np.array([[1.0]], dtype=np.float64)
            while h.shape[0] < size:
                h = np.block([[h, h], [h, -h]])
            return (h / np.sqrt(size)).astype(np.float32)

        def _quantize_activations(x, bits=ACT_BITS):
            pos = 2 ** (bits - 1) - 1
            neg = 2 ** (bits - 1)
            scale = jnp.clip(jnp.max(jnp.abs(jax.lax.stop_gradient(x)), axis=-1, keepdims=True), 1e-05) / pos
            q = jnp.clip(jnp.round(x / scale), -neg, pos) * scale
            return x + jax.lax.stop_gradient(q - x)

        def _ternary_quantize_ste(w):
            scale = jnp.clip(jnp.mean(jnp.abs(jax.lax.stop_gradient(w)), axis=1, keepdims=True), 1e-05)
            n = w / scale
            tern = jnp.where(n > 0.5, 1.0, jnp.where(n < -0.5, -1.0, 0.0))
            q = tern * scale
            return w + jax.lax.stop_gradient(q - w)
        key = jax.random.key(seed)
        k1, k2 = jax.random.split(key)
        x = jax.random.normal(k1, (8, 2048, IN_FEATURES), dtype=jnp.float32)
        bound = 1.0 / np.sqrt(IN_FEATURES)
        weight = jax.random.uniform(k2, (256, IN_FEATURES), dtype=jnp.float32, minval=-bound, maxval=bound)
        return {'x': x, 'weight': weight}
    _L0_ffn_all = _L0_ffn_setup()
    _L0_ffn_in = {k: v for k, v in _L0_ffn_all.items() if k in ('weight',)}
    del _L0_ffn_all

    def _L1_xattn_setup():
        import jax, jax.numpy as jnp
        import numpy as np
        EMBED_DIM = 256
        NUM_HEADS = 16
        HEAD_DIM = EMBED_DIM // NUM_HEADS
        ROPE_BASE = 10000.0

        def _rope_cos_sin(seq_len, dim):
            inv_freq = 1.0 / ROPE_BASE ** (jnp.arange(0, dim, 2, dtype=jnp.float32) / dim)
            freqs = jnp.arange(seq_len, dtype=jnp.float32)[:, None] * inv_freq[None, :]
            emb = jnp.concatenate([freqs, freqs], axis=-1)
            return (jnp.cos(emb), jnp.sin(emb))

        def _rotate_half(x):
            d = x.shape[-1] // 2
            return jnp.concatenate([-x[..., d:], x[..., :d]], axis=-1)
        key = jax.random.key(seed)
        ks = jax.random.split(key, 12)
        B, S, E = (2, 512, EMBED_DIM)
        s = 1.0 / np.sqrt(E)
        return {'query': jax.random.normal(ks[0], (B, S, E), jnp.float32), 'key': jax.random.normal(ks[1], (B, S, E), jnp.float32), 'value': jax.random.normal(ks[2], (B, S, E), jnp.float32), 'mask': jnp.ones((B, 1, 1, S), jnp.int32), 'Wq': jax.random.normal(ks[3], (E, E), jnp.float32) * s, 'bq': jnp.zeros((E,), jnp.float32), 'Wk': jax.random.normal(ks[4], (E, E), jnp.float32) * s, 'bk': jnp.zeros((E,), jnp.float32), 'Wv': jax.random.normal(ks[5], (E, E), jnp.float32) * s, 'bv': jnp.zeros((E,), jnp.float32), 'Wo': jax.random.normal(ks[6], (E, E), jnp.float32) * s, 'bo': jnp.zeros((E,), jnp.float32)}
    _L1_xattn_all = _L1_xattn_setup()
    _L1_xattn_in = {k: v for k, v in _L1_xattn_all.items() if k in ('Wq', 'bq', 'Wk', 'bk', 'Wv', 'bv', 'Wo', 'bo')}
    del _L1_xattn_all

    def _L1_ffn_setup():
        import jax, jax.numpy as jnp
        import numpy as np
        B, S, H, E, DFF = (4, 1024, 256, 8, 1024)
        key = jax.random.key(seed)
        k0, k1, k2, k3 = jax.random.split(key, 4)
        hidden_states = jax.random.normal(k0, (B, S, H), dtype=jnp.float32)
        gate_w = jax.random.normal(k1, (E, H), dtype=jnp.float32) * 0.02
        w1 = jax.random.normal(k2, (E, H, DFF), dtype=jnp.float32) * 0.02
        b1 = jnp.zeros((E, DFF), dtype=jnp.float32)
        w2 = jax.random.normal(k3, (E, DFF, H), dtype=jnp.float32) * 0.02
        b2 = jnp.zeros((E, H), dtype=jnp.float32)
        return {'hidden_states': hidden_states, 'gate_w': gate_w, 'w1': w1, 'b1': b1, 'w2': w2, 'b2': b2}
    _L1_ffn_all = _L1_ffn_setup()
    _L1_ffn_in = {k: v for k, v in _L1_ffn_all.items() if k in ('gate_w', 'w1', 'b1', 'w2', 'b2')}
    del _L1_ffn_all

    def _L2_xattn_setup():
        import jax, jax.numpy as jnp
        import numpy as np
        M, T, D, H = (2, 512, 256, 16)
        HD = D // H
        SCALE = 1.0 / np.sqrt(D).astype(np.float32)
        key = jax.random.key(seed)
        ks = jax.random.split(key, 8)

        def lin(k):
            kw, kb = jax.random.split(k)
            W = jax.random.normal(kw, (D, D), dtype=jnp.float32) * (1.0 / np.sqrt(D))
            b = jax.random.normal(kb, (D,), dtype=jnp.float32) * 0.01
            return (W, b)
        Wq, bq = lin(ks[0])
        Wk, bk = lin(ks[1])
        Wv, bv = lin(ks[2])
        Wo, bo = lin(ks[3])
        Q = jax.random.normal(ks[4], (M, T, D), dtype=jnp.float32)
        K = jax.random.normal(ks[5], (M, T, D), dtype=jnp.float32)
        V = jax.random.normal(ks[6], (M, T, D), dtype=jnp.float32)
        mask = jnp.ones((M, 1, 1, T), dtype=jnp.int32)
        return {'Q': Q, 'K': K, 'V': V, 'mask': mask, 'Wq': Wq, 'bq': bq, 'Wk': Wk, 'bk': bk, 'Wv': Wv, 'bv': bv, 'Wo': Wo, 'bo': bo}
    _L2_xattn_all = _L2_xattn_setup()
    _L2_xattn_in = {k: v for k, v in _L2_xattn_all.items() if k in ('Wq', 'bq', 'Wk', 'bk', 'Wv', 'bv', 'Wo', 'bo')}
    del _L2_xattn_all

    def _L2_ffn_setup():
        import jax, jax.numpy as jnp
        import numpy as np
        key = jax.random.key(seed)
        ks = jax.random.split(key, 4)
        B, T, M, E, F = (4, 512, 256, 8, 1024)
        hidden_states = jax.random.normal(ks[0], (B, T, M), dtype=jnp.float32)
        wg = jax.random.normal(ks[1], (M, E), dtype=jnp.float32) * (1.0 / np.sqrt(M))
        w1 = jax.random.normal(ks[2], (E, M, F), dtype=jnp.float32) * (1.0 / np.sqrt(M))
        b1 = jnp.zeros((E, F), dtype=jnp.float32)
        w2 = jax.random.normal(ks[3], (E, F, M), dtype=jnp.float32) * (1.0 / np.sqrt(F))
        b2 = jnp.zeros((E, M), dtype=jnp.float32)
        return {'hidden_states': hidden_states, 'wg': wg, 'w1': w1, 'b1': b1, 'w2': w2, 'b2': b2}
    _L2_ffn_all = _L2_ffn_setup()
    _L2_ffn_in = {k: v for k, v in _L2_ffn_all.items() if k in ('wg', 'w1', 'b1', 'w2', 'b2')}
    del _L2_ffn_all

    def _L3_xattn_setup():
        import jax, jax.numpy as jnp
        import numpy as np
        D_MODEL = 256
        key = jax.random.key(seed)
        ks = jax.random.split(key, 11)
        B, Sq, Skv, D = (16, 512, 512, D_MODEL)
        s = 1.0 / np.sqrt(D)
        return {'q': jax.random.normal(ks[0], (B, Sq, D), jnp.float32), 'k': jax.random.normal(ks[1], (B, Skv, D), jnp.float32), 'v': jax.random.normal(ks[2], (B, Skv, D), jnp.float32), 'Wq': jax.random.normal(ks[3], (D, D), jnp.float32) * s, 'bq': jnp.zeros((D,), jnp.float32), 'Wk': jax.random.normal(ks[4], (D, D), jnp.float32) * s, 'bk': jnp.zeros((D,), jnp.float32), 'Wv': jax.random.normal(ks[5], (D, D), jnp.float32) * s, 'bv': jnp.zeros((D,), jnp.float32), 'Wo': jax.random.normal(ks[6], (D, D), jnp.float32) * s, 'bo': jnp.zeros((D,), jnp.float32)}
    _L3_xattn_all = _L3_xattn_setup()
    _L3_xattn_in = {k: v for k, v in _L3_xattn_all.items() if k in ('Wq', 'bq', 'Wk', 'bk', 'Wv', 'bv', 'Wo', 'bo')}
    del _L3_xattn_all

    def _L3_ffn_setup():
        import jax, jax.numpy as jnp
        import numpy as np
        B, S, H, F, E, K = (2, 512, 256, 1024, 8, 2)

        def _init_w(key, shape, fan_in):
            return jax.random.normal(key, shape, jnp.float32) * fan_in ** (-0.5)

        def _ffn(x, wi, bi, wo, bo):
            return jax.nn.selu(x @ wi + bi) @ wo + bo
        key = jax.random.key(seed)
        ks = jax.random.split(key, 6)
        return {'x': jax.random.normal(ks[0], (B, S, H), jnp.float32), 'gate_wi': _init_w(ks[1], (H, F), H), 'gate_bi': jnp.zeros((F,), jnp.float32), 'gate_wo': _init_w(ks[2], (F, H), F), 'gate_bo': jnp.zeros((H,), jnp.float32), 'exp_wi': _init_w(ks[3], (E, H, F), H), 'exp_bi': jnp.zeros((E, F), jnp.float32), 'exp_wo': _init_w(ks[4], (E, F, H), F), 'exp_bo': jnp.zeros((E, H), jnp.float32)}
    _L3_ffn_all = _L3_ffn_setup()
    _L3_ffn_in = {k: v for k, v in _L3_ffn_all.items() if k in ('gate_wi', 'gate_bi', 'gate_wo', 'gate_bo', 'exp_wi', 'exp_bi', 'exp_wo', 'exp_bo')}
    del _L3_ffn_all
    return {'x': x, 'ctx_1024': ctx_1024, 'mask_Bx1x1xS2_if1': mask_Bx1x1xS2_if1, 'g_xattn': g_xattn, 'g_ffn': g_ffn, 'L0_xattn_Wq': _L0_xattn_in['Wq'], 'L0_xattn_bq': _L0_xattn_in['bq'], 'L0_xattn_Wk': _L0_xattn_in['Wk'], 'L0_xattn_bk': _L0_xattn_in['bk'], 'L0_xattn_Wv': _L0_xattn_in['Wv'], 'L0_xattn_bv': _L0_xattn_in['bv'], 'L0_xattn_Wo': _L0_xattn_in['Wo'], 'L0_xattn_bo': _L0_xattn_in['bo'], 'L0_ffn_weight': _L0_ffn_in['weight'], 'L1_xattn_Wq': _L1_xattn_in['Wq'], 'L1_xattn_bq': _L1_xattn_in['bq'], 'L1_xattn_Wk': _L1_xattn_in['Wk'], 'L1_xattn_bk': _L1_xattn_in['bk'], 'L1_xattn_Wv': _L1_xattn_in['Wv'], 'L1_xattn_bv': _L1_xattn_in['bv'], 'L1_xattn_Wo': _L1_xattn_in['Wo'], 'L1_xattn_bo': _L1_xattn_in['bo'], 'L1_ffn_gate_w': _L1_ffn_in['gate_w'], 'L1_ffn_w1': _L1_ffn_in['w1'], 'L1_ffn_b1': _L1_ffn_in['b1'], 'L1_ffn_w2': _L1_ffn_in['w2'], 'L1_ffn_b2': _L1_ffn_in['b2'], 'L2_xattn_Wq': _L2_xattn_in['Wq'], 'L2_xattn_bq': _L2_xattn_in['bq'], 'L2_xattn_Wk': _L2_xattn_in['Wk'], 'L2_xattn_bk': _L2_xattn_in['bk'], 'L2_xattn_Wv': _L2_xattn_in['Wv'], 'L2_xattn_bv': _L2_xattn_in['bv'], 'L2_xattn_Wo': _L2_xattn_in['Wo'], 'L2_xattn_bo': _L2_xattn_in['bo'], 'L2_ffn_wg': _L2_ffn_in['wg'], 'L2_ffn_w1': _L2_ffn_in['w1'], 'L2_ffn_b1': _L2_ffn_in['b1'], 'L2_ffn_w2': _L2_ffn_in['w2'], 'L2_ffn_b2': _L2_ffn_in['b2'], 'L3_xattn_Wq': _L3_xattn_in['Wq'], 'L3_xattn_bq': _L3_xattn_in['bq'], 'L3_xattn_Wk': _L3_xattn_in['Wk'], 'L3_xattn_bk': _L3_xattn_in['bk'], 'L3_xattn_Wv': _L3_xattn_in['Wv'], 'L3_xattn_bv': _L3_xattn_in['bv'], 'L3_xattn_Wo': _L3_xattn_in['Wo'], 'L3_xattn_bo': _L3_xattn_in['bo'], 'L3_ffn_gate_wi': _L3_ffn_in['gate_wi'], 'L3_ffn_gate_bi': _L3_ffn_in['gate_bi'], 'L3_ffn_gate_wo': _L3_ffn_in['gate_wo'], 'L3_ffn_gate_bo': _L3_ffn_in['gate_bo'], 'L3_ffn_exp_wi': _L3_ffn_in['exp_wi'], 'L3_ffn_exp_bi': _L3_ffn_in['exp_bi'], 'L3_ffn_exp_wo': _L3_ffn_in['exp_wo'], 'L3_ffn_exp_bo': _L3_ffn_in['exp_bo']}

def reference(x, ctx_1024, mask_Bx1x1xS2_if1, g_xattn, g_ffn, L0_xattn_Wq, L0_xattn_bq, L0_xattn_Wk, L0_xattn_bk, L0_xattn_Wv, L0_xattn_bv, L0_xattn_Wo, L0_xattn_bo, L0_ffn_weight, L1_xattn_Wq, L1_xattn_bq, L1_xattn_Wk, L1_xattn_bk, L1_xattn_Wv, L1_xattn_bv, L1_xattn_Wo, L1_xattn_bo, L1_ffn_gate_w, L1_ffn_w1, L1_ffn_b1, L1_ffn_w2, L1_ffn_b2, L2_xattn_Wq, L2_xattn_bq, L2_xattn_Wk, L2_xattn_bk, L2_xattn_Wv, L2_xattn_bv, L2_xattn_Wo, L2_xattn_bo, L2_ffn_wg, L2_ffn_w1, L2_ffn_b1, L2_ffn_w2, L2_ffn_b2, L3_xattn_Wq, L3_xattn_bq, L3_xattn_Wk, L3_xattn_bk, L3_xattn_Wv, L3_xattn_bv, L3_xattn_Wo, L3_xattn_bo, L3_ffn_gate_wi, L3_ffn_gate_bi, L3_ffn_gate_wo, L3_ffn_gate_bo, L3_ffn_exp_wi, L3_ffn_exp_bi, L3_ffn_exp_wo, L3_ffn_exp_bo):
    import jax
    import jax.numpy as jnp

    def _L0_xattn_ref(x, context, Wq, bq, Wk, bk, Wv, bv, Wo, bo):
        import jax, jax.numpy as jnp
        import numpy as np
        D_MODEL = 256
        NUM_HEADS = 16
        DEPTH = D_MODEL // NUM_HEADS
        B, T, D = x.shape
        C = context.shape[1]
        H, d = (NUM_HEADS, DEPTH)
        q = x @ Wq.T + bq
        k = context @ Wk.T + bk
        v = context @ Wv.T + bv
        q = q.reshape(B, T, H, d).transpose(0, 2, 1, 3)
        k = k.reshape(B, C, H, d).transpose(0, 2, 1, 3)
        v = v.reshape(B, C, H, d).transpose(0, 2, 1, 3)
        scores = jnp.einsum('bhtd,bhcd->bhtc', q, k) / jnp.sqrt(jnp.asarray(d, x.dtype))
        attn = jax.nn.softmax(scores, axis=-1)
        out = jnp.einsum('bhtc,bhcd->bhtd', attn, v)
        out = out.transpose(0, 2, 1, 3).reshape(B, T, D)
        return out @ Wo.T + bo

    def _L0_ffn_ref(x, weight):
        import jax, jax.numpy as jnp
        import numpy as np
        IN_FEATURES = 256
        ACT_BITS = 4

        def _hadamard(size: int) -> np.ndarray:
            h = np.array([[1.0]], dtype=np.float64)
            while h.shape[0] < size:
                h = np.block([[h, h], [h, -h]])
            return (h / np.sqrt(size)).astype(np.float32)

        def _quantize_activations(x, bits=ACT_BITS):
            pos = 2 ** (bits - 1) - 1
            neg = 2 ** (bits - 1)
            scale = jnp.clip(jnp.max(jnp.abs(jax.lax.stop_gradient(x)), axis=-1, keepdims=True), 1e-05) / pos
            q = jnp.clip(jnp.round(x / scale), -neg, pos) * scale
            return x + jax.lax.stop_gradient(q - x)

        def _ternary_quantize_ste(w):
            scale = jnp.clip(jnp.mean(jnp.abs(jax.lax.stop_gradient(w)), axis=1, keepdims=True), 1e-05)
            n = w / scale
            tern = jnp.where(n > 0.5, 1.0, jnp.where(n < -0.5, -1.0, 0.0))
            q = tern * scale
            return w + jax.lax.stop_gradient(q - w)
        H = jnp.asarray(_hadamard(IN_FEATURES))
        xh = x @ H
        xq = _quantize_activations(xh)
        wq = _ternary_quantize_ste(weight)
        return jnp.einsum('bsi,oi->bso', xq, wq)

    def _L1_xattn_ref(query, key, value, mask, Wq, bq, Wk, bk, Wv, bv, Wo, bo):
        import jax, jax.numpy as jnp
        import numpy as np
        EMBED_DIM = 256
        NUM_HEADS = 16
        HEAD_DIM = EMBED_DIM // NUM_HEADS
        ROPE_BASE = 10000.0

        def _rope_cos_sin(seq_len, dim):
            inv_freq = 1.0 / ROPE_BASE ** (jnp.arange(0, dim, 2, dtype=jnp.float32) / dim)
            freqs = jnp.arange(seq_len, dtype=jnp.float32)[:, None] * inv_freq[None, :]
            emb = jnp.concatenate([freqs, freqs], axis=-1)
            return (jnp.cos(emb), jnp.sin(emb))

        def _rotate_half(x):
            d = x.shape[-1] // 2
            return jnp.concatenate([-x[..., d:], x[..., :d]], axis=-1)
        B, Sq, E = query.shape
        Sk = key.shape[1]
        H, D = (NUM_HEADS, HEAD_DIM)
        q = (query @ Wq + bq).reshape(B, Sq, H, D)
        k = (key @ Wk + bk).reshape(B, Sk, H, D)
        v = (value @ Wv + bv).reshape(B, Sk, H, D)
        cos, sin = _rope_cos_sin(max(Sq, Sk), D)
        cq, sq_ = (cos[:Sq][None, :, None, :], sin[:Sq][None, :, None, :])
        ck, sk_ = (cos[:Sk][None, :, None, :], sin[:Sk][None, :, None, :])
        q = q * cq + _rotate_half(q) * sq_
        k = k * ck + _rotate_half(k) * sk_
        scores = jnp.einsum('bqhd,bkhd->bhqk', q, k) / jnp.sqrt(jnp.float32(D))
        scores = jnp.where(mask == 0, jnp.float32(-1e+30), scores)
        attn = jax.nn.softmax(scores, axis=-1)
        ctx = jnp.einsum('bhqk,bkhd->bqhd', attn, v).reshape(B, Sq, E)
        return ctx @ Wo + bo

    def _L1_ffn_ref(hidden_states, gate_w, w1, b1, w2, b2):
        import jax, jax.numpy as jnp
        import numpy as np
        B, S, H, E, DFF = (4, 1024, 256, 8, 1024)
        b, s, h = hidden_states.shape
        x = hidden_states.reshape(-1, h)
        gate_logits = x @ gate_w.T
        gate_probs = jax.nn.softmax(gate_logits, axis=-1)
        expert_idx = jnp.argmax(gate_probs, axis=-1)
        expert_w = jnp.take_along_axis(gate_probs, expert_idx[:, None], axis=1)[:, 0]
        out = jnp.zeros_like(x)
        n_experts = w1.shape[0]
        for e in range(n_experts):
            ye = jax.nn.relu(x @ w1[e] + b1[e]) @ w2[e] + b2[e]
            sel = (expert_idx == e)[:, None]
            out = out + jnp.where(sel, ye * expert_w[:, None], 0.0)
        return out.reshape(b, s, h)

    def _L2_xattn_ref(Q, K, V, mask, Wq, bq, Wk, bk, Wv, bv, Wo, bo):
        import jax, jax.numpy as jnp
        import numpy as np
        M, T, D, H = (2, 512, 256, 16)
        HD = D // H
        SCALE = 1.0 / np.sqrt(D).astype(np.float32)
        m = Q.shape[0]
        q = (Q @ Wq.T + bq).reshape(m, -1, H, HD)
        k = (K @ Wk.T + bk).reshape(m, -1, H, HD)
        v = (V @ Wv.T + bv).reshape(m, -1, H, HD)
        energy = jnp.einsum('mqhd,mkhd->mhqk', q, k) * SCALE
        if mask is not None:
            energy = jnp.where(mask == 0, jnp.float32(-1e+20), energy)
        attn = jax.nn.softmax(energy, axis=3)
        out = jnp.einsum('mhqk,mkhd->mqhd', attn, v)
        concat = out.reshape(m, -1, H * HD)
        return concat @ Wo.T + bo

    def _L2_ffn_ref(hidden_states, wg, w1, b1, w2, b2):
        import jax, jax.numpy as jnp
        import numpy as np
        B, T, M = hidden_states.shape
        E = wg.shape[1]
        S = B * T
        MIN_CAPACITY = 4
        C = max((S + E - 1) // E, MIN_CAPACITY)
        x = hidden_states.reshape(S, M)
        logits = x @ wg
        gates = jax.nn.softmax(logits, axis=-1)
        idx = jnp.argmax(gates, axis=-1)
        mask1 = jax.nn.one_hot(idx, E, dtype=gates.dtype)
        l_aux = jnp.sum(gates.mean(0) * mask1.mean(0)) * E
        locations1 = jnp.cumsum(mask1, axis=0) - 1.0
        mask1 = mask1 * (locations1 < C)
        gates1_s = jnp.sum(gates * mask1, axis=1)
        loc_s = jnp.sum(locations1 * mask1, axis=1).astype(jnp.int32)
        loc_sc = jax.nn.one_hot(loc_s, C, dtype=gates.dtype)
        combine_weights = jnp.einsum('se,sc->sec', gates1_s[:, None] * mask1, loc_sc)
        dispatch_mask = (combine_weights > 0).astype(x.dtype)
        dispatched = jnp.einsum('sec,sm->ecm', dispatch_mask, x)
        h = jax.nn.gelu(jnp.einsum('ecm,emf->ecf', dispatched, w1) + b1[:, None, :])
        expert_out = jnp.einsum('ecf,efm->ecm', h, w2) + b2[:, None, :]
        out = jnp.einsum('sec,ecm->sm', combine_weights, expert_out)
        return out.reshape(B, T, M)

    def _L3_xattn_ref(q, k, v, Wq, bq, Wk, bk, Wv, bv, Wo, bo):
        import jax, jax.numpy as jnp
        import numpy as np
        D_MODEL = 256
        D = q.shape[-1]
        query = q @ Wq + bq
        key_p = k @ Wk + bk
        value = v @ Wv + bv
        scores = jnp.einsum('bqd,bkd->bqk', query / jnp.sqrt(jnp.float32(D)), key_p)
        attn = jax.nn.softmax(scores, axis=-1)
        out = jnp.einsum('bqk,bkd->bqd', attn, value)
        return out @ Wo + bo

    def _L3_ffn_ref(x, gate_wi, gate_bi, gate_wo, gate_bo, exp_wi, exp_bi, exp_wo, exp_bo):
        import jax, jax.numpy as jnp
        import numpy as np
        B, S, H, F, E, K = (2, 512, 256, 1024, 8, 2)

        def _init_w(key, shape, fan_in):
            return jax.random.normal(key, shape, jnp.float32) * fan_in ** (-0.5)

        def _ffn(x, wi, bi, wo, bo):
            return jax.nn.selu(x @ wi + bi) @ wo + bo
        Bb, Ss, Hh = x.shape
        xf = x.reshape(-1, Hh)
        gate_logits = _ffn(xf, gate_wi, gate_bi, gate_wo, gate_bo)
        topv, topi = jax.lax.top_k(gate_logits, K)
        topv = topv / jnp.sum(topv, axis=-1, keepdims=True)
        onehot = (topi[..., None] == jnp.arange(E)).astype(x.dtype)
        w = jnp.einsum('nk,nke->ne', topv, onehot)
        h = jax.nn.selu(jnp.einsum('nh,ehf->enf', xf, exp_wi) + exp_bi[:, None, :])
        out_e = jnp.einsum('enf,efh->enh', h, exp_wo) + exp_bo[:, None, :]
        out = jnp.einsum('enh,ne->nh', out_e, w)
        return out.reshape(Bb, Ss, Hh)
    x = x + jnp.tanh(g_xattn[0]) * _L0_xattn_ref(_layernorm(x, axis=-1), ctx_1024, L0_xattn_Wq, L0_xattn_bq, L0_xattn_Wk, L0_xattn_bk, L0_xattn_Wv, L0_xattn_bv, L0_xattn_Wo, L0_xattn_bo)
    x = x + jnp.tanh(g_ffn[0]) * _L0_ffn_ref(_layernorm(x, axis=-1), L0_ffn_weight)
    x = x + jnp.tanh(g_xattn[1]) * _L1_xattn_ref(_layernorm(x, axis=-1), ctx_1024, ctx_1024, mask_Bx1x1xS2_if1, L1_xattn_Wq, L1_xattn_bq, L1_xattn_Wk, L1_xattn_bk, L1_xattn_Wv, L1_xattn_bv, L1_xattn_Wo, L1_xattn_bo)
    x = x + jnp.tanh(g_ffn[1]) * _L1_ffn_ref(_layernorm(x, axis=-1), L1_ffn_gate_w, L1_ffn_w1, L1_ffn_b1, L1_ffn_w2, L1_ffn_b2)
    x = x + jnp.tanh(g_xattn[2]) * _L2_xattn_ref(_layernorm(x, axis=-1), ctx_1024, ctx_1024, mask_Bx1x1xS2_if1, L2_xattn_Wq, L2_xattn_bq, L2_xattn_Wk, L2_xattn_bk, L2_xattn_Wv, L2_xattn_bv, L2_xattn_Wo, L2_xattn_bo)
    x = x + jnp.tanh(g_ffn[2]) * _L2_ffn_ref(_layernorm(x, axis=-1), L2_ffn_wg, L2_ffn_w1, L2_ffn_b1, L2_ffn_w2, L2_ffn_b2)
    x = x + jnp.tanh(g_xattn[3]) * _L3_xattn_ref(_layernorm(x, axis=-1), ctx_1024, ctx_1024, L3_xattn_Wq, L3_xattn_bq, L3_xattn_Wk, L3_xattn_bk, L3_xattn_Wv, L3_xattn_bv, L3_xattn_Wo, L3_xattn_bo)
    x = x + jnp.tanh(g_ffn[3]) * _L3_ffn_ref(_layernorm(x, axis=-1), L3_ffn_gate_wi, L3_ffn_gate_bi, L3_ffn_gate_wo, L3_ffn_gate_bo, L3_ffn_exp_wi, L3_ffn_exp_bi, L3_ffn_exp_wo, L3_ffn_exp_bo)
    return x

_drawn_inputs = setup_inputs


def setup_inputs(seed=0):
    import zlib

    import numpy as np

    out = dict(_drawn_inputs(seed))
    spreads = {'L0_xattn_bq': (0.0, 0.1),
     'L0_xattn_bk': (0.0, 2.0),
     'L0_xattn_bv': (0.0, 0.1),
     'L0_xattn_bo': (0.0, 0.1),
     'L1_xattn_bq': (0.0, 0.319),
     'L1_xattn_bk': (0.0, 0.407),
     'L1_xattn_bv': (0.0, 0.1),
     'L1_xattn_bo': (0.0, 0.1),
     'L1_ffn_b1': (0.0, 0.492),
     'L1_ffn_b2': (0.0, 0.289),
     'L2_ffn_b1': (0.0, 0.333),
     'L2_ffn_b2': (0.0, 0.1),
     'L3_xattn_bq': (0.0, 0.378),
     'L3_xattn_bk': (0.0, 2.0),
     'L3_xattn_bv': (0.0, 0.1),
     'L3_xattn_bo': (0.0, 0.1),
     'L3_ffn_gate_bi': (0.0, 0.1),
     'L3_ffn_gate_bo': (0.0, 0.1),
     'L3_ffn_exp_bi': (0.0, 0.8),
     'L3_ffn_exp_bo': (0.0, 0.8)}
    factors = {'g_ffn': 8.0,
     'L2_xattn_bq': 33.191,
     'L2_xattn_bk': 64.0,
     'L2_xattn_bv': 3.561,
     'L2_xattn_bo': 3.596}
    for name, (base, spread) in spreads.items():
        noise = np.random.default_rng([zlib.crc32(name.encode()), seed]).standard_normal(out[name].shape)
        drawn = base * np.exp(spread * noise) if base else spread * noise
        out[name] = jnp.asarray(drawn.astype(out[name].dtype))
    for name, factor in factors.items():
        out[name] = (out[name] * factor).astype(out[name].dtype)
    return out
```

```python
from contextlib import ExitStack, contextmanager

import numpy as np

import concourse.bass as bass
import concourse.mybir as mybir

F32, BF16, I32 = mybir.dt.float32, mybir.dt.bfloat16, mybir.dt.int32
U32 = mybir.dt.uint32
ALU, ACT, AX = mybir.AluOpType, mybir.ActivationFunctionType, mybir.AxisListType

B, T, D, S2 = 4, 512, 256, 1601
N = B * T
H, HD = 16, 16
NE, FF = 8, 1024
P = 128
TT = T // P
NT = N // P
DC = D // P
FC = FF // P
KT = -(-S2 // P)
KW = [min(P, S2 - P * k) for k in range(KT)]
MOST = 2 * N // P + NE - 1
EPS = 1e-5


class Tick:

    def __init__(self, stream, scope, base, local):
        self.stream, self.scope, self.base, self.local = stream, scope, base, local


class LastRound(Tick):
    pass


class Scope:

    def __init__(self, index, count, per):
        self.index, self.count, self.per = index, count, per


class Stream:

    def __init__(self, prog, name, step=1):
        self.prog, self.name, self.step = prog, name, step
        self.sem = prog.ctx.enter_context(prog.nc.semaphore(name))
        self.base, self.local = 0, 0
        prog.streams.append(self)

    def now(self):
        return Tick(self, self.prog.scope, self.base, self.local)

    def after(self, instruction):
        instruction.then_inc(self.sem, self.step)
        self.local += self.step
        return self.now()


class Engine:

    def __init__(self, prog, name, eng):
        self.prog, self.eng = prog, eng
        self.done = Stream(prog, f"{name}_done")
        self.seen, self.pending = {}, []

    def wait(self, *ticks):
        todo = [w for w in map(self.value, ticks) if w is not None]
        if self is self.prog.sp:
            self.pending += todo
            return
        for sem, v in todo:
            self.eng.wait_ge(sem, v)

    def flush(self):
        todo = [(sem, v if isinstance(v, int) else self.eng.to_reg(v)) for sem, v in self.pending]
        self.pending = []
        for sem, v in todo:
            self.eng.wait_ge(sem, v)

    def dma(self, stream, out, in_):
        self.flush()
        return stream.after(self.eng.dma_start(out, in_))

    def value(self, t):
        if t is None:
            return None
        scope, s = self.prog.scope, t.stream
        if isinstance(t, LastRound):
            per = scope.per.get(s.name, 1)
            back = t.local - per
            if t.base + back <= 0:
                back = 0
            assert t.base > 0 and back <= 0, (s.name, t.base, t.local, per)
            return s.sem, scope.index * per + (t.base + back)
        if t.scope is not None and scope is None:
            total = t.base + (t.scope.count - 1) * t.scope.per.get(s.name, 1) + t.local
        else:
            assert t.scope is None or t.scope is scope
            total = t.base + t.local
        key = (s.name, scope, t.scope)
        if self.seen.get(key, 0) >= total:
            return None
        self.seen[key] = total
        if t.scope is not None and scope is not None:
            return s.sem, scope.index * scope.per.get(s.name, 1) + total
        return s.sem, total

    def do(self, instruction):
        return self.done.after(instruction)

    def seq(self, instruction):
        t = self.do(instruction)
        self.wait(t)
        return t


class Program:
    def __init__(self, nc, ctx, loops):
        self.nc, self.ctx, self.loops = nc, ctx, loops
        self.scope, self.streams, self.n_loops, self.measured = None, [], 0, []
        self.pe = Engine(self, "pe", nc.tensor)
        self.act = Engine(self, "act", nc.scalar)
        self.dve = Engine(self, "dve", nc.vector)
        self.pool = Engine(self, "pool", nc.gpsimd)
        self.sp = Engine(self, "sp", nc.sync)
        self.engines = [self.pe, self.act, self.dve, self.pool, self.sp]
        self.n_names = 0
        self.rings, self.kept = [], {}

    def sbuf(self, ctx, name, shape, dt=F32):
        self.n_names += 1
        return ctx.enter_context(self.nc.sbuf_tensor(f"{name}_{self.n_names}", shape, dt))

    def psum(self, ctx, name, shape, dt=F32):
        self.n_names += 1
        return ctx.enter_context(self.nc.psum_tensor(f"{name}_{self.n_names}", shape, dt))

    def stream(self, name, step=16):
        self.n_names += 1
        return Stream(self, f"{name}_{self.n_names}", step)

    @contextmanager
    def loop(self, count):
        n = self.n_loops
        self.n_loops += 1
        per = self.loops[n] if n < len(self.loops) else {}
        for s in self.streams:
            s.base, s.local = s.base + s.local, 0
        made = len(self.streams)
        for r in self.rings:
            r.enter(per)
        self.sp.flush()
        self.kept = {}
        with self.nc.Fori(0, count) as index:
            self.scope = Scope(index, count, per)
            yield index
            for r in self.rings:
                r.leave()
            assert not self.sp.pending
        self.scope = None
        assert made == len(self.streams)
        self.measured.append({s.name: s.local for s in self.streams if s.local} | self.kept)
        for s in self.streams:
            s.base, s.local = s.base + count * s.local, 0

    def keep(self, name, tick):
        self.kept["@" + name] = (tick.stream.name, tick.local)

    def last_round(self, name):
        if "@" + name not in self.scope.per:
            return None
        where, local = self.scope.per["@" + name]
        s = next(s for s in self.streams if s.name == where)
        return LastRound(s, self.scope, s.base, local)

    def barrier(self):
        for e in self.engines:
            if e.done.base + e.done.local:
                for other in self.engines:
                    other.wait(e.done.now())


class Ring:

    def __init__(self, prog, name, slots):
        self.prog, self.name, self.slots = prog, name, slots
        self.n, self.freed = 0, [None] * len(slots)
        prog.rings.append(self)

    def take(self):
        i = self.n % len(self.slots)
        self.n += 1
        self.prog.pe.wait(self.freed[i])
        return i, self.slots[i]

    def free(self, i, tick):
        self.freed[i] = tick

    def enter(self, per):
        self.prog.pe.wait(*self.freed)
        self.n, self.freed = 0, [None] * len(self.slots)
        for i in range(len(self.slots)):
            if f"@{self.name}{i}" in per:
                where, local = per[f"@{self.name}{i}"]
                s = next(s for s in self.prog.streams if s.name == where)
                self.freed[i] = LastRound(s, None, s.base, local)

    def leave(self):
        for i, t in enumerate(self.freed):
            if t is not None and not isinstance(t, LastRound):
                self.prog.keep(f"{self.name}{i}", t)


def normalised(pg, x, xnT, cst, psum, keep=None):
    nc, pe, act, dve, pool = pg.nc, pg.pe, pg.act, pg.dve, pg.pool
    pg.barrier()
    G = 4
    with ExitStack() as ctx:
        stats = pg.sbuf(ctx, "stats", [P, NT, 6])
        mv, rstd = cst["mv"], cst["rstd"]
        xn = pg.sbuf(ctx, "xn", [P, G, D])
        ring = Ring(pg, f"t_ring{pg.n_names}", [p[:] for p in psum])
        for n in range(NT):
            dve.do(nc.vector.bn_stats(stats[:, n, :], x[:, n, :]))
        dve.wait(dve.done.now())
        for n in range(NT):
            dve.do(nc.vector.bn_aggr(mv[:, n, :], stats[:, n, :]))
        dve.wait(dve.done.now())
        t = dve.do(nc.vector.tensor_scalar(rstd[:], mv[:, :, 1], EPS, None, ALU.add))
        pool.wait(t)
        t = pool.do(nc.gpsimd.tensor_tensor(rstd[:], rstd[:], cst["mhalf"][:, 0:NT], ALU.pow))
        dve.wait(t)
        uid = pg.n_names
        used = None
        with pg.loop(NT // G) as i:
            dve.wait(pg.last_round(f"xn{uid}"))
            for g in range(G):
                n = bass.ds(i * G + g, 1)
                t = dve.do(nc.vector.tensor_scalar(
                    xn[:, g, :], x[:, n, :].rearrange("p a n -> p (a n)"), mv[:, n, 0:1].rearrange("p a n -> p (a n)"),
                    rstd[:, n], ALU.subtract, ALU.mult))
                pe.wait(t)
                if keep is not None:
                    keep(i * G + g, xn[:, g, :], t)
                k, slot = ring.take()
                for c in range(DC):
                    m = nc.tensor.transpose(slot[:, P * c:P * c + P], xn[:, g, P * c:P * c + P], cst["ident"][:])
                used = pe.do(m)
                act.wait(used)
                t = act.do(nc.scalar.copy(xnT[:, :, bass.ds((i * G + g) * P, P)],
                                          slot[:, 0:D].rearrange("p (c n) -> p c n", c=DC)))
                ring.free(k, t)
            pg.keep(f"xn{uid}", used)
        done = act.done.now()
        pe.wait(done)
        dve.wait(done, pe.done.now())
        pg.rings.remove(ring)
    return done


SLOTS = ((0, 0), (1, 0), (0, 1), (2, 0), (0, 2), (1, 1))
R_MASK = 16 * len(SLOTS)
R_MAX = R_MASK + 1
R_ALL = R_MAX + 3
HG = 4
NG = H // HG
QC = T // P
VW = HD + 1
VG = HG * VW + 32 - VW
PIECE = 400
CHUNKS = [(c, min(512, S2 - c)) for c in range(0, S2, 512)]


def split3(pg, ctx_tiles, src, parts, n, after):
    e = pg.dve
    rest = ctx_tiles
    e.wait(after)
    e.seq(e.eng.tensor_copy(parts[0], src))
    e.seq(e.eng.tensor_tensor(rest, src, parts[0], ALU.subtract))
    e.seq(e.eng.tensor_copy(parts[1], rest))
    return e.do(e.eng.tensor_tensor(parts[2], rest, parts[1], ALU.subtract))


def head_attention(pg, x, xnT, cst, w, gate, scale, rope=None, mask=None):
    nc, pe, act, dve, pool, sp = pg.nc, pg.pe, pg.act, pg.dve, pg.pool, pg.sp
    pg.barrier()
    with ExitStack() as ctx:
        sb = lambda name, shape, dt=F32: pg.sbuf(ctx, name, shape, dt)
        wq, wk, wv = (sb(n, [P, DC, D]) for n in ("wq", "wk", "wv"))
        bq, bk = sb("bq", [P, DC]), sb("bk", [P, DC])
        if rope:
            wqr, wkr = sb("wqr", [P, DC, D]), sb("wkr", [P, DC, D])
            bqr, bkr = sb("bqr", [P, DC]), sb("bkr", [P, DC])
            turn = sb("turn", [P, 2, 2, 512])
        woa = sb("woa", [P, NG, D])
        bva = sb("bva", [P, NG])
        bob = sb("bob", [P, D])
        ctxb = sb("ctxb", [P, 2, DC, 512])
        kf = sb("kf", [P, 2, 512])
        rest = sb("rest", [P, 512])
        ks = sb("ks", [P, 2, DC, 3, 512], BF16)
        kaug = sb("kaug", [P, NG, HG, S2], BF16)
        qaug = sb("qaug", [P, NG, HG, T], BF16)
        v = sb("v", [P, KT, NG, VG])
        v3 = sb("v3", [P, KT, HG, HD])
        e_t = sb("e_t", [P, 2, HG, T])
        mxp = sb("mxp", [P, 2, HG * QC])
        mx = sb("mx", [P, 2, HG * QC])
        nm = sb("nm", [P, P // (HG * QC), HG * QC], BF16)
        tm = sb("tm", [P, P], BF16)
        z, r = sb("z", [P, T]), sb("r", [P, T])
        bvr = z[:].rearrange("p (g n) -> p g n", g=NG)
        ot = sb("ot", [P, NG, T])
        yo = sb("yo", [P, D])

        s_ring = Ring(pg, f"s_ring{pg.n_names}", [pg.psum(ctx, f"s{i}", [P, 512]) for i in range(3)])
        m_ring = Ring(pg, f"m_ring{pg.n_names}", [pg.psum(ctx, f"m{i}", [P, 1024]) for i in range(2)])
        pv = pg.psum(ctx, "pv", [P, T])

        ld = pg.stream("ld")
        row = lambda a: a.rearrange("(c p) n -> p c n", p=P)
        col = lambda a: a.rearrange("(c p) -> p c", p=P)
        load = lambda out, src: sp.dma(ld, out, src)
        for t, n in ((wq, "wq"), (wk, "wk"), (wv, "wv")):
            load(t[:], row(w[n]))
        with nc.allow_non_contiguous_dma("small"):
            load(bq[:], col(w["bq"]))
            load(bk[:], col(w["bk"]))
            if rope:
                for t, n in ((wqr, "wq"), (wkr, "wk")):
                    for c in range(DC):
                        s = w[n][P * c:P * c + P, :].rearrange("p (h a e) -> p h a e", a=2, e=HD // 2)
                        o = t[:, c, :].rearrange("p (h a e) -> p h a e", a=2, e=HD // 2)
                        for a in range(2):
                            load(o[:, :, a, :], s[:, :, 1 - a, :])
                for t, n in ((bqr, "bq"), (bkr, "bk")):
                    for h in range(P // HD):
                        for a in range(2):
                            o = h * HD + a * HD // 2
                            s = h * HD + (1 - a) * HD // 2
                            load(t[o:o + HD // 2, :], w[n].rearrange("(c p) -> p c", p=P)[s:s + HD // 2, :])
            zeroed = [pool.seq(nc.gpsimd.memset(woa[:], 0.0)), pool.seq(nc.gpsimd.memset(bva[:], 0.0))]
            sp.wait(*zeroed)
            for j in range(HG):
                load(woa[32 * j:32 * j + HD, :, :],
                     w["wo"].rearrange("(g j d) n -> j d g n", j=HG, d=HD)[j])
                load(bva[32 * j:32 * j + HD, :], w["bv"].rearrange("(g j d) -> j d g", j=HG, d=HD)[j])
            load(bob[:], w["bo"].rearrange("(a n) -> a n", a=1).to_broadcast([P, D]))
        loaded = ld.now()

        pool.seq(nc.gpsimd.memset(v[:], 0.0))
        pool.wait(pool.done.now())
        v_ones = v[:, :, :, 0:HG * VW].rearrange("p k g (j c) -> p k g j c", c=VW)
        for g in range(NG):
            pool.seq(nc.gpsimd.memset(v_ones[:, :, g, :, HD:VW], 1.0))
        pool.seq(nc.gpsimd.memset(v3[:], 0.0))
        pool.seq(nc.gpsimd.memset(nm[:], 0.0))
        pool.seq(nc.gpsimd.memset(kaug[96:128, :, :, :], 1.0))
        t = pool.seq(nc.gpsimd.memset(qaug[96:128, :, :, :], 1.0))
        pool.wait(t)
        if mask is None:
            pool.seq(nc.gpsimd.memset(kaug[R_MASK:R_MASK + 1, :, :, :], 0.0))
        ready = pool.done.now()

        dve.wait(loaded, ready)
        for g in range(NG):
            dve.do(nc.vector.tensor_scalar(bvr[:, g, :], cst["ones"][:], bva[:, g:g + 1], None, ALU.mult))
        act.wait(loaded)
        pe.wait(loaded, dve.done.now(), ready)
        i, slot = m_ring.take()
        for g in range(NG):
            m = nc.tensor.matmul(slot[:, 0:D], bvr[:, g, :], woa[:, g, :], start=g == 0, stop=g == NG - 1)
        dve.wait(pe.do(m))
        t = dve.seq(nc.vector.tensor_tensor(bob[:], slot[:, 0:D], bob[:], ALU.add))
        m_ring.free(i, t)
        for b_ in (bq, bqr) if rope else (bq,):
            dve.do(nc.vector.tensor_scalar(b_[:], b_[:], scale, None, ALU.mult))
        act.wait(dve.done.now())
        dve.wait(dve.done.now())

        cd = [pg.stream("ctx0"), pg.stream("ctx1")]
        kd = [pg.stream(f"kd{n}") for n in ("01", "2", "3")]
        td = pg.stream("td")
        stored = [pg.stream("stored0"), pg.stream("stored1")]
        rd = [pg.stream("turn0"), pg.stream("turn1")]
        st = dict(kf=[None, None], kfn=0, ctx=[None, None], e=[None, None], en=0, pv=None, z=None,
                  ot=None, k_free=[None] * NG, v3=None, nm=None, staged=[None] * 3, put=[None, None], turn=[None, None])

        def project(nb):
            def evac(slot_i, slot, n, mul, bias, mm):
                f = st["kfn"] % 2
                st["kfn"] += 1
                act.wait(mm, st["kf"][f])
                a = act.do(nc.scalar.activation(kf[:, f, 0:n], slot[:, 0:n], ACT.Identity, bias=bias, scale=mul))
                s_ring.free(slot_i, a)
                return f, a

            def one(wt, wr, rhs, n, c, mul, b0, b1, pos, turn_in, dst, live):
                i, slot = s_ring.take()
                for kc in range(DC):
                    m = nc.tensor.matmul(slot[:, 0:n], wt[:, kc, P * c:P * c + P], rhs(kc),
                                         start=kc == 0, stop=kc == DC - 1)
                f, a = evac(i, slot, n, mul, b0[:, c:c + 1], pe.do(m))
                src = kf[:, f, 0:n]
                dve.wait(a)
                if rope:
                    i, slot = m_ring.take()
                    for kc in range(DC):
                        m = nc.tensor.matmul(slot[:, 0:n], wr[:, kc, P * c:P * c + P], rhs(kc),
                                             start=kc == 0, stop=kc == DC - 1)
                    mm = pe.do(m)
                    dve.wait(turn_in)
                    dve.seq(nc.vector.tensor_tensor(src, src, turn[:, pos, 0, 0:n], ALU.mult))
                    dve.wait(mm)
                    if mul != 1.0:
                        t = dve.seq(nc.vector.tensor_scalar(rest[:, 0:n], slot[:, 0:n], mul, b1[:, c:c + 1],
                                                            ALU.mult, ALU.add))
                        dve.seq(nc.vector.tensor_tensor(rest[:, 0:n], rest[:, 0:n], turn[:, pos, 1, 0:n], ALU.mult))
                    else:
                        t = dve.seq(nc.vector.scalar_tensor_tensor(rest[:, 0:n], slot[:, 0:n], b1[:, c:c + 1],
                                                                   turn[:, pos, 1, 0:n], ALU.add, ALU.mult))
                    m_ring.free(i, t)
                    dve.seq(nc.vector.tensor_tensor(src, src, rest[:, 0:n], ALU.add))
                if live is not None:
                    dve.seq(nc.vector.tensor_scalar(src, src, live, None, ALU.mult))
                t = split3(pg, rest[:, 0:n], src, dst, n, None)
                dve.wait(t)
                st["kf"][f] = t
                return t

            live = mask[1][:, bass.ds(nb, 1)] if mask else None
            sp.wait(*st["staged"])

            def turns(f, c0, n):
                if not rope:
                    return None
                sp.wait(st["turn"][f])
                return sp.dma(rd[f], turn[:, f, :, 0:n], rope[:, :, c0:c0 + n])

            def store(f, name, c0, n):
                st["turn"][f] = dve.done.now()
                sp.wait(dve.done.now())
                for c in range(DC):
                    sp.dma(stored[f], 
                        w[name][:, P * c:P * c + P, c0:c0 + n].rearrange("a p k -> p a k"), ks[:, f, c, :, 0:n])
                st["put"][f] = stored[f].now()

            t_in = turns(0, 0, T)
            dve.wait(st["put"][0])
            for c in range(DC):
                one(wq, wqr if rope else None, lambda kc: xnT[:, kc, bass.ds(nb * T, T)], T, c, scale, bq,
                    bqr if rope else None, 0, t_in, [ks[:, 0, c, k, :] for k in range(3)], live)
            store(0, "qparts", 0, T)
            for n_c, (c0, n) in enumerate(CHUNKS):
                f = (n_c + 1) % 2
                pool.wait(st["ctx"][f])
                arrived = cd[f].after(nc.gpsimd.dma_start(
                    ctxb[:, f, :, 0:n], w["ctxT"][bass.ds(nb, 1), :, c0:c0 + n].rearrange("a (c p) n -> p (a c) n", p=P)))
                t_in = turns(f, c0, n)
                pe.wait(arrived)
                dve.wait(st["put"][f])
                for c in range(DC):
                    one(wk, wkr if rope else None, lambda kc: ctxb[:, f, kc, 0:n], n, c, 1.0, bk,
                        bkr if rope else None, f, t_in, [ks[:, f, c, k, 0:n] for k in range(3)], None)
                store(f, "kparts", c0, n)
                for k in range(c0 // P, -(-(c0 + n) // P)):
                    i, slot = s_ring.take()
                    for kc in range(DC):
                        m = nc.tensor.matmul(slot[0:KW[k], 0:D], ctxb[:, f, kc, k * P - c0:k * P - c0 + KW[k]],
                                             wv[:, kc, :], start=kc == 0, stop=kc == DC - 1)
                    mm = pe.do(m)
                    act.wait(mm, ready, st["v3"])
                    sv = slot[0:KW[k], 0:D].rearrange("p (g j d) -> p g j d", g=NG, j=HG)
                    for g in range(NG - 1):
                        act.do(nc.scalar.copy(v_ones[0:KW[k], k, g, :, 0:HD], sv[:, g, :, :]))
                    t = act.do(nc.scalar.copy(v3[0:KW[k], k, :, :], sv[:, NG - 1, :, :]))
                    s_ring.free(i, t)
                st["ctx"][f] = pe.done.now()
            vals = act.done.now()
            sp.wait(*st["put"])
            out = []
            for n_g, groups in enumerate(((0, 2), (2, 3), (3, 4))):
                sp.wait(*[st["k_free"][g] for g in range(*groups)])
                ka = kaug[:, groups[0]:groups[1], :, :].rearrange("p g j k -> p (g j) k")
                qa = qaug[:, groups[0]:groups[1], :, :].rearrange("p g j k -> p (g j) k")
                h0, h1 = HG * HD * groups[0], HG * HD * groups[1]
                for s, (pq, pk) in enumerate(SLOTS):
                    sp.dma(kd[n_g], 
                        qa[HD * s:HD * s + HD, :, :], w["qparts"][pq, h0:h1, :].rearrange("(h d) k -> d h k", d=HD))
                    sp.dma(kd[n_g], 
                        ka[HD * s:HD * s + HD, :, :], w["kparts"][pk, h0:h1, :].rearrange("(h d) k -> d h k", d=HD))
                if mask:
                    src = mask[0][bass.ds(nb, 1), :]
                    for g in range(*groups):
                        for j in range(HG):
                            sp.dma(kd[n_g], kaug[R_MASK:R_MASK + 1, g, j, :], src)
                out.append(kd[n_g].now())
                if n_g == 1:
                    yield out[0], out[1], vals
            st["staged"] = [out[0], out[1], out[2]]
            yield out[2]

        def max_chunks(g):
            pe.wait(st["arrived"][g])
            for j in range(HG):
                for qc in range(QC):
                    for half in range(2):
                        i, slot = m_ring.take()
                        for k in range(2):
                            k0 = PIECE * (2 * half + k)
                            m = nc.tensor.matmul(slot[:, 512 * k:512 * k + PIECE + 1],
                                                 qaug[0:R_MAX, g, j, P * qc:P * qc + P],
                                                 kaug[0:R_MAX, g, j, k0:k0 + PIECE + 1], start=True, stop=True)
                        dve.wait(pe.do(m))
                        n = j * QC + qc
                        t = dve.do(nc.vector.tensor_reduce(
                            mxp[:, half, n:n + 1], slot[:].rearrange("p (a n) -> p a n", a=2)[:, :, 0:PIECE + 1],
                            AX.XY, ALU.max))
                        m_ring.free(i, t)
                        yield

        def max_rows(g):
            dve.wait(dve.done.now())
            dve.seq(nc.vector.tensor_tensor(mx[:, 0, :], mxp[:, 0, :], mxp[:, 1, :], ALU.max))
            dve.seq(nc.vector.tensor_scalar(mx[:, 0, :], mx[:, 0, :], -1.0, None, ALU.mult))
            t = split3(pg, mx[:, 1, :], mx[:, 0, :], [nm[:, k, :] for k in range(3)], 16, st["nm"])
            i, slot = m_ring.take()
            o = slot[:].bitcast(BF16)[:, 0:P]
            pe.wait(t)
            st["nm"] = pe.do(nc.tensor.transpose(o, nm[:].rearrange("p a n -> p (a n)"), cst["identb"][:]))
            dve.wait(st["nm"], st.get("td"))
            t = dve.do(nc.vector.tensor_copy(tm[:], o))
            m_ring.free(i, t)
            sp.wait(t)
            for k in range(3):
                sp.dma(td, 
                    qaug[R_MAX + k:R_MAX + k + 1, g, :, :].rearrange("a j (c q) -> a (j c) q", q=P),
                    tm[16 * k:16 * k + 16, :])
            st["td"] = td.now()

        def normalise(g):
            i, slot = m_ring.take()
            pe.wait(st["z"])
            t = pe.do(nc.tensor.matmul(slot[:, 0:T], cst["sel"][:], z[:], start=True, stop=True))
            dve.wait(t, st["ot"])
            t = dve.seq(nc.vector.reciprocal(r[:], slot[:, 0:T]))
            m_ring.free(i, t)
            st["norm"] = dve.do(nc.vector.tensor_tensor(ot[:, g, :], z[:], r[:], ALU.mult))

        def attend(g, chunks, before):
            pe.wait(st["td"], st["v3"] if g == NG - 1 else None)

            def values(k, jobs):
                e = st["en"] % 2
                st["en"] += 1
                pe.wait(*jobs)
                if k == 0:
                    pe.wait(st["z"])
                for j in range(HG):
                    m = nc.tensor.matmul(pv[32 * j:32 * j + 32, :], v[0:KW[k], k, g, VW * j:VW * j + 32],
                                         e_t[0:KW[k], e, j, :], start=k == 0, stop=k == KT - 1)
                st["e"][e] = pe.do(m)
            last = None
            for k in range(KT):
                jobs = []
                for j in range(HG):
                    i, slot = s_ring.take()
                    mm = pe.do(nc.tensor.matmul(slot[0:KW[k], :], kaug[0:R_ALL, g, j, P * k:P * k + KW[k]],
                                                qaug[0:R_ALL, g, j, :], start=True, stop=True))
                    e = (st["en"] + (1 if last else 0)) % 2
                    act.wait(mm, st["e"][e] if j == 0 else None)
                    t = act.do(nc.scalar.activation(e_t[0:KW[k], e, j, :], slot[0:KW[k], :], ACT.Exp))
                    s_ring.free(i, t)
                    jobs.append(t)
                    if j > 0:
                        next(chunks, None)
                if k == 1 and before:
                    before()
                if last:
                    values(k - 1, last)
                last = jobs
            st["k_free"][g] = pe.done.now()
            for _ in chunks:
                pass
            values(KT - 1, last)
            dve.wait(st["e"][(st["en"] - 1) % 2], st.get("norm"))
            st["z"] = dve.do(nc.vector.tensor_copy(z[:], pv[:]))

        def output(b):
            for tt in range(TT):
                i, slot = m_ring.take()
                if tt == 0:
                    pe.wait(st["norm"])
                for g in range(NG):
                    m = nc.tensor.matmul(slot[:, 0:D], ot[:, g, P * tt:P * tt + P], woa[:, g, :],
                                         start=g == 0, stop=g == NG - 1)
                dve.wait(pe.do(m), dve.done.now())
                t = dve.seq(nc.vector.tensor_tensor(yo[:], slot[:, 0:D], bob[:], ALU.add))
                m_ring.free(i, t)
                xt = x[:, bass.ds(b * TT + tt, 1), :].rearrange("p a n -> p (a n)")
                dve.do(nc.vector.scalar_tensor_tensor(xt, yo[:], gate, xt, ALU.mult, ALU.add))
            st["ot"] = pe.done.now()

        def batch(b, last):
            for g in range(NG):
                if g < NG - 1:
                    nxt = g + 1
                else:
                    nxt = None if last else 0
                attend(g, max_chunks(nxt) if nxt is not None else iter(()),
                       (lambda: normalise(g - 1)) if g else None)
                if nxt is not None:
                    max_rows(nxt)
                if g == NG - 2 and not last:
                    p = project(b + 1)
                    a, c, vals = next(p)
                    st["arrived"][0] = st["arrived"][1] = a
                    st["arrived"][2] = c
                    st["vals"] = vals
                    st["project"] = p
            normalise(NG - 1)
            output(b)
            if not last:
                sp_done = next(st["project"])
                st["arrived"][3] = sp_done
                act.wait(st["vals"], pe.done.now())
                st["v3"] = act.do(nc.scalar.copy(v_ones[:, :, NG - 1, :, 0:HD], v3[:]))

        st["arrived"] = [None] * NG
        p = project(0)
        a, c, vals = next(p)
        st["arrived"] = [a, a, c, next(p)]
        act.wait(vals)
        st["v3"] = act.do(nc.scalar.copy(v_ones[:, :, NG - 1, :, 0:HD], v3[:]))
        for _ in max_chunks(0):
            pass
        max_rows(0)
        keys = ("z", "ot", "v3", "nm", "td", "norm")

        def all_ticks():
            for key in keys:
                yield key, (lambda t, key=key: st.__setitem__(key, t)), st.get(key)
            for name in ("put", "turn", "kf", "ctx", "e", "arrived", "k_free", "staged"):
                for i, t in enumerate(st[name] or []):
                    yield f"{name}{i}", (lambda t, name=name, i=i: st[name].__setitem__(i, t)), t

        uid = pg.n_names
        for e in pg.engines:
            e.wait(*[t for _, _, t in all_ticks() if t is not None])
        with pg.loop(B - 1) as b:
            st["kfn"] = st["en"] = 0
            names = [n for n, _, _ in all_ticks()]
            for n, put, _ in list(all_ticks()):
                put(pg.last_round(f"{n}@{uid}"))
            batch(b, False)
            for n, _, t in all_ticks():
                if t is not None and not isinstance(t, LastRound):
                    pg.keep(f"{n}@{uid}", t)
        batch(B - 1, True)


def wide_attention(pg, x, xnT, cst, w, gate):
    nc, pe, act, dve, pool, sp = pg.nc, pg.pe, pg.act, pg.dve, pg.pool, pg.sp
    pg.barrier()
    scale = 1.0 / D ** 0.5
    with ExitStack() as ctx:
        sb = lambda name, shape, dt=F32: pg.sbuf(ctx, name, shape, dt)
        wq, wk, wv, wo = (sb(n, [P, DC, D]) for n in ("wq", "wk", "wv", "wo"))
        bq, bk = sb("bq", [P, DC]), sb("bk", [P, DC])
        bvb, bob = sb("bvb", [P, D]), sb("bob", [P, D])
        ctxb = sb("ctxb", [P, 2, DC, 512])
        kT = sb("kT", [P, DC, S2])
        v = sb("v", [P, KT, D])
        qT = sb("qT", [P, DC, T])
        e_t = sb("e_t", [P, 2, S2])
        eT = sb("eT", [P, 2, KT, P])
        stat = sb("stat", [P, 2, 4])
        o, oT, yo = sb("o", [P, 2, D]), sb("oT", [P, 2, DC, P]), sb("yo", [P, D])
        s_ps = pg.psum(ctx, "s", [P, 4 * 512])
        t_ring = Ring(pg, f"t{pg.n_names}", [pg.psum(ctx, f"t{i}", [P, 512]) for i in range(3)])
        y_ring = Ring(pg, f"y{pg.n_names}", [pg.psum(ctx, f"y{i}", [P, 512]) for i in range(1)])
        ld = pg.stream("ld")
        with nc.allow_non_contiguous_dma("biases: small"):
            for t, n in ((wq, "wq"), (wk, "wk"), (wv, "wv"), (wo, "wo")):
                sp.dma(ld, t[:], w[n].rearrange("(c p) n -> p c n", p=P))
            for t, n in ((bq, "bq"), (bk, "bk")):
                sp.dma(ld, t[:], w[n].rearrange("(c p) -> p c", p=P))
            for t, n in ((bvb, "bv"), (bob, "bo")):
                sp.dma(ld, t[:], w[n].rearrange("(a n) -> a n", a=1).to_broadcast([P, D]))
        for e in (pe, act, dve):
            e.wait(ld.now())
        act.wait(dve.seq(nc.vector.tensor_scalar(bq[:], bq[:], scale, None, ALU.mult)))
        cd = [pg.stream("c0"), pg.stream("c1")]
        st = dict(ctx=[None] * 2, e=[None] * 2, eT=[None] * 2, oT=[None] * 2, o=[None] * 2, s=None)

        def project(b):
            def one(dst, wt, c, bias, mul, n, rhs):
                k, slot = t_ring.take()
                for kc in range(DC):
                    m = nc.tensor.matmul(slot[:, 0:n], wt[:, kc, P * c:P * c + P], rhs(kc),
                                         start=kc == 0, stop=kc == DC - 1)
                act.wait(pe.do(m))
                t_ring.free(k, act.do(nc.scalar.activation(dst, slot[:, 0:n], ACT.Identity, bias=bias[:, c:c + 1],
                                                           scale=mul)))
            for c in range(DC):
                one(qT[:, c, :], wq, c, bq, scale, T, lambda kc: xnT[:, kc, bass.ds(b * T, T)])
            for n_c, (c0, n) in enumerate(CHUNKS):
                f = n_c % 2
                pool.wait(st["ctx"][f])
                pe.wait(cd[f].after(nc.gpsimd.dma_start(
                    ctxb[:, f, :, 0:n], w["ctxT"][bass.ds(b, 1), :, c0:c0 + n].rearrange("a (c p) n -> p (a c) n", p=P))))
                for c in range(DC):
                    one(kT[:, c, c0:c0 + n], wk, c, bk, 1.0, n, lambda kc: ctxb[:, f, kc, 0:n])
                for k_ in range(c0 // P, -(-(c0 + n) // P)):
                    k, slot = t_ring.take()
                    for kc in range(DC):
                        m = nc.tensor.matmul(slot[0:KW[k_], 0:D], ctxb[:, f, kc, P * k_ - c0:P * k_ - c0 + KW[k_]],
                                             wv[:, kc, :], start=kc == 0, stop=kc == DC - 1)
                    act.wait(pe.do(m))
                    t_ring.free(k, act.do(nc.scalar.copy(v[0:KW[k_], k_, :], slot[0:KW[k_], 0:D])))
                st["ctx"][f] = pe.done.now()
            return act.done.now()

        def attend(b, qc, ready):
            u = qc % 2
            pe.wait(ready, st["s"])
            for c0, n in CHUNKS:
                for c in range(DC):
                    m = nc.tensor.matmul(s_ps[:, c0:c0 + n], qT[:, c, P * qc:P * qc + P], kT[:, c, c0:c0 + n],
                                         start=c == 0, stop=c == DC - 1)
            mm = pe.do(m)
            dve.wait(mm, st["e"][u])
            dve.seq(nc.vector.tensor_reduce(stat[:, u, 0:1], s_ps[:, 0:S2], AX.X, ALU.max))
            t = dve.do(nc.vector.tensor_scalar(stat[:, u, 1:2], stat[:, u, 0:1], -1.0, None, ALU.mult))
            act.wait(t, st["e"][u])
            t = act.do(nc.scalar.activation(e_t[:, u, :], s_ps[:, 0:S2], ACT.Exp, bias=stat[:, u, 1:2],
                                            accum_out=stat[:, u, 2:3]))
            st["s"] = t
            dve.wait(t)
            dve.do(nc.vector.reciprocal(stat[:, u, 3:4], stat[:, u, 2:3]))
            pe.wait(t)
            for k0 in range(0, KT, 4):
                k, slot = t_ring.take()
                ks_ = range(k0, min(KT, k0 + 4))
                for n in ks_:
                    m = nc.tensor.transpose(slot[0:KW[n], P * (n - k0):P * (n - k0) + P],
                                            e_t[:, u, P * n:P * n + KW[n]], cst["ident"][:])
                mm = pe.do(m)
                w_ = KW[ks_[-1]]
                act.wait(mm, st["eT"][u])
                t = act.do(nc.scalar.copy(eT[0:w_, u, k0:k0 + len(ks_), :],
                                          slot[0:w_, 0:P * len(ks_)].rearrange("p (k n) -> p k n", n=P)))
                t_ring.free(k, t)
            st["e"][u] = pe.done.now()
            pe.wait(t)
            k, slot = y_ring.take()
            for n in range(KT):
                m = nc.tensor.matmul(slot[:, 0:D], eT[0:KW[n], u, n, :], v[0:KW[n], n, :],
                                     start=n == 0, stop=n == KT - 1)
            st["eT"][u] = pe.do(m)
            dve.wait(st["eT"][u], st["o"][u], dve.done.now())
            t = dve.do(nc.vector.scalar_tensor_tensor(o[:, u, :], slot[:, 0:D], stat[:, u, 3:4], bvb[:], ALU.mult, ALU.add))
            y_ring.free(k, t)
            act.wait(st["oT"][u])
            t = transposed(pg, t_ring, oT[:, u, :, :], o[:, u, :], cst, t)
            st["o"][u] = pe.done.now()
            pe.wait(t)
            k, slot = y_ring.take()
            for c in range(DC):
                m = nc.tensor.matmul(slot[:, 0:D], oT[:, u, c, :], wo[:, c, :], start=c == 0, stop=c == DC - 1)
            st["oT"][u] = pe.do(m)
            dve.wait(st["oT"][u], dve.done.now())
            t = dve.seq(nc.vector.tensor_tensor(yo[:], slot[:, 0:D], bob[:], ALU.add))
            y_ring.free(k, t)
            xt = x[:, bass.ds(b * TT + qc, 1), :].rearrange("p a n -> p (a n)")
            dve.do(nc.vector.scalar_tensor_tensor(xt, yo[:], gate, xt, ALU.mult, ALU.add))

        names = ("ctx", "e", "eT", "oT", "o")
        with pg.loop(B) as b:
            for name in names:
                for p in range(2):
                    st[name][p] = pg.last_round(f"{name}{p}@wide")
            st["s"] = pg.last_round("s@wide")
            ready = project(b)
            for qc in range(QC):
                attend(b, qc, ready)
            for name in names:
                for p in range(2):
                    pg.keep(f"{name}{p}@wide", st[name][p])
            pg.keep("s@wide", st["s"])
        for r in (t_ring, y_ring):
            pg.rings.remove(r)


LAMBDA, ALPHA = 1.0507009873554804934193349852946, 1.6732632423543772848170429916717


def transposed(pg, ring, out, src, cst, after, nr=2):
    nc, pe, act = pg.nc, pg.pe, pg.act
    pe.wait(after)
    k, slot = ring.take()
    for c in range(nr):
        m = nc.tensor.transpose(slot[:, P * c:P * c + P], src[:, P * c:P * c + P], cst["ident"][:])
    act.wait(pe.do(m))
    t = act.do(nc.scalar.copy(out, slot[:, 0:P * nr].rearrange("p (c n) -> p c n", c=nr)))
    ring.free(k, t)
    return t


def quantised_linear(pg, x, xnT, cst, weight, hadamard, gate):
    nc, pe, act, dve, pool, sp = pg.nc, pg.pe, pg.act, pg.dve, pg.pool, pg.sp
    pg.barrier()
    POS, NEG, ROUND = 7.0, 8.0, 1.5 * 2.0 ** 23
    with ExitStack() as ctx:
        sb = lambda name, shape, dt=F32: pg.sbuf(ctx, name, shape, dt)
        wt, hd = sb("wt", [P, DC, D]), sb("hd", [P, DC, D])
        wsc, wn, wa, wb = sb("wsc", [P, DC, 3]), sb("wn", [P, DC, D]), sb("wa", [P, DC, D]), sb("wb", [P, DC, D])
        wqT = sb("wqT", [P, DC, D])
        xh = sb("xh", [P, 2, D])
        xc = sb("xc", [P, 2, DC, P])
        sc = sb("sc", [P, 2, 4])
        t1, t2 = sb("t1", [P, 2, D]), sb("t2", [P, 2, D])
        xq, xqT = sb("xq", [P, 2, D]), sb("xqT", [P, 2, DC, P])
        h_ring = Ring(pg, f"h{pg.n_names}", [pg.psum(ctx, f"h{i}", [P, D]) for i in range(2)])
        t_ring = Ring(pg, f"t{pg.n_names}", [pg.psum(ctx, f"t{i}", [P, D]) for i in range(2)])
        y_ring = Ring(pg, f"y{pg.n_names}", [pg.psum(ctx, f"y{i}", [P, D]) for i in range(2)])
        ld = pg.stream("ld")
        sp.dma(ld, wt[:], weight.rearrange("(c p) n -> p c n", p=P))
        sp.dma(ld, hd[:], hadamard.rearrange("(c p) n -> p c n", p=P))
        dve.wait(ld.now())
        pe.wait(ld.now())
        for c in range(DC):
            dve.seq(nc.vector.tensor_scalar(wn[:, c, :], wt[:, c, :], -1.0, None, ALU.mult))
            dve.seq(nc.vector.tensor_tensor(wa[:, c, :], wn[:, c, :], wt[:, c, :], ALU.max))
            dve.seq(nc.vector.tensor_reduce(wsc[:, c, 0:1], wa[:, c, :], AX.X, ALU.add))
            dve.seq(nc.vector.tensor_scalar(wsc[:, c, 1:2], wsc[:, c, 0:1], 1.0 / D, 1e-5, ALU.mult, ALU.max))
            dve.seq(nc.vector.reciprocal(wsc[:, c, 2:3], wsc[:, c, 1:2]))
            dve.seq(nc.vector.tensor_scalar(wn[:, c, :], wt[:, c, :], wsc[:, c, 2:3], None, ALU.mult))
            dve.seq(nc.vector.tensor_scalar(wa[:, c, :], wn[:, c, :], 0.5, None, ALU.is_gt))
            dve.seq(nc.vector.tensor_scalar(wb[:, c, :], wn[:, c, :], -0.5, None, ALU.is_lt))
            dve.seq(nc.vector.tensor_tensor(wa[:, c, :], wa[:, c, :], wb[:, c, :], ALU.subtract))
            dve.seq(nc.vector.scalar_tensor_tensor(wb[:, c, :], wa[:, c, :], wsc[:, c, 1:2], wt[:, c, :],
                                                   ALU.mult, ALU.subtract))
            t = dve.seq(nc.vector.tensor_tensor(wn[:, c, :], wb[:, c, :], wt[:, c, :], ALU.add))
            t = transposed(pg, t_ring, wqT[:, :, P * c:P * c + P], wn[:, c, :], cst, t)
        pe.wait(t)
        uid = pg.n_names
        with pg.loop(NT // 2) as i:
            done = {}
            for g in range(2):
                n = bass.ds(i * 2 + g, 1)
                xt = x[:, n, :].rearrange("p a n -> p (a n)")
                act.wait(pg.last_round(f"xc{g}@{uid}"))
                pe.wait(act.do(nc.scalar.copy(xc[:, g, :, :], xnT[:, :, bass.ds((i * 2 + g) * P, P)])))
                k, slot = h_ring.take()
                for c in range(DC):
                    m = nc.tensor.matmul(slot[:], xc[:, g, c, :], hd[:, c, :], start=c == 0, stop=c == DC - 1)
                t = pe.do(m)
                pg.keep(f"xc{g}@{uid}", t)
                dve.wait(t)
                t = dve.seq(nc.vector.tensor_copy(xh[:, g, :], slot[:]))
                h_ring.free(k, t)
                s = sc[:, g, :]
                dve.do(nc.vector.tensor_reduce(s[:, 0:1], xh[:, g, :], AX.X, ALU.max))
                dve.seq(nc.vector.tensor_reduce(s[:, 1:2], xh[:, g, :], AX.X, ALU.min))
                dve.seq(nc.vector.scalar_tensor_tensor(s[:, 2:3], s[:, 1:2], -1.0, s[:, 0:1], ALU.mult, ALU.max))
                dve.seq(nc.vector.tensor_scalar(s[:, 2:3], s[:, 2:3], 1e-5, 1.0 / POS, ALU.max, ALU.mult))
                dve.seq(nc.vector.reciprocal(s[:, 3:4], s[:, 2:3]))
                dve.seq(nc.vector.tensor_scalar(t1[:, g, :], xh[:, g, :], s[:, 3:4], ROUND, ALU.mult, ALU.add))
                dve.seq(nc.vector.tensor_scalar(t2[:, g, :], t1[:, g, :], ROUND, POS, ALU.subtract, ALU.min))
                dve.seq(nc.vector.tensor_scalar(t1[:, g, :], t2[:, g, :], -NEG, s[:, 2:3], ALU.max, ALU.mult))
                dve.seq(nc.vector.tensor_tensor(t2[:, g, :], t1[:, g, :], xh[:, g, :], ALU.subtract))
                dve.wait(pg.last_round(f"xq{g}@{uid}"))
                t = dve.do(nc.vector.tensor_tensor(xq[:, g, :], t2[:, g, :], xh[:, g, :], ALU.add))
                act.wait(pg.last_round(f"xqT{g}@{uid}"))
                t = transposed(pg, t_ring, xqT[:, g, :, :], xq[:, g, :], cst, t)
                pg.keep(f"xq{g}@{uid}", pe.done.now())
                pe.wait(t)
                k, slot = y_ring.take()
                for c in range(DC):
                    m = nc.tensor.matmul(slot[:], xqT[:, g, c, :], wqT[:, c, :], start=c == 0, stop=c == DC - 1)
                t = pe.do(m)
                pg.keep(f"xqT{g}@{uid}", t)
                dve.wait(t)
                t = dve.do(nc.vector.scalar_tensor_tensor(xt, slot[:], gate, xt, ALU.mult, ALU.add))
                y_ring.free(k, t)
        for r in (h_ring, t_ring, y_ring):
            pg.rings.remove(r)


def experts(pg, x, xnT, cst, w, gate, kind, dram):
    nc, pe, act, dve, pool, sp = pg.nc, pg.pe, pg.act, pg.dve, pg.pool, pg.sp
    pg.barrier()
    K = 2 if kind == "selu" else 1
    CAP = N // NE
    M = N // P if kind == "gelu" else K * N // P + NE - 1
    NX = NE + (kind == "selu")
    xs, ys = dram["xs"], dram["ys"]
    with ExitStack() as ctx:
        sb = lambda name, shape, dt=F32: pg.sbuf(ctx, name, shape, dt)
        w1, w2 = sb("w1", [P, 2, DC, FF]), sb("w2", [P, NX, FC, D])
        b1, b2 = sb("b1", [P, NX, FC]), sb("b2", [P, NX, D])
        oh = sb("oh", [P, K * NT, NE])
        wk = sb("wk", [P, K * NT])
        slot_u = sb("slot_u", [P, K * NT], U32)
        to_u = sb("to_u", [P, K * NT], U32)
        slot_f = sb("slot_f", [P, K * NT])
        valid = sb("valid", [P, K * NT])
        tile_e = sb("tile_e", [1, 64], I32)
        xt = sb("xt", [P, 2, D])
        xtT = sb("xtT", [P, 2, DC, P])
        hT = sb("hT", [P, 2, FC, P])
        y = sb("y", [P, 2, D])
        bank = [pg.psum(ctx, f"b{i}", [P, 512]) for i in range(2)]
        h_ring = Ring(pg, f"h{pg.n_names}", [pg.psum(ctx, f"h{i}", [P, FC * P]) for i in range(2)])
        y_ring = Ring(pg, f"y{pg.n_names}", [pg.psum(ctx, f"y{i}", [P, 512]) for i in range(2)])
        t_ring = Ring(pg, f"t{pg.n_names}", bank)

        ld = [pg.stream(f"ldw{e}") for e in range(NX)]
        order = ([NE] if kind == "selu" else []) + list(range(NE))
        small = pg.stream("lds")
        with nc.allow_non_contiguous_dma("biases: small"):
            sp.dma(small, b1[:, 0:NE, :], w["b1"].rearrange("e (f p) -> p e f", p=P))
            if kind == "selu":
                sp.dma(small, b1[:, NE, :], w["gb1"].rearrange("(f p) -> p f", p=P))
            else:
                gw = sb("gw", [P, DC, NE])
                sp.dma(small, gw[:], w["gate"].rearrange("(c p) e -> p c e", p=P))
        for e in range(NE):
            sp.dma(small, b2[:, e, :], w["b2"][e:e + 1, :].to_broadcast([P, D]))
        if kind == "selu":
            sp.dma(small, b2[:, NE, :], w["gb2"].rearrange("(a n) -> a n", a=1).to_broadcast([P, D]))
        for e in order:
            s2 = w["w2"][e] if e < NE else w["gw2"]
            if e == NE:
                sp.dma(ld[e], w1[:, 0, :, :], w["gw1"].rearrange("(c p) f -> p c f", p=P))
            sp.dma(ld[e], w2[:, e, :, :], s2.rearrange("(f p) n -> p f n", p=P))
        pe.wait(small.now())
        act.wait(small.now())
        dve.wait(small.now())
        scale = LAMBDA if kind == "selu" else 1.0
        used = dict(w1=[None, None], hT=[None, None], x=[None, None], xT=[None, None], y=[None, None], z=None, e=None)
        if kind == "selu":
            z, ez = sb("z", [P, FC * P]), sb("ez", [P, FC * P])

        def hidden(xT, w1_at, e, p):
            k, slot = h_ring.take()
            for f in range(FC):
                for c in range(DC):
                    m = nc.tensor.matmul(slot[:, P * f:P * f + P], w1[:, w1_at, c, P * f:P * f + P], xT(c),
                                         start=c == 0, stop=c == DC - 1)
            mm = pe.do(m)
            act.wait(mm, used["hT"][p])
            bias = lambda f: (b1[:, e, f:f + 1] if isinstance(e, int) else
                              b1[:, bass.ds(e, 1), f:f + 1].rearrange("p a n -> p (a n)"))
            if kind != "selu":
                func = ACT.Relu if kind == "relu" else ACT.Gelu_apprx_tanh
                for f in range(FC):
                    t = act.do(nc.scalar.activation(hT[:, p, f, :], slot[:, P * f:P * f + P], func, bias=bias(f)))
                h_ring.free(k, t)
                return t
            act.wait(used["z"])
            for f in range(FC):
                t = act.do(nc.scalar.activation(z[:, P * f:P * f + P], slot[:, P * f:P * f + P], ACT.Identity, bias=bias(f)))
            h_ring.free(k, t)
            dve.wait(t)
            t = dve.do(nc.vector.tensor_scalar(ez[:], z[:], 0.0, None, ALU.min))
            act.wait(t)
            t = act.do(nc.scalar.activation(ez[:], ez[:], ACT.Exp))
            dve.wait(t)
            dve.seq(nc.vector.tensor_scalar(ez[:], ez[:], ALPHA, ALPHA, ALU.mult, ALU.subtract))
            dve.wait(used["hT"][p])
            t = dve.seq(nc.vector.scalar_tensor_tensor(hT[:, p, :, :].rearrange("p f n -> p (f n)"), z[:], 0.0, ez[:],
                                                       ALU.max, ALU.add))
            used["z"] = t
            return t

        def projected(e, p, after, to, free):
            pe.wait(after)
            k, slot = y_ring.take()
            for f in range(FC):
                m = nc.tensor.matmul(slot[:, 0:D], hT[:, p, f, :],
                                     w2[:, e[0], f, :] if isinstance(e[0], int) else
                                     w2[:, bass.ds(e[0], 1), f, :].rearrange("p a n -> p (a n)"),
                                     start=f == 0, stop=f == FC - 1)
            used["hT"][p] = pe.do(m)
            dve.wait(used["hT"][p], free)
            t = dve.do(nc.vector.scalar_tensor_tensor(
                to, slot[:, 0:D], scale, b2[:, e[1], :] if isinstance(e[1], int) else
                b2[:, bass.ds(e[1], 1), :].rearrange("p a n -> p (a n)"), ALU.mult, ALU.add))
            y_ring.free(k, t)
            return t

        if kind == "selu":
            top = sb("top", [P, NT, 8])
            top_i = sb("top_i", [P, NT, 8], U32)
            topf = sb("topf", [P, 2, NT])
            sums = sb("sums", [P, NT])
            pe.wait(ld[NE].now())
            for n in range(NT):
                t = hidden(lambda c: xnT[:, c, P * n:P * n + P], 0, NE, n % 2)
                t = projected((NE, NE), n % 2, t, y[:, n % 2, :], None)
                dve.wait(t)
                dve.seq(nc.vector.max(top[:, n, :], y[:, n % 2, :]))
                dve.seq(nc.vector.max_index(top_i[:, n, :], top[:, n, :], y[:, n % 2, :]))
            dve.seq(nc.vector.tensor_copy(topf[:].rearrange("p k n -> p n k"), top_i[:, :, 0:2]))
            dve.seq(nc.vector.tensor_tensor(sums[:], top[:, :, 0], top[:, :, 1], ALU.add))
            dve.seq(nc.vector.reciprocal(sums[:], sums[:]))
            for k in range(K):
                dve.seq(nc.vector.tensor_tensor(wk[:, NT * k:NT * k + NT], top[:, :, k], sums[:], ALU.mult))
            chosen = topf[:].rearrange("p k n -> p (k n)")
        else:
            pr, red = sb("pr", [P, NT, NE]), sb("red", [P, 3, NT])
            k, slot = t_ring.take()
            lg = slot[:, 0:NT * NE].rearrange("p (n e) -> p n e", e=NE)
            for n in range(NT):
                for c in range(DC):
                    m = nc.tensor.matmul(lg[:, n, :], xnT[:, c, P * n:P * n + P], gw[:, c, :],
                                         start=c == 0, stop=c == DC - 1)
            dve.wait(pe.do(m))
            dve.seq(nc.vector.tensor_reduce(red[:, 0, :], lg, AX.X, ALU.max))
            over = lambda r: r.rearrange("p (n a) -> p n a", a=1).to_broadcast([P, NT, NE])
            t = dve.seq(nc.vector.tensor_tensor(pr[:], lg, over(red[:, 0, :]), ALU.subtract))
            t_ring.free(k, t)
            act.wait(t)
            t = act.do(nc.scalar.activation(pr[:], pr[:], ACT.Exp))
            dve.wait(t)
            dve.seq(nc.vector.tensor_reduce(red[:, 1, :], pr[:], AX.X, ALU.add))
            dve.seq(nc.vector.reciprocal(red[:, 1, :], red[:, 1, :]))
            dve.seq(nc.vector.tensor_tensor(pr[:], pr[:], over(red[:, 1, :]), ALU.mult))
            dve.seq(nc.vector.tensor_reduce(wk[:], pr[:], AX.X, ALU.max))
            dve.seq(nc.vector.tensor_tensor(pr[:], pr[:], over(wk[:]), ALU.is_lt))
            dve.seq(nc.vector.scalar_tensor_tensor(pr[:].rearrange("p n e -> p (n e)"), pr[:].rearrange("p n e -> p (n e)"), float(NE),
                                                   cst["iota_e"][:, 0:NT * NE], ALU.mult, ALU.add))
            dve.seq(nc.vector.tensor_reduce(red[:, 2, :], pr[:], AX.X, ALU.min))
            chosen = red[:, 2, :]
        iota = cst["iota_e"][:, 0:K * NT * NE].rearrange("p (n e) -> p n e", e=NE)
        overk = lambda r: r.rearrange("p (n a) -> p n a", a=1).to_broadcast([P, K * NT, NE])
        dve.seq(nc.vector.tensor_tensor(oh[:], iota, overk(chosen), ALU.is_equal))

        rank, tot = sb("rank", [P, K * NT, NE]), sb("tot", [P, 2, K * NT, NE])
        flat = oh[:].rearrange("p n e -> p (n e)")
        pe.wait(dve.done.now())
        k, slot = t_ring.take()
        k2, slot2 = t_ring.take()
        n_all = K * NT * NE
        nc.tensor.matmul(slot[:, 0:n_all], cst["tri"][:], flat, start=True, stop=True)
        dve.wait(pe.do(nc.tensor.matmul(slot2[:, 0:n_all], cst["ones"][:], flat, start=True, stop=True)))
        dve.do(nc.vector.tensor_copy(tot[:, 0, :, :].rearrange("p n e -> p (n e)"), slot2[:, 0:n_all]))
        t = dve.seq(nc.vector.tensor_copy(rank[:].rearrange("p n e -> p (n e)"), slot[:, 0:n_all]))
        t_ring.free(k, t)
        t_ring.free(k2, t)
        a, step = 0, 1
        while step < K * NT:
            dve.do(nc.vector.tensor_copy(tot[:, 1 - a, 0:step, :], tot[:, a, 0:step, :]))
            dve.seq(nc.vector.tensor_tensor(tot[:, 1 - a, step:, :], tot[:, a, step:, :], tot[:, a, 0:K * NT - step, :], ALU.add))
            a, step = 1 - a, 2 * step
        dve.seq(nc.vector.tensor_tensor(rank[:, 1:, :], rank[:, 1:, :], tot[:, a, 0:K * NT - 1, :], ALU.add))
        base = sb("base", [P, 2, NE])
        ends = sb("ends", [P, NE])
        if kind == "gelu":
            dve.do(nc.vector.tensor_scalar(base[:, 0, :], cst["iota_e"][:, 0:NE], float(CAP), None, ALU.mult))
            dve.seq(nc.vector.tensor_scalar(ends[:], cst["iota_e"][:, 0:NE], float(CAP), float(CAP), ALU.mult, ALU.add))
        else:
            cnt = sb("cnt", [P, NE], I32)
            dve.seq(nc.vector.tensor_scalar(ends[:], tot[:, a, K * NT - 1, :], float(P - 1), None, ALU.add))
            dve.seq(nc.vector.tensor_copy(cnt[:], ends[:]))
            dve.seq(nc.vector.tensor_scalar(cnt[:], cnt[:], 7, 7, ALU.arith_shift_right, ALU.arith_shift_left))
            dve.seq(nc.vector.tensor_copy(ends[:], cnt[:]))
            dve.seq(nc.vector.tensor_copy(base[:, 0, :], ends[:]))
            c0, step = 0, 1
            while step < NE:
                dve.do(nc.vector.tensor_copy(base[:, 1 - c0, 0:step], base[:, c0, 0:step]))
                dve.seq(nc.vector.tensor_tensor(base[:, 1 - c0, step:], base[:, c0, step:], base[:, c0, 0:NE - step], ALU.add))
                c0, step = 1 - c0, 2 * step
            dve.seq(nc.vector.tensor_tensor(base[:, 1 - c0, :], base[:, c0, :], ends[:], ALU.subtract))
            dve.seq(nc.vector.tensor_copy(ends[:], base[:, c0, :]))
            if c0 == 0:
                dve.seq(nc.vector.tensor_copy(base[:, 0, :], base[:, 1, :]))
        if kind == "gelu":
            dve.seq(nc.vector.tensor_scalar(tot[:, 0, :, :], rank[:], float(CAP), None, ALU.is_le))
            dve.seq(nc.vector.tensor_tensor(oh[:], oh[:], tot[:, 0, :, :], ALU.mult))
        bb = base[:, 0:1, :].to_broadcast([P, K * NT, NE])
        dve.seq(nc.vector.tensor_tensor(rank[:], rank[:], bb, ALU.add))
        dve.seq(nc.vector.tensor_scalar(rank[:], rank[:], -1.0, None, ALU.add))
        dve.seq(nc.vector.tensor_tensor(rank[:], rank[:], oh[:], ALU.mult))
        dve.seq(nc.vector.tensor_reduce(slot_f[:], rank[:], AX.X, ALU.add))
        dve.seq(nc.vector.tensor_copy(slot_u[:], slot_f[:]))
        dve.seq(nc.vector.tensor_reduce(valid[:], oh[:], AX.X, ALU.add))
        dve.seq(nc.vector.tensor_tensor(wk[:], wk[:], valid[:], ALU.mult))
        dve.seq(nc.vector.tensor_scalar(valid[:], valid[:], -1.0, 1.0, ALU.mult, ALU.add))
        dve.seq(nc.vector.tensor_tensor(valid[:], valid[:], cst["aside"][:, 0:K * NT], ALU.mult))
        dve.seq(nc.vector.tensor_tensor(slot_f[:], slot_f[:], valid[:], ALU.add))
        dve.seq(nc.vector.tensor_copy(to_u[:], slot_f[:]))
        dve.seq(nc.vector.tensor_scalar(wk[:], wk[:], gate, None, ALU.mult))
        te = sb("te", [1, 2, 64])
        dve.seq(nc.vector.tensor_scalar(te[:, 0, :], cst["starts"][0:1, :], ends[0:1, 0:1], None, ALU.is_ge))
        for e in range(1, NE - 1):
            dve.seq(nc.vector.scalar_tensor_tensor(te[:, e % 2, :], cst["starts"][0:1, :], ends[0:1, e:e + 1],
                                                   te[:, 1 - e % 2, :], ALU.is_ge, ALU.add))
        routed = dve.seq(nc.vector.tensor_copy(tile_e[:], te[:, (NE - 2) % 2, :]))

        xn = sb("xn", [P, 2, D])
        sent = [None, None]
        sc_s = [pg.stream("sc0"), pg.stream("sc1")]
        pool.wait(dram["zeroed"], routed)
        for n in range(NT):
            p = n % 2
            dve.wait(sent[p])
            t = dve.do(nc.vector.tensor_scalar(xn[:, p, :], x[:, n, :], cst["mv"][:, n, 0:1], cst["rstd"][:, n:n + 1],
                                               ALU.subtract, ALU.mult))
            pool.wait(t)
            for k in range(K):
                sc_s[p].after(nc.gpsimd.indirect_dma_start(
                    out=xs, out_offset=bass.IndirectOffsetOnAxis(ap=to_u[:, k * NT + n:k * NT + n + 1], axis=0),
                    in_=xn[:, p, :], in_offset=None))
            sent[p] = sc_s[p].now()
        sp.wait(*sent)

        wl = [pg.stream("wl0"), pg.stream("wl1")]
        xl, yl = [pg.stream("xl0"), pg.stream("xl1")], [pg.stream("yl0"), pg.stream("yl1")]
        for e in range(NE):
            pe.wait(ld[e].now())
        pool.wait(*sent, routed)
        pe.wait(routed)
        act.wait(routed)
        dve.wait(routed)
        st = dict(w1=[None, None], arrived=[None, None], xT=[None, None], xTt=[None, None], h=[None, None])

        def load(m, p):
            sp.wait(used["x"][p])
            st["arrived"][p] = sp.dma(xl[p], xt[:, p, :], xs[bass.ds(m * P, P), :])

        def turn(p):
            act.wait(used["xT"][p])
            st["xTt"][p] = transposed(pg, t_ring, xtT[:, p, :, :], xt[:, p, :], cst, st["arrived"][p])
            used["x"][p] = pe.done.now()

        def expert_of(eng, m):
            return eng.eng.value_load(tile_e[0:1, bass.ds(m, 1)], min_val=0, max_val=NE - 1)

        def weights(m, p):
            e = expert_of(pool, m)
            pool.wait(used["w1"][p])
            st["w1"][p] = wl[p].after(nc.gpsimd.dma_start(
                w1[:, p, :, :], w["w1"][bass.ds(e, 1), :, :].rearrange("a (c p) f -> p (a c) f", p=P)))

        def up(m, p):
            e = expert_of(act, m)
            pe.wait(st["xTt"][p], st["w1"][p])
            st["h"][p] = hidden(lambda c: xtT[:, p, c, :], p, e, p)
            used["xT"][p] = used["w1"][p] = pe.done.now()

        def down(m, p):
            e = (expert_of(pe, m), expert_of(dve, m))
            t = projected(e, p, st["h"][p], y[:, p, :], used["y"][p])
            sp.wait(t)
            used["y"][p] = sp.dma(yl[p], ys[bass.ds(m * P, P), :], y[:, p, :])

        dve.wait(dve.done.now())
        sp.wait(dve.do(nc.vector.memset(y[:], 0.0)))
        for p in range(2):
            used["y"][p] = sp.dma(yl[p], ys[(MOST + p) * P:(MOST + p + 1) * P, :], y[:, p, :])
            used["w1"][p] = pe.done.now()
            weights(p, p)
        load(0, 0)
        load(1, 1)
        turn(0)
        up(0, 0)
        weights(2, 0)
        load(2, 0)
        turn(1)
        uid = pg.n_names
        rounds = (M - 1) // 2
        kept = [("used", k) for k in ("hT", "x", "xT", "y", "w1")] + [("st", k) for k in ("w1", "arrived", "xTt", "h")]
        where = {"used": used, "st": st}
        for e in pg.engines:
            e.wait(*[where[a][k][p] for a, k in kept for p in range(2)], used["z"])
        with pg.loop(rounds) as i:
            for a, k in kept:
                for p in range(2):
                    where[a][k][p] = pg.last_round(f"{a}{k}{p}@{uid}")
            used["z"] = pg.last_round(f"z@{uid}")
            for p in (1, 0):
                m = i * 2 + (1 if p else 2)
                up(m, p)
                weights(m + 2, p)
                load(m + 2, p)
                turn(1 - p)
                down(m - 1, 1 - p)
            for a, k in kept:
                for p in range(2):
                    if where[a][k][p] is not None and not isinstance(where[a][k][p], LastRound):
                        pg.keep(f"{a}{k}{p}@{uid}", where[a][k][p])
            if used["z"] is not None and not isinstance(used["z"], LastRound):
                pg.keep(f"z@{uid}", used["z"])
        m = 2 * rounds + 1
        if m < M:
            up(m, 1)
            down(m - 1, 0)
            down(m, 1)
        else:
            down(m - 1, 0)
        yg = sb("yg", [P, 2, D])
        got = [pg.stream("got0"), pg.stream("got1")]
        pool.wait(*used["y"])
        taken = [None, None]
        q = 0
        for n in range(NT):
            for k in range(K):
                p = q % 2
                q += 1
                pool.wait(taken[p])
                t = got[p].after(nc.gpsimd.indirect_dma_start(
                    out=yg[:, p, :], out_offset=None, in_=ys,
                    in_offset=bass.IndirectOffsetOnAxis(ap=slot_u[:, k * NT + n:k * NT + n + 1], axis=0)))
                dve.wait(t, dve.done.now())
                taken[p] = dve.do(nc.vector.scalar_tensor_tensor(
                    x[:, n, :], yg[:, p, :], wk[:, k * NT + n:k * NT + n + 1], x[:, n, :], ALU.mult, ALU.add))
        for r in (h_ring, t_ring, y_ring):
            pg.rings.remove(r)


def masked_keys(pg, cst, mask, maskrow, live):
    nc, pe, dve, sp = pg.nc, pg.pe, pg.dve, pg.sp
    with ExitStack() as ctx:
        mi = pg.sbuf(ctx, "mi", [B, S2], I32)
        off, any_, dg = pg.sbuf(ctx, "off", [B, S2]), pg.sbuf(ctx, "any", [B, 1]), pg.sbuf(ctx, "dg", [B, B])
        row = pg.sbuf(ctx, "row", [B, S2], BF16)
        ps = pg.psum(ctx, "ps", [P, B])
        ld = pg.stream("mask")
        sp.dma(ld, mi[:], mask.rearrange("b x y k -> (b x y) k"))
        dve.wait(ld.now())
        dve.seq(nc.vector.tensor_copy(off[:], mi[:]))
        dve.seq(nc.vector.tensor_scalar(off[:], off[:], 0.0, None, ALU.is_equal))
        dve.seq(nc.vector.tensor_reduce(any_[:], off[:], AX.X, ALU.min))
        dve.seq(nc.vector.tensor_scalar(any_[:], any_[:], -1.0, 1.0, ALU.mult, ALU.add))
        dve.seq(nc.vector.tensor_scalar(off[:], off[:], any_[:, 0:1], -1e30, ALU.mult, ALU.mult))
        t = dve.seq(nc.vector.tensor_copy(row[:], off[:]))
        sp.wait(t)
        st = pg.stream("maskrow")
        out = sp.dma(st, maskrow, row[:])
        t = dve.seq(nc.vector.tensor_scalar(dg[:], cst["ident"][0:B, 0:B], any_[:, 0:1], None, ALU.mult))
        pe.wait(t)
        t = pe.do(nc.tensor.matmul(ps[:], cst["ones"][0:B, :], dg[:], start=True, stop=True))
        dve.wait(t)
        dve.seq(nc.vector.tensor_copy(live[:], ps[:]))
        sp.wait(out)
        return out


def build(nc, a, loops):
    with ExitStack() as ctx:
        pg = Program(nc, ctx, loops)
        pe, act, dve, pool, sp = pg.pe, pg.act, pg.dve, pg.pool, pg.sp
        x, xnT = pg.sbuf(ctx, "x", [P, NT, D]), pg.sbuf(ctx, "xnT", [P, DC, N])
        cst = {n: pg.sbuf(ctx, n, s) for n, s in (
            ("ident", [P, P]), ("sel", [P, P]), ("tri", [P, P]), ("ones", [P, P]), ("mhalf", [P, NT]),
            ("iota_e", [P, 2 * NT * NE]), ("aside", [P, 2 * NT]), ("starts", [1, 64]), ("mv", [P, NT, 2]), ("rstd", [P, NT]))}
        cst["identb"] = pg.sbuf(ctx, "identb", [P, P], BF16)
        gates, live = pg.sbuf(ctx, "gates", [P, 8]), pg.sbuf(ctx, "live", [P, B])
        dram = {}
        for n, s, dt in (("xs", [(MOST + 2) * P + 2 * N, D], F32), ("ys", [(MOST + 2) * P, D], F32), ("kparts", [3, D, S2], BF16),
                         ("qparts", [3, D, T], BF16), ("maskrow", [B, S2], BF16)):
            dram[n] = nc.dram_tensor(n, s, dt).ap()

        ld = pg.stream("constants")
        for n in ("ident", "sel", "tri", "iota_e", "aside", "starts"):
            sp.dma(ld, cst[n][:], a[n])
        sp.dma(ld, x[:], a["x"].rearrange("b (t p) d -> p (b t) d", p=P))
        with nc.allow_non_contiguous_dma("8 numbers"):
            for k, n in enumerate(("g_xattn", "g_ffn")):
                sp.dma(ld, gates[:, 4 * k:4 * k + 4], a[n].rearrange("(a n) -> a n", a=1).to_broadcast([P, 4]))
        for e in (dve, act, pe, pool):
            e.wait(ld.now())
        dve.do(nc.vector.memset(cst["ones"][:], 1.0))
        dve.do(nc.vector.memset(cst["mhalf"][:], -0.5))
        dve.do(nc.vector.tensor_copy(cst["identb"][:], cst["ident"][:]))
        dve.wait(act.do(nc.scalar.activation(gates[:], gates[:], ACT.Tanh)))
        for e in (dve, act, pe, pool):
            e.wait(dve.done.now())

        with ExitStack() as c:
            zero = pg.sbuf(c, "zero", [P, D])
            sp.wait(pool.seq(nc.gpsimd.memset(zero[:], 0.0)))
            zs = pg.stream("zeroed")
            for n in range(MOST + 2):
                for m in ("xs", "ys"):
                    sp.dma(zs, dram[m][P * n:P * n + P, :], zero[:])
            dram["zeroed"] = zs.now()
            masked = masked_keys(pg, cst, a["mask"], dram["maskrow"], live)
            for e in pg.engines:
                e.wait(zs.now(), masked)

        def norm():
            with ExitStack() as c:
                normalised(pg, x, xnT, cst, [pg.psum(c, f"t{i}", [P, 512]) for i in range(3)])

        for layer in range(4):
            w = {n: a[f"L{layer}_{n}"] for n in ("wq", "bq", "wk", "bk", "wv", "bv", "wo", "bo")}
            w |= dict(ctxT=a["ctxT"], kparts=dram["kparts"], qparts=dram["qparts"])
            g_x, g_f = gates[:, layer:layer + 1], gates[:, 4 + layer:5 + layer]
            norm()
            if layer < 3:
                head_attention(pg, x, xnT, cst, w, g_x, 1 / 16 if layer == 2 else 1 / 4,
                               a["rope"] if layer == 1 else None, (dram["maskrow"], live) if layer else None)
            else:
                wide_attention(pg, x, xnT, cst, w, g_x)
            norm()
            if layer == 0:
                quantised_linear(pg, x, xnT, cst, a["L0_weight"], a["hadamard"], g_f)
            else:
                names = ("gate", "w1", "b1", "w2", "b2") if layer < 3 else ("gw1", "gb1", "gw2", "gb2", "w1", "b1", "w2", "b2")
                experts(pg, x, xnT, cst, {n: a[f"L{layer}_{n}"] for n in names}, g_f,
                        (None, "relu", "gelu", "selu")[layer], dram)
        pg.barrier()
        o = pg.stream("out")
        sp.dma(o, a["out"].rearrange("b (t p) d -> p (b t) d", p=P), x[:])
        sp.wait(o.now())
        sp.flush()
        return pg.measured


def constants():
    f = np.float32
    c = {"ident": np.eye(P, dtype=f)}
    p = np.arange(P)
    c["sel"] = (p[:, None] == 32 * (p[None, :] // 32) + HD).astype(f)
    c["tri"] = (p[:, None] <= p[None, :]).astype(f)
    c["iota_e"] = np.tile(np.arange(NE, dtype=f), (P, 2 * NT))
    c["aside"] = ((MOST + 2) * P + P * np.arange(2 * NT)[None, :] + p[:, None]).astype(f)
    c["starts"] = (P * np.arange(64, dtype=f))[None, :]
    inv = f(1.0) / f(10000.0) ** (np.arange(0, HD, 2, dtype=f) / f(HD))
    emb = np.arange(S2, dtype=f)[:, None] * inv[None, :]
    emb = np.concatenate([emb, emb], axis=-1).T
    sign = np.where(np.arange(HD) < HD // 2, -1, 1).astype(f)[:, None]
    c["rope"] = np.ascontiguousarray(np.tile(np.stack([np.cos(emb), np.sin(emb) * sign], 1), (P // HD, 1, 1)))
    h = np.array([[1.0]])
    while h.shape[0] < D:
        h = np.block([[h, h], [h, -h]])
    c["hadamard"] = (h / np.sqrt(D)).astype(f)
    return c


def laid_out(i):
    out = dict(x=i["x"], ctxT=i["ctx_1024"].transpose(0, 2, 1), mask=i["mask_Bx1x1xS2_if1"], g_xattn=i["g_xattn"],
               g_ffn=i["g_ffn"], L0_weight=i["L0_ffn_weight"])
    for n in range(4):
        for m in "qkvo":
            w = i[f"L{n}_xattn_W{m}"]
            out[f"L{n}_w{m}"] = w.T if n in (0, 2) else w
            out[f"L{n}_b{m}"] = i[f"L{n}_xattn_b{m}"]
    out["L1_gate"], out["L2_gate"] = i["L1_ffn_gate_w"].T, i["L2_ffn_wg"]
    for n in (1, 2):
        for m in ("w1", "b1", "w2", "b2"):
            out[f"L{n}_{m}"] = i[f"L{n}_ffn_{m}"]
    for k, m in (("w1", "wi"), ("b1", "bi"), ("w2", "wo"), ("b2", "bo")):
        out[f"L3_g{k}"], out[f"L3_{k}"] = i[f"L3_ffn_gate_{m}"], i[f"L3_ffn_exp_{m}"]
    return {n: np.ascontiguousarray(a) for n, a in out.items()}


def kernel(**inputs):
    import concourse.bacc as bacc
    from concourse.bass_utils import run_bass_kernel_spmd

    arrays = laid_out({n: np.asarray(v) for n, v in inputs.items()}) | constants()

    def program(loops):
        nc = bacc.Bacc("TRN2", target_bir_lowering=False, num_devices=1)
        a = {n: nc.dram_tensor(f"in_{n}", v.shape, mybir.dt.from_np(v.dtype), kind="ExternalInput").ap()
             for n, v in arrays.items()}
        a["out"] = nc.dram_tensor("out_x", (B, T, D), F32, kind="ExternalOutput").ap()
        return nc, build(nc, a, loops)

    _, loops = program([])
    nc, _ = program(loops)
    r = run_bass_kernel_spmd(nc, [{f"in_{n}": v for n, v in arrays.items()}], core_ids=[0])
    return r.results[0]["out_x"]
```

```python
from contextlib import ExitStack, contextmanager

import numpy as np

import concourse.bass as bass
import concourse.mybir as mybir

F32, BF16, I32 = mybir.dt.float32, mybir.dt.bfloat16, mybir.dt.int32
U32 = mybir.dt.uint32
ALU, ACT, AX = mybir.AluOpType, mybir.ActivationFunctionType, mybir.AxisListType

B, T, D, S2 = 4, 512, 256, 1601
N = B * T
H, HD = 16, 16
NE, FF = 8, 1024
P = 128
TT = T // P
NT = N // P
DC = D // P
FC = FF // P
KT = -(-S2 // P)
KW = [min(P, S2 - P * k) for k in range(KT)]
MOST = 2 * N // P + NE - 1
EPS = 1e-5


class Tick:

    def __init__(self, stream, scope, base, local):
        self.stream, self.scope, self.base, self.local = stream, scope, base, local


class LastRound(Tick):
    pass


class Scope:

    def __init__(self, index, count, per):
        self.index, self.count, self.per = index, count, per


class Stream:

    def __init__(self, prog, name, step=1):
        self.prog, self.name, self.step = prog, name, step
        self.sem = prog.ctx.enter_context(prog.nc.semaphore(name))
        self.base, self.local = 0, 0
        prog.streams.append(self)

    def now(self):
        return Tick(self, self.prog.scope, self.base, self.local)

    def after(self, instruction):
        instruction.then_inc(self.sem, self.step)
        self.local += self.step
        return self.now()


class Engine:

    def __init__(self, prog, name, eng):
        self.prog, self.eng = prog, eng
        self.done = Stream(prog, f"{name}_done")
        self.seen, self.pending = {}, []

    def wait(self, *ticks):
        todo = [w for w in map(self.value, ticks) if w is not None]
        if self is self.prog.sp:
            self.pending += todo
            return
        for sem, v in todo:
            self.eng.wait_ge(sem, v)

    def flush(self):
        todo = [(sem, v if isinstance(v, int) else self.eng.to_reg(v)) for sem, v in self.pending]
        self.pending = []
        for sem, v in todo:
            self.eng.wait_ge(sem, v)

    def dma(self, stream, out, in_):
        self.flush()
        return stream.after(self.eng.dma_start(out, in_))

    def value(self, t):
        if t is None:
            return None
        scope, s = self.prog.scope, t.stream
        if isinstance(t, LastRound):
            per = scope.per.get(s.name, 1)
            back = t.local - per
            if t.base + back <= 0:
                back = 0
            assert t.base > 0 and back <= 0, (s.name, t.base, t.local, per)
            return s.sem, scope.index * per + (t.base + back)
        if t.scope is not None and scope is None:
            total = t.base + (t.scope.count - 1) * t.scope.per.get(s.name, 1) + t.local
        else:
            assert t.scope is None or t.scope is scope
            total = t.base + t.local
        key = (s.name, scope, t.scope)
        if self.seen.get(key, 0) >= total:
            return None
        self.seen[key] = total
        if t.scope is not None and scope is not None:
            return s.sem, scope.index * scope.per.get(s.name, 1) + total
        return s.sem, total

    def do(self, instruction):
        return self.done.after(instruction)

    def seq(self, instruction):
        t = self.do(instruction)
        self.wait(t)
        return t


class Program:
    def __init__(self, nc, ctx, loops):
        self.nc, self.ctx, self.loops = nc, ctx, loops
        self.scope, self.streams, self.n_loops, self.measured = None, [], 0, []
        self.pe = Engine(self, "pe", nc.tensor)
        self.act = Engine(self, "act", nc.scalar)
        self.dve = Engine(self, "dve", nc.vector)
        self.pool = Engine(self, "pool", nc.gpsimd)
        self.sp = Engine(self, "sp", nc.sync)
        self.engines = [self.pe, self.act, self.dve, self.pool, self.sp]
        self.n_names = 0
        self.rings, self.kept = [], {}

    def sbuf(self, ctx, name, shape, dt=F32):
        self.n_names += 1
        return ctx.enter_context(self.nc.sbuf_tensor(f"{name}_{self.n_names}", shape, dt))

    def psum(self, ctx, name, shape, dt=F32):
        self.n_names += 1
        return ctx.enter_context(self.nc.psum_tensor(f"{name}_{self.n_names}", shape, dt))

    def stream(self, name, step=16):
        self.n_names += 1
        return Stream(self, f"{name}_{self.n_names}", step)

    @contextmanager
    def loop(self, count):
        n = self.n_loops
        self.n_loops += 1
        per = self.loops[n] if n < len(self.loops) else {}
        for s in self.streams:
            s.base, s.local = s.base + s.local, 0
        made = len(self.streams)
        for r in self.rings:
            r.enter(per)
        self.sp.flush()
        self.kept = {}
        with self.nc.Fori(0, count) as index:
            self.scope = Scope(index, count, per)
            yield index
            for r in self.rings:
                r.leave()
            assert not self.sp.pending
        self.scope = None
        assert made == len(self.streams)
        self.measured.append({s.name: s.local for s in self.streams if s.local} | self.kept)
        for s in self.streams:
            s.base, s.local = s.base + count * s.local, 0

    def keep(self, name, tick):
        self.kept["@" + name] = (tick.stream.name, tick.local)

    def last_round(self, name):
        if "@" + name not in self.scope.per:
            return None
        where, local = self.scope.per["@" + name]
        s = next(s for s in self.streams if s.name == where)
        return LastRound(s, self.scope, s.base, local)

    def barrier(self):
        for e in self.engines:
            if e.done.base + e.done.local:
                for other in self.engines:
                    other.wait(e.done.now())


def drain(*generators):
    for g in generators:
        for _ in g:
            pass


class Ring:

    def __init__(self, prog, name, slots):
        self.prog, self.name, self.slots = prog, name, slots
        self.n, self.freed = 0, [None] * len(slots)
        prog.rings.append(self)

    def take(self):
        i = self.n % len(self.slots)
        self.n += 1
        self.prog.pe.wait(self.freed[i])
        return i, self.slots[i]

    def free(self, i, tick):
        self.freed[i] = tick

    def enter(self, per):
        self.prog.pe.wait(*self.freed)
        self.n, self.freed = 0, [None] * len(self.slots)
        for i in range(len(self.slots)):
            if f"@{self.name}{i}" in per:
                where, local = per[f"@{self.name}{i}"]
                s = next(s for s in self.prog.streams if s.name == where)
                self.freed[i] = LastRound(s, None, s.base, local)

    def leave(self):
        for i, t in enumerate(self.freed):
            if t is not None and not isinstance(t, LastRound):
                self.prog.keep(f"{self.name}{i}", t)


def normalised(pg, x, xnT, cst, psum, stats, xn):
    nc, pe, act, dve, pool = pg.nc, pg.pe, pg.act, pg.dve, pg.pool
    G = 4
    with ExitStack() as ctx:
        mv, rstd = cst["mv"], cst["rstd"]
        for n in range(NT):
            dve.do(nc.vector.bn_stats(stats[:, n, :], x[:, n, :]))
        dve.wait(dve.done.now())
        for n in range(NT):
            dve.do(nc.vector.bn_aggr(mv[:, n, :], stats[:, n, :]))
        dve.wait(dve.done.now())
        t = dve.do(nc.vector.tensor_scalar(rstd[:], mv[:, :, 1], EPS, None, ALU.add))
        pool.wait(t)
        t = pool.do(nc.gpsimd.tensor_tensor(rstd[:], rstd[:], cst["mhalf"][:, 0:NT], ALU.pow))
        dve.wait(t)
        yield
        uid = pg.n_names
        ring = Ring(pg, f"t_ring{uid}", psum)
        used = None
        with pg.loop(NT // G) as i:
            dve.wait(pg.last_round(f"xn{uid}"))
            for g in range(G):
                n = bass.ds(i * G + g, 1)
                t = dve.do(nc.vector.tensor_scalar(
                    xn[:, g, :], x[:, n, :].rearrange("p a n -> p (a n)"), mv[:, n, 0:1].rearrange("p a n -> p (a n)"),
                    rstd[:, n], ALU.subtract, ALU.mult))
                pe.wait(t)
                k, slot = ring.take()
                for c in range(DC):
                    m = nc.tensor.transpose(slot[:, P * c:P * c + P], xn[:, g, P * c:P * c + P], cst["ident"][:])
                used = pe.do(m)
                act.wait(used)
                t = act.do(nc.scalar.copy(xnT[:, :, bass.ds((i * G + g) * P, P)],
                                          slot[:, 0:D].rearrange("p (c n) -> p c n", c=DC)))
                ring.free(k, t)
            pg.keep(f"xn{uid}", used)
        done = act.done.now()
        pe.wait(done)
        dve.wait(done, pe.done.now())
        pg.rings.remove(ring)


RUNS = ((0, 0, 3), (3, 1, 2), (5, 2, 1))
R_MASK = 16 * 6
R_MAX = R_MASK + 1
R_ALL = R_MAX + 3
HG = 4
NG = H // HG
QC = T // P
VW = HD + 1
VG = HG * VW + 32 - VW
PIECE = 400
CHUNKS = [(c, min(512, S2 - c)) for c in range(0, S2, 512)]


def split3(e, one, rest, src, parts):
    e.seq(e.eng.tensor_tensor(parts[0], src, one, ALU.mult))
    e.seq(e.eng.tensor_tensor(rest, src, parts[0], ALU.subtract))
    e.seq(e.eng.tensor_tensor(parts[1], rest, one, ALU.mult))
    return e.do(e.eng.tensor_tensor(parts[2], rest, parts[1], ALU.subtract))


def head_attention(pg, x, xnT, cst, w, gate, scale, norm, rope=None, mask=None):
    nc, pe, act, dve, pool, sp = pg.nc, pg.pe, pg.act, pg.dve, pg.pool, pg.sp
    pg.barrier()
    with ExitStack() as ctx:
        sb = lambda name, shape, dt=F32: pg.sbuf(ctx, name, shape, dt)
        wq, wk, wv = (sb(n, [P, DC, D]) for n in ("wq", "wk", "wv"))
        bq, bk = sb("bq", [P, DC]), sb("bk", [P, DC])
        if rope:
            wqr, wkr = sb("wqr", [P, DC, D]), sb("wkr", [P, DC, D])
            bqr, bkr = sb("bqr", [P, DC]), sb("bkr", [P, DC])
            turn = sb("turn", [P, 2, 2, 512])
        woa = sb("woa", [P, NG, D])
        bva = sb("bva", [P, NG])
        bob = sb("bob", [P, D])
        ctxb = sb("ctxb", [P, 2, DC, 512])
        kf = sb("kf", [P, 2, 512])
        kr = sb("kr", [P, 2, 512])
        ks = sb("ks", [P, 2, 3, 512], BF16)
        kaug = sb("kaug", [P, NG, HG, S2], BF16)
        qaug = sb("qaug", [P, NG, HG, T], BF16)
        v = sb("v", [P, KT, NG, VG])
        vn = sb("vn", [P, KT, NG, HG, HD])
        e_t = sb("e_t", [P, 2, HG, T])
        mxp = sb("mxp", [P, 2, 2, HG * QC])
        mx = sb("mx", [P, 2, HG * QC])
        nm = sb("nm", [P, P // (HG * QC), HG * QC], BF16)
        tm = sb("tm", [P, P], BF16)
        z, r = sb("z", [P, T]), sb("r", [P, T])
        bvr = z[:].rearrange("p (g n) -> p g n", g=NG)
        ot = sb("ot", [P, NG, T])
        live_now = sb("live_now", [P, 1])

        s_ring = Ring(pg, f"s_ring{pg.n_names}", [pg.psum(ctx, f"s{i}", [P, 512]) for i in range(3)])
        m_ring = Ring(pg, f"m_ring{pg.n_names}", [pg.psum(ctx, f"m{i}", [P, 1024]) for i in range(2)])
        pv = pg.psum(ctx, "pv", [P, T])

        ld = pg.stream("ld")
        row = lambda a: a.rearrange("(c p) n -> p c n", p=P)
        col = lambda a: a.rearrange("(c p) -> p c", p=P)
        load = lambda out, src: sp.dma(ld, out, src)
        for t, n in ((wq, "wq"), (wk, "wk"), (wv, "wv")):
            load(t[:], row(w[n]))
        with nc.allow_non_contiguous_dma("small"):
            load(bq[:], col(w["bq"]))
            load(bk[:], col(w["bk"]))
            if rope:
                for t, n in ((wqr, "wqr"), (wkr, "wkr")):
                    load(t[:], row(w[n]))
                for t, n in ((bqr, "bqr"), (bkr, "bkr")):
                    load(t[:], col(w[n]))
            zeroed = [pool.seq(nc.gpsimd.memset(woa[:], 0.0)), pool.seq(nc.gpsimd.memset(bva[:], 0.0))]
            sp.wait(*zeroed)
            for j in range(HG):
                load(woa[32 * j:32 * j + HD, :, :],
                     w["wo"].rearrange("(g j d) n -> j d g n", j=HG, d=HD)[j])
                load(bva[32 * j:32 * j + HD, :], w["bv"].rearrange("(g j d) -> j d g", j=HG, d=HD)[j])
            load(bob[:], w["bo"].rearrange("(a n) -> a n", a=1).to_broadcast([P, D]))
        loaded = ld.now()

        v_ones = v[:, :, :, 0:HG * VW].rearrange("p k g (j c) -> p k g j c", c=VW)
        pool.do(nc.gpsimd.memset(v[:, :, :, HG * VW:VG], 0.0))
        for g in range(NG):
            pool.seq(nc.gpsimd.memset(v_ones[:, :, g, :, HD:VW], 1.0))
        pool.seq(nc.gpsimd.memset(vn[:, KT - 1, :, :, :], 0.0))
        pool.seq(nc.gpsimd.memset(nm[:], 0.0))
        sp.wait(pool.done.now())
        rows = pg.stream("rows")
        fill = e_t[:].rearrange("p a j n -> p (a j n)").bitcast(BF16)
        pool.do(nc.gpsimd.memset(fill[0:R_ALL - R_MASK, 0:S2], 1.0))
        pool.do(nc.gpsimd.memset(fill[0:1, S2:2 * S2], 0.0))
        sp.wait(pool.done.now())
        spread = lambda a: a.rearrange("p (a n) -> p a n", a=1).to_broadcast([a.shape[0], H, a.shape[1]])
        for t, n in ((kaug, S2), (qaug, T)):
            sp.dma(rows, t[R_MASK:R_ALL, :, :, :].rearrange("p g j n -> p (g j) n"), spread(fill[0:R_ALL - R_MASK, 0:n]))
        sp.wait(rows.now())
        if mask is None:
            sp.dma(rows, kaug[R_MASK:R_MASK + 1, :, :, :].rearrange("p g j n -> p (g j) n"), spread(fill[0:1, S2:2 * S2]))
        ready = pool.done.now()
        norm = norm([s[:] for s in s_ring.slots], z[:, 0:6 * NT].rearrange("p (n k) -> p n k", k=6),
             ot[:].rearrange("p g (a d) -> p (g a) d", d=D)[:, 0:4, :])
        next(norm)

        dve.wait(loaded, ready)
        for g in range(NG):
            dve.do(nc.vector.tensor_scalar(bvr[:, g, :], cst["ones"][:], bva[:, g:g + 1], None, ALU.mult))
        act.wait(loaded, rows.now())
        pe.wait(loaded, dve.done.now(), ready, rows.now())
        i, slot = m_ring.take()
        for g in range(NG):
            m = nc.tensor.matmul(slot[:, 0:D], bvr[:, g, :], woa[:, g, :], start=g == 0, stop=g == NG - 1)
        dve.wait(pe.do(m))
        t = dve.seq(nc.vector.tensor_tensor(bob[:], slot[:, 0:D], bob[:], ALU.add))
        m_ring.free(i, t)
        dve.do(nc.vector.tensor_scalar(bob[:], bob[:], gate, None, ALU.mult))
        for b_ in (bq, bqr) if rope else (bq,):
            dve.do(nc.vector.tensor_scalar(b_[:], b_[:], scale, None, ALU.mult))
        act.wait(dve.done.now())
        dve.wait(dve.done.now())

        cd = [pg.stream("ctx0"), pg.stream("ctx1")]
        kd = [pg.stream(f"kd{g}") for g in range(NG)]
        td = pg.stream("td")
        stored = [pg.stream("stored0"), pg.stream("stored1")]
        rd = [pg.stream("turn0"), pg.stream("turn1")]
        st = dict(kf=[None, None], ctx=[None, None], put=[None, None], turn=[None, None], e=[None, None],
                  k_free=[None] * NG, v_free=[None] * NG, arrived=[None] * NG, v=[None] * NG, td=[None] * NG,
                  z=[None], ot=[None], nm=[None], norm=[None], vn=[None], taken=[None],
                  peaks=[None] * 2, live=[None], live_now=[None])
        count = dict(kf=0, e=0)

        def project(nb, engines, before_q=None):
            live = None
            if mask:
                live = live_now[:, 0:1]
                act.wait(*st["live"])
                st["live_now"] = [act.do(nc.scalar.copy(live, mask[1][:, bass.ds(nb, 1)]))]

            def one(wt, wr, rhs, n, c, mul, b0, b1, pos, turn_in, dst, live):
                f = count["kf"] % 2
                e = engines[count["kf"] % len(engines)]
                count["kf"] += 1
                act.wait(st["kf"][f])
                for t, wm, b_ in ((kf, wt, b0), (kr, wr, b1)) if rope else ((kf, wt, b0),):
                    i, slot = s_ring.take()
                    for kc in range(DC):
                        m = nc.tensor.matmul(slot[:, 0:n], wm[:, kc, P * c:P * c + P], rhs(kc),
                                             start=kc == 0, stop=kc == DC - 1)
                    act.wait(pe.do(m))
                    a = act.do(nc.scalar.activation(t[:, f, 0:n], slot[:, 0:n], ACT.Identity, bias=b_[:, c:c + 1],
                                                    scale=mul))
                    s_ring.free(i, a)
                src = kf[:, f, 0:n]
                e.wait(a)
                if rope:
                    o = kr[:, f, 0:n]
                    e.wait(turn_in)
                    e.do(e.eng.tensor_tensor(src, src, turn[:, pos, 0, 0:n], ALU.mult))
                    e.seq(e.eng.tensor_tensor(o, o, turn[:, pos, 1, 0:n], ALU.mult))
                    e.seq(e.eng.tensor_tensor(src, src, o, ALU.add))
                if live is not None:
                    e.wait(*st["live_now"])
                    st["live"] = [e.seq(e.eng.tensor_tensor(src, src, live.to_broadcast([P, n]), ALU.mult))]
                e.wait(st["put"][f])
                t = split3(e, cst["ones"][:, 0:1].to_broadcast([P, n]), kr[:, f, 0:n], src, [ks[:, f, k, 0:n] for k in range(3)])
                e.wait(t)
                st["kf"][f] = st["turn"][pos] = t
                sp.wait(t)
                st["put"][f] = sp.dma(stored[f], dst[:, P * c:P * c + P, :].rearrange("a p k -> p a k"), ks[:, f, :, 0:n])

            def turns(f, c0, n):
                if not rope:
                    return None
                sp.wait(st["turn"][f])
                return sp.dma(rd[f], turn[:, f, :, 0:n], rope[:, :, c0:c0 + n])

            def context(n_c):
                c0, n = CHUNKS[n_c]
                f = (n_c + 1) % 2
                sp.wait(st["ctx"][f])
                return sp.dma(cd[f], ctxb[:, f, :, 0:n],
                              w["ctxT"][bass.ds(nb, 1), :, c0:c0 + n].rearrange("a (c p) n -> p (a c) n", p=P))

            arrived = [context(0), context(1)]
            sp.wait(*st["arrived"])
            for n_c, (c0, n) in enumerate(CHUNKS):
                f = (n_c + 1) % 2
                t_in = turns(f, c0, n)
                pe.wait(arrived[n_c])
                for c in range(DC):
                    one(wk, wkr if rope else None, lambda kc: ctxb[:, f, kc, 0:n], n, c, 1.0, bk,
                        bkr if rope else None, f, t_in, w["kparts"][:, :, c0:c0 + n], None)
                    yield
                for k in range(c0 // P, -(-(c0 + n) // P)):
                    i, slot = s_ring.take()
                    for kc in range(DC):
                        m = nc.tensor.matmul(slot[0:KW[k], 0:D], ctxb[:, f, kc, k * P - c0:k * P - c0 + KW[k]],
                                             wv[:, kc, :], start=kc == 0, stop=kc == DC - 1)
                    act.wait(pe.do(m), st["taken"][0])
                    t = act.do(nc.scalar.copy(vn[0:KW[k], k, :, :, :].rearrange("p g j d -> p (g j d)"),
                                              slot[0:KW[k], 0:D]))
                    s_ring.free(i, t)
                    yield
                st["ctx"][f] = pe.done.now()
                if n_c + 2 < len(CHUNKS):
                    arrived.append(context(n_c + 2))
            st["vn"] = [t]
            if before_q:
                before_q()
            t_in = turns(0, 0, T)
            for c in range(DC):
                one(wq, wqr if rope else None, lambda kc: xnT[:, kc, bass.ds(nb * T, T)], T, c, scale, bq,
                    bqr if rope else None, 0, t_in, w["qparts"], live)
                yield

        def fetch(g, nb):
            sp.wait(*st["put"], st["k_free"][g])
            h0, h1 = HG * HD * g, HG * HD * (g + 1)
            for s, pq, n in RUNS:
                for k in range(n):
                    r0 = HD * (s + k)
                    sp.dma(kd[g], qaug[r0:r0 + HD, g, :, :], w["qparts"][pq, h0:h1, :].rearrange("(h d) k -> d h k", d=HD))
                    sp.dma(kd[g], kaug[r0:r0 + HD, g, :, :], w["kparts"][k, h0:h1, :].rearrange("(h d) k -> d h k", d=HD))
            if mask:
                for j in range(HG):
                    sp.dma(kd[g], kaug[R_MASK:R_MASK + 1, g, j, :], mask[0][bass.ds(nb, 1), :])
            st["arrived"][g] = kd[g].now()

        def values_of(g):
            act.wait(*st["vn"], st["v_free"][g])
            st["v"][g] = st["taken"][0] = act.do(nc.scalar.copy(v_ones[:, :, g, :, 0:HD], vn[:, :, g, :, :]))

        def maxima(g, begin=0, end=None):
            u = g % 2
            pe.wait(st["arrived"][g])
            t = None
            for j in range(HG):
                for qc in range(QC):
                    for half in range(2):
                        step = 2 * (j * QC + qc) + half
                        if step < begin:
                            continue
                        if end is not None and step >= end:
                            return
                        i, slot = m_ring.take()
                        for k in range(2):
                            k0 = PIECE * (2 * half + k)
                            m = nc.tensor.matmul(slot[:, 512 * k:512 * k + PIECE + 1],
                                                 qaug[0:R_MAX, g, j, P * qc:P * qc + P],
                                                 kaug[0:R_MAX, g, j, k0:k0 + PIECE + 1], start=True, stop=True)
                        dve.wait(pe.do(m))
                        n = j * QC + qc
                        t = dve.do(nc.vector.tensor_reduce(
                            mxp[:, u, half, n:n + 1], slot[:].rearrange("p (a n) -> p a n", a=2)[:, :, 0:PIECE + 1],
                            AX.XY, ALU.max))
                        m_ring.free(i, t)
                        st["peaks"][u] = t
                        yield
            dve.wait(t, st["peaks"][g % 2], *st["nm"])
            dve.seq(nc.vector.tensor_tensor(mx[:, 0, :], mxp[:, u, 0, :], mxp[:, u, 1, :], ALU.max))
            dve.seq(nc.vector.tensor_scalar(mx[:, 0, :], mx[:, 0, :], -1.0, None, ALU.mult))
            t = split3(dve, cst["ones"][:, 0:HG * QC], mx[:, 1, :], mx[:, 0, :], [nm[:, k, :] for k in range(3)])
            yield
            i, slot = m_ring.take()
            o = slot[:].bitcast(BF16)[:, 0:P]
            pe.wait(t)
            tick = pe.do(nc.tensor.transpose(o, nm[:].rearrange("p a n -> p (a n)"), cst["identb"][:]))
            st["nm"] = [tick]
            dve.wait(tick, st["td"][(g - 1) % NG])
            t = dve.do(nc.vector.tensor_copy(tm[:], o))
            m_ring.free(i, t)
            sp.wait(t)
            for k in range(3):
                sp.dma(td, qaug[R_MAX + k:R_MAX + k + 1, g, :, :].rearrange("a j (c q) -> a (j c) q", q=P),
                       tm[16 * k:16 * k + 16, :])
            st["td"][g] = td.now()
            yield

        MAX_STEPS = 2 * HG * QC + 2

        def normalise(g):
            i, slot = m_ring.take()
            pe.wait(*st["z"])
            t = pe.do(nc.tensor.matmul(slot[:, 0:T], cst["sel"][:], z[:], start=True, stop=True))
            act.wait(t, *st["norm"])
            t = act.do(nc.scalar.copy(r[:], slot[:, 0:T]))
            m_ring.free(i, t)
            dve.wait(t, *st["ot"])
            for c in range(QC):
                part = slice(P * c, P * c + P)
                dve.seq(nc.vector.reciprocal(r[:, part], r[:, part]))
                st["norm"] = [dve.do(nc.vector.tensor_tensor(ot[:, g, part], z[:, part], r[:, part], ALU.mult))]
                yield

        def output(b):
            for tt in range(TT):
                i, slot = m_ring.take()
                if tt == 0:
                    pe.wait(*st["norm"])
                for g in range(NG):
                    m = nc.tensor.matmul(slot[:, 0:D], ot[:, g, P * tt:P * tt + P], woa[:, g, :],
                                         start=g == 0, stop=g == NG - 1)
                xt = x[:, bass.ds(b * TT + tt, 1), :].rearrange("p a n -> p (a n)")
                dve.wait(pe.do(m))
                t = dve.seq(nc.vector.scalar_tensor_tensor(xt, slot[:, 0:D], gate, xt, ALU.mult, ALU.add))
                m_ring.free(i, t)
                dve.do(nc.vector.tensor_tensor(xt, xt, bob[:], ALU.add))
                yield
            st["ot"] = [pe.done.now()]

        waiting = []

        def attend(g, *work):
            pe.wait(st["td"][g])

            def values(k, jobs):
                e = count["e"] % 2
                count["e"] += 1
                pe.wait(*jobs, *((st["v"][g], *st["z"]) if k == 0 else ()))
                for j in range(HG):
                    m = nc.tensor.matmul(pv[32 * j:32 * j + 32, :], v[0:KW[k], k, g, VW * j:VW * j + 32],
                                         e_t[0:KW[k], e, j, :], start=k == 0, stop=k == KT - 1)
                st["e"][e] = pe.do(m)
                if k == KT - 1:
                    st["v_free"][g] = st["e"][e]
                    dve.wait(st["e"][e], *st["norm"])
                    st["z"] = [dve.do(nc.vector.tensor_copy(z[:], pv[:]))]
            given = [0] * len(work)
            for k in range(KT):
                jobs = []
                for j in range(HG):
                    i, slot = s_ring.take()
                    mm = pe.do(nc.tensor.matmul(slot[0:KW[k], :], kaug[0:R_ALL, g, j, P * k:P * k + KW[k]],
                                                qaug[0:R_ALL, g, j, :], start=True, stop=True))
                    e = (count["e"] + len(waiting)) % 2
                    act.wait(mm, st["e"][e] if j == 0 else None)
                    t = act.do(nc.scalar.activation(e_t[0:KW[k], e, j, :], slot[0:KW[k], :], ACT.Exp))
                    s_ring.free(i, t)
                    jobs.append(t)
                    n = HG * k + j
                    for a, (gen, steps, first, last) in enumerate(work):
                        while n >= first and given[a] * (last - first + 1) < steps * (n - first + 1):
                            given[a] += 1
                            next(gen, None)
                if waiting:
                    waiting.pop()()
                waiting.append(lambda k=k, jobs=jobs: values(k, jobs))
            st["k_free"][g] = pe.done.now()

        def finish():
            if waiting:
                waiting.pop()()

        def then(f, *a):
            f(*a)
            yield

        def chain(*gens):
            for gen in gens:
                yield from gen

        JOBS = HG * KT
        LEAD = 8

        drain(project(0, (dve, pool), lambda: [None for _ in norm]))
        for g in range(NG):
            fetch(g, 0)
            values_of(g)
        drain(maxima(0))
        attend(0, (chain(maxima(1), maxima(2, 0, LEAD)), MAX_STEPS + LEAD, 0, JOBS - 1))
        finish()

        def all_ticks():
            for name, ticks in st.items():
                for i, t in enumerate(ticks):
                    yield f"{name}{i}", (lambda t, name=name, i=i: st[name].__setitem__(i, t)), t

        uid = pg.n_names
        for e in pg.engines:
            e.wait(*[t for _, _, t in all_ticks() if t is not None])
        with pg.loop(B - 1) as b:
            count["kf"] = count["e"] = 0
            for n, put, _ in list(all_ticks()):
                put(pg.last_round(f"{n}@{uid}"))
            peaks = (chain(maxima(2, LEAD), maxima(3), maxima(0), maxima(1), maxima(2, 0, LEAD)), MAX_STEPS, 0, JOBS - 1)
            projected = chain(project(b + 1, (pool,)), *(then(fetch, g, b + 1) for g in (0, 1)))
            attend(1, peaks, (projected, 16, 6, JOBS - 1), (normalise(0), QC, 2 * HG, JOBS - 1))
            attend(2, peaks, (projected, 10, 0, 20), (normalise(1), QC, 2 * HG, JOBS - 1))
            attend(3, peaks, (chain(then(fetch, 2, b + 1), *(then(values_of, g) for g in range(3))), 4, 8, 24),
                   (normalise(2), QC, 2 * HG, JOBS - 1))
            attend(0, peaks, (chain(then(fetch, 3, b + 1), then(values_of, 3)), 2, 8, 24),
                   (chain(normalise(3), output(b)), QC + TT + 1, 2 * HG, JOBS - 1))
            finish()
            for n, _, t in all_ticks():
                if t is not None and not isinstance(t, LastRound):
                    pg.keep(f"{n}@{uid}", t)
        peaks = (chain(maxima(2, LEAD), maxima(3)), MAX_STEPS, 0, JOBS - 1)
        for g in range(1, NG):
            attend(g, peaks, (normalise(g - 1), QC, 2 * HG, JOBS - 1))
        finish()
        drain(normalise(NG - 1), output(B - 1))
        for ring in (s_ring, m_ring):
            pg.rings.remove(ring)


def wide_attention(pg, x, xnT, cst, w, gate):
    nc, pe, act, dve, pool, sp = pg.nc, pg.pe, pg.act, pg.dve, pg.pool, pg.sp
    pg.barrier()
    scale = 1.0 / D ** 0.5
    with ExitStack() as ctx:
        sb = lambda name, shape, dt=F32: pg.sbuf(ctx, name, shape, dt)
        wq, wk, wv, wo = (sb(n, [P, DC, D]) for n in ("wq", "wk", "wv", "wo"))
        bq, bk = sb("bq", [P, DC]), sb("bk", [P, DC])
        bvb, bob = sb("bvb", [P, D]), sb("bob", [P, D])
        ctxb = sb("ctxb", [P, 2, DC, 512])
        kT = sb("kT", [P, DC, S2])
        v = sb("v", [P, KT, D])
        qT = sb("qT", [P, DC, T])
        e_t = sb("e_t", [P, 2, S2])
        eT = sb("eT", [P, 2, KT, P])
        stat = sb("stat", [P, 2, 4])
        o, oT, yo = sb("o", [P, 2, D]), sb("oT", [P, 2, DC, P]), sb("yo", [P, D])
        s_ps = pg.psum(ctx, "s", [P, 4 * 512])
        t_ring = Ring(pg, f"t{pg.n_names}", [pg.psum(ctx, f"t{i}", [P, 512]) for i in range(3)])
        y_ring = Ring(pg, f"y{pg.n_names}", [pg.psum(ctx, f"y{i}", [P, 512]) for i in range(1)])
        ld = pg.stream("ld")
        with nc.allow_non_contiguous_dma("biases: small"):
            for t, n in ((wq, "wq"), (wk, "wk"), (wv, "wv"), (wo, "wo")):
                sp.dma(ld, t[:], w[n].rearrange("(c p) n -> p c n", p=P))
            for t, n in ((bq, "bq"), (bk, "bk")):
                sp.dma(ld, t[:], w[n].rearrange("(c p) -> p c", p=P))
            for t, n in ((bvb, "bv"), (bob, "bo")):
                sp.dma(ld, t[:], w[n].rearrange("(a n) -> a n", a=1).to_broadcast([P, D]))
        for e in (pe, act, dve):
            e.wait(ld.now())
        act.wait(dve.seq(nc.vector.tensor_scalar(bq[:], bq[:], scale, None, ALU.mult)))
        cd = [pg.stream("c0"), pg.stream("c1")]
        st = dict(ctx=[None] * 2, e=[None] * 2, eT=[None] * 2, oT=[None] * 2, o=[None] * 2, s=None)

        def project(b):
            def one(dst, wt, c, bias, mul, n, rhs):
                k, slot = t_ring.take()
                for kc in range(DC):
                    m = nc.tensor.matmul(slot[:, 0:n], wt[:, kc, P * c:P * c + P], rhs(kc),
                                         start=kc == 0, stop=kc == DC - 1)
                act.wait(pe.do(m))
                t_ring.free(k, act.do(nc.scalar.activation(dst, slot[:, 0:n], ACT.Identity, bias=bias[:, c:c + 1],
                                                           scale=mul)))
            for c in range(DC):
                one(qT[:, c, :], wq, c, bq, scale, T, lambda kc: xnT[:, kc, bass.ds(b * T, T)])
            for n_c, (c0, n) in enumerate(CHUNKS):
                f = n_c % 2
                pool.wait(st["ctx"][f])
                pe.wait(cd[f].after(nc.gpsimd.dma_start(
                    ctxb[:, f, :, 0:n], w["ctxT"][bass.ds(b, 1), :, c0:c0 + n].rearrange("a (c p) n -> p (a c) n", p=P))))
                for c in range(DC):
                    one(kT[:, c, c0:c0 + n], wk, c, bk, 1.0, n, lambda kc: ctxb[:, f, kc, 0:n])
                for k_ in range(c0 // P, -(-(c0 + n) // P)):
                    k, slot = t_ring.take()
                    for kc in range(DC):
                        m = nc.tensor.matmul(slot[0:KW[k_], 0:D], ctxb[:, f, kc, P * k_ - c0:P * k_ - c0 + KW[k_]],
                                             wv[:, kc, :], start=kc == 0, stop=kc == DC - 1)
                    act.wait(pe.do(m))
                    t_ring.free(k, act.do(nc.scalar.copy(v[0:KW[k_], k_, :], slot[0:KW[k_], 0:D])))
                st["ctx"][f] = pe.done.now()
            return act.done.now()

        def attend(b, qc, ready):
            u = qc % 2
            pe.wait(ready, st["s"])
            for c0, n in CHUNKS:
                for c in range(DC):
                    m = nc.tensor.matmul(s_ps[:, c0:c0 + n], qT[:, c, P * qc:P * qc + P], kT[:, c, c0:c0 + n],
                                         start=c == 0, stop=c == DC - 1)
            mm = pe.do(m)
            dve.wait(mm, st["e"][u])
            dve.seq(nc.vector.tensor_reduce(stat[:, u, 0:1], s_ps[:, 0:S2], AX.X, ALU.max))
            t = dve.do(nc.vector.tensor_scalar(stat[:, u, 1:2], stat[:, u, 0:1], -1.0, None, ALU.mult))
            act.wait(t, st["e"][u])
            t = act.do(nc.scalar.activation(e_t[:, u, :], s_ps[:, 0:S2], ACT.Exp, bias=stat[:, u, 1:2],
                                            accum_out=stat[:, u, 2:3]))
            st["s"] = t
            dve.wait(t)
            dve.do(nc.vector.reciprocal(stat[:, u, 3:4], stat[:, u, 2:3]))
            pe.wait(t)
            for k0 in range(0, KT, 4):
                k, slot = t_ring.take()
                ks_ = range(k0, min(KT, k0 + 4))
                for n in ks_:
                    m = nc.tensor.transpose(slot[0:KW[n], P * (n - k0):P * (n - k0) + P],
                                            e_t[:, u, P * n:P * n + KW[n]], cst["ident"][:])
                mm = pe.do(m)
                w_ = KW[ks_[-1]]
                act.wait(mm, st["eT"][u])
                t = act.do(nc.scalar.copy(eT[0:w_, u, k0:k0 + len(ks_), :],
                                          slot[0:w_, 0:P * len(ks_)].rearrange("p (k n) -> p k n", n=P)))
                t_ring.free(k, t)
            st["e"][u] = pe.done.now()
            pe.wait(t)
            k, slot = y_ring.take()
            for n in range(KT):
                m = nc.tensor.matmul(slot[:, 0:D], eT[0:KW[n], u, n, :], v[0:KW[n], n, :],
                                     start=n == 0, stop=n == KT - 1)
            st["eT"][u] = pe.do(m)
            dve.wait(st["eT"][u], st["o"][u], dve.done.now())
            t = dve.do(nc.vector.scalar_tensor_tensor(o[:, u, :], slot[:, 0:D], stat[:, u, 3:4], bvb[:], ALU.mult, ALU.add))
            y_ring.free(k, t)
            act.wait(st["oT"][u])
            t = transposed(pg, t_ring, oT[:, u, :, :], o[:, u, :], cst, t)
            st["o"][u] = pe.done.now()
            pe.wait(t)
            k, slot = y_ring.take()
            for c in range(DC):
                m = nc.tensor.matmul(slot[:, 0:D], oT[:, u, c, :], wo[:, c, :], start=c == 0, stop=c == DC - 1)
            st["oT"][u] = pe.do(m)
            dve.wait(st["oT"][u], dve.done.now())
            t = dve.seq(nc.vector.tensor_tensor(yo[:], slot[:, 0:D], bob[:], ALU.add))
            y_ring.free(k, t)
            xt = x[:, bass.ds(b * TT + qc, 1), :].rearrange("p a n -> p (a n)")
            dve.do(nc.vector.scalar_tensor_tensor(xt, yo[:], gate, xt, ALU.mult, ALU.add))

        names = ("ctx", "e", "eT", "oT", "o")
        with pg.loop(B) as b:
            for name in names:
                for p in range(2):
                    st[name][p] = pg.last_round(f"{name}{p}@wide")
            st["s"] = pg.last_round("s@wide")
            ready = project(b)
            for qc in range(QC):
                attend(b, qc, ready)
            for name in names:
                for p in range(2):
                    pg.keep(f"{name}{p}@wide", st[name][p])
            pg.keep("s@wide", st["s"])
        for r in (t_ring, y_ring):
            pg.rings.remove(r)


LAMBDA, ALPHA = 1.0507009873554804934193349852946, 1.6732632423543772848170429916717


def transposed(pg, ring, out, src, cst, after, nr=2):
    nc, pe, act = pg.nc, pg.pe, pg.act
    pe.wait(after)
    k, slot = ring.take()
    for c in range(nr):
        m = nc.tensor.transpose(slot[:, P * c:P * c + P], src[:, P * c:P * c + P], cst["ident"][:])
    act.wait(pe.do(m))
    t = act.do(nc.scalar.copy(out, slot[:, 0:P * nr].rearrange("p (c n) -> p c n", c=nr)))
    ring.free(k, t)
    return t


def quantised_linear(pg, x, xnT, cst, weight, hadamard, gate):
    nc, pe, act, dve, pool, sp = pg.nc, pg.pe, pg.act, pg.dve, pg.pool, pg.sp
    pg.barrier()
    POS, NEG, ROUND = 7.0, 8.0, 1.5 * 2.0 ** 23
    with ExitStack() as ctx:
        sb = lambda name, shape, dt=F32: pg.sbuf(ctx, name, shape, dt)
        wt, hd = sb("wt", [P, DC, D]), sb("hd", [P, DC, D])
        wsc, wn, wa, wb = sb("wsc", [P, DC, 3]), sb("wn", [P, DC, D]), sb("wa", [P, DC, D]), sb("wb", [P, DC, D])
        wqT = sb("wqT", [P, DC, D])
        xh = sb("xh", [P, 2, D])
        xc = sb("xc", [P, 2, DC, P])
        sc = sb("sc", [P, 2, 4])
        t1, t2 = sb("t1", [P, 2, D]), sb("t2", [P, 2, D])
        xq, xqT = sb("xq", [P, 2, D]), sb("xqT", [P, 2, DC, P])
        h_ring = Ring(pg, f"h{pg.n_names}", [pg.psum(ctx, f"h{i}", [P, D]) for i in range(2)])
        t_ring = Ring(pg, f"t{pg.n_names}", [pg.psum(ctx, f"t{i}", [P, D]) for i in range(2)])
        y_ring = Ring(pg, f"y{pg.n_names}", [pg.psum(ctx, f"y{i}", [P, D]) for i in range(2)])
        ld = pg.stream("ld")
        sp.dma(ld, wt[:], weight.rearrange("(c p) n -> p c n", p=P))
        sp.dma(ld, hd[:], hadamard.rearrange("(c p) n -> p c n", p=P))
        dve.wait(ld.now())
        pe.wait(ld.now())
        for c in range(DC):
            dve.seq(nc.vector.tensor_scalar(wn[:, c, :], wt[:, c, :], -1.0, None, ALU.mult))
            dve.seq(nc.vector.tensor_tensor(wa[:, c, :], wn[:, c, :], wt[:, c, :], ALU.max))
            dve.seq(nc.vector.tensor_reduce(wsc[:, c, 0:1], wa[:, c, :], AX.X, ALU.add))
            dve.seq(nc.vector.tensor_scalar(wsc[:, c, 1:2], wsc[:, c, 0:1], 1.0 / D, 1e-5, ALU.mult, ALU.max))
            dve.seq(nc.vector.reciprocal(wsc[:, c, 2:3], wsc[:, c, 1:2]))
            dve.seq(nc.vector.tensor_scalar(wn[:, c, :], wt[:, c, :], wsc[:, c, 2:3], None, ALU.mult))
            dve.seq(nc.vector.tensor_scalar(wa[:, c, :], wn[:, c, :], 0.5, None, ALU.is_gt))
            dve.seq(nc.vector.tensor_scalar(wb[:, c, :], wn[:, c, :], -0.5, None, ALU.is_lt))
            dve.seq(nc.vector.tensor_tensor(wa[:, c, :], wa[:, c, :], wb[:, c, :], ALU.subtract))
            dve.seq(nc.vector.scalar_tensor_tensor(wb[:, c, :], wa[:, c, :], wsc[:, c, 1:2], wt[:, c, :],
                                                   ALU.mult, ALU.subtract))
            t = dve.seq(nc.vector.tensor_tensor(wn[:, c, :], wb[:, c, :], wt[:, c, :], ALU.add))
            t = transposed(pg, t_ring, wqT[:, :, P * c:P * c + P], wn[:, c, :], cst, t)
        pe.wait(t)
        uid = pg.n_names
        with pg.loop(NT // 2) as i:
            done = {}
            for g in range(2):
                n = bass.ds(i * 2 + g, 1)
                xt = x[:, n, :].rearrange("p a n -> p (a n)")
                act.wait(pg.last_round(f"xc{g}@{uid}"))
                pe.wait(act.do(nc.scalar.copy(xc[:, g, :, :], xnT[:, :, bass.ds((i * 2 + g) * P, P)])))
                k, slot = h_ring.take()
                for c in range(DC):
                    m = nc.tensor.matmul(slot[:], xc[:, g, c, :], hd[:, c, :], start=c == 0, stop=c == DC - 1)
                t = pe.do(m)
                pg.keep(f"xc{g}@{uid}", t)
                dve.wait(t)
                t = dve.seq(nc.vector.tensor_copy(xh[:, g, :], slot[:]))
                h_ring.free(k, t)
                s = sc[:, g, :]
                dve.do(nc.vector.tensor_reduce(s[:, 0:1], xh[:, g, :], AX.X, ALU.max))
                dve.seq(nc.vector.tensor_reduce(s[:, 1:2], xh[:, g, :], AX.X, ALU.min))
                dve.seq(nc.vector.scalar_tensor_tensor(s[:, 2:3], s[:, 1:2], -1.0, s[:, 0:1], ALU.mult, ALU.max))
                dve.seq(nc.vector.tensor_scalar(s[:, 2:3], s[:, 2:3], 1e-5, 1.0 / POS, ALU.max, ALU.mult))
                dve.seq(nc.vector.reciprocal(s[:, 3:4], s[:, 2:3]))
                dve.seq(nc.vector.tensor_scalar(t1[:, g, :], xh[:, g, :], s[:, 3:4], ROUND, ALU.mult, ALU.add))
                dve.seq(nc.vector.tensor_scalar(t2[:, g, :], t1[:, g, :], ROUND, POS, ALU.subtract, ALU.min))
                dve.seq(nc.vector.tensor_scalar(t1[:, g, :], t2[:, g, :], -NEG, s[:, 2:3], ALU.max, ALU.mult))
                dve.seq(nc.vector.tensor_tensor(t2[:, g, :], t1[:, g, :], xh[:, g, :], ALU.subtract))
                dve.wait(pg.last_round(f"xq{g}@{uid}"))
                t = dve.do(nc.vector.tensor_tensor(xq[:, g, :], t2[:, g, :], xh[:, g, :], ALU.add))
                act.wait(pg.last_round(f"xqT{g}@{uid}"))
                t = transposed(pg, t_ring, xqT[:, g, :, :], xq[:, g, :], cst, t)
                pg.keep(f"xq{g}@{uid}", pe.done.now())
                pe.wait(t)
                k, slot = y_ring.take()
                for c in range(DC):
                    m = nc.tensor.matmul(slot[:], xqT[:, g, c, :], wqT[:, c, :], start=c == 0, stop=c == DC - 1)
                t = pe.do(m)
                pg.keep(f"xqT{g}@{uid}", t)
                dve.wait(t)
                t = dve.do(nc.vector.scalar_tensor_tensor(xt, slot[:], gate, xt, ALU.mult, ALU.add))
                y_ring.free(k, t)
        for r in (h_ring, t_ring, y_ring):
            pg.rings.remove(r)


def experts(pg, x, xnT, cst, w, gate, kind, dram):
    nc, pe, act, dve, pool, sp = pg.nc, pg.pe, pg.act, pg.dve, pg.pool, pg.sp
    pg.barrier()
    K = 2 if kind == "selu" else 1
    CAP = N // NE
    M = N // P if kind == "gelu" else K * N // P + NE - 1
    NX = NE + (kind == "selu")
    xs, ys = dram["xs"], dram["ys"]
    with ExitStack() as ctx:
        sb = lambda name, shape, dt=F32: pg.sbuf(ctx, name, shape, dt)
        w1, w2 = sb("w1", [P, 2, DC, FF]), sb("w2", [P, NX, FC, D])
        b1, b2 = sb("b1", [P, NX, FC]), sb("b2", [P, NX, D])
        oh = sb("oh", [P, K * NT, NE])
        wk = sb("wk", [P, K * NT])
        slot_u = sb("slot_u", [P, K * NT], U32)
        to_u = sb("to_u", [P, K * NT], U32)
        slot_f = sb("slot_f", [P, K * NT])
        valid = sb("valid", [P, K * NT])
        tile_e = sb("tile_e", [1, 64], I32)
        xt = sb("xt", [P, 2, D])
        xtT = sb("xtT", [P, 2, DC, P])
        hT = sb("hT", [P, 2, FC, P])
        y = sb("y", [P, 2, D])
        bank = [pg.psum(ctx, f"b{i}", [P, 512]) for i in range(2)]
        h_ring = Ring(pg, f"h{pg.n_names}", [pg.psum(ctx, f"h{i}", [P, FC * P]) for i in range(2)])
        y_ring = Ring(pg, f"y{pg.n_names}", [pg.psum(ctx, f"y{i}", [P, 512]) for i in range(2)])
        t_ring = Ring(pg, f"t{pg.n_names}", bank)

        ld = [pg.stream(f"ldw{e}") for e in range(NX)]
        order = ([NE] if kind == "selu" else []) + list(range(NE))
        small = pg.stream("lds")
        with nc.allow_non_contiguous_dma("biases: small"):
            sp.dma(small, b1[:, 0:NE, :], w["b1"].rearrange("e (f p) -> p e f", p=P))
            if kind == "selu":
                sp.dma(small, b1[:, NE, :], w["gb1"].rearrange("(f p) -> p f", p=P))
            else:
                gw = sb("gw", [P, DC, NE])
                sp.dma(small, gw[:], w["gate"].rearrange("(c p) e -> p c e", p=P))
        for e in range(NE):
            sp.dma(small, b2[:, e, :], w["b2"][e:e + 1, :].to_broadcast([P, D]))
        if kind == "selu":
            sp.dma(small, b2[:, NE, :], w["gb2"].rearrange("(a n) -> a n", a=1).to_broadcast([P, D]))
        for e in order:
            s2 = w["w2"][e] if e < NE else w["gw2"]
            if e == NE:
                sp.dma(ld[e], w1[:, 0, :, :], w["gw1"].rearrange("(c p) f -> p c f", p=P))
            sp.dma(ld[e], w2[:, e, :, :], s2.rearrange("(f p) n -> p f n", p=P))
        pe.wait(small.now())
        act.wait(small.now())
        dve.wait(small.now())
        scale = LAMBDA if kind == "selu" else 1.0
        used = dict(w1=[None, None], hT=[None, None], x=[None, None], xT=[None, None], y=[None, None], z=None, e=None)
        if kind == "selu":
            z, ez = sb("z", [P, FC * P]), sb("ez", [P, FC * P])

        def hidden(xT, w1_at, e, p):
            k, slot = h_ring.take()
            for f in range(FC):
                for c in range(DC):
                    m = nc.tensor.matmul(slot[:, P * f:P * f + P], w1[:, w1_at, c, P * f:P * f + P], xT(c),
                                         start=c == 0, stop=c == DC - 1)
            mm = pe.do(m)
            act.wait(mm, used["hT"][p])
            bias = lambda f: (b1[:, e, f:f + 1] if isinstance(e, int) else
                              b1[:, bass.ds(e, 1), f:f + 1].rearrange("p a n -> p (a n)"))
            if kind != "selu":
                func = ACT.Relu if kind == "relu" else ACT.Gelu_apprx_tanh
                for f in range(FC):
                    t = act.do(nc.scalar.activation(hT[:, p, f, :], slot[:, P * f:P * f + P], func, bias=bias(f)))
                h_ring.free(k, t)
                return t
            act.wait(used["z"])
            for f in range(FC):
                t = act.do(nc.scalar.activation(z[:, P * f:P * f + P], slot[:, P * f:P * f + P], ACT.Identity, bias=bias(f)))
            h_ring.free(k, t)
            dve.wait(t)
            t = dve.do(nc.vector.tensor_scalar(ez[:], z[:], 0.0, None, ALU.min))
            act.wait(t)
            t = act.do(nc.scalar.activation(ez[:], ez[:], ACT.Exp))
            dve.wait(t)
            dve.seq(nc.vector.tensor_scalar(ez[:], ez[:], ALPHA, ALPHA, ALU.mult, ALU.subtract))
            dve.wait(used["hT"][p])
            t = dve.seq(nc.vector.scalar_tensor_tensor(hT[:, p, :, :].rearrange("p f n -> p (f n)"), z[:], 0.0, ez[:],
                                                       ALU.max, ALU.add))
            used["z"] = t
            return t

        def projected(e, p, after, to, free):
            pe.wait(after)
            k, slot = y_ring.take()
            for f in range(FC):
                m = nc.tensor.matmul(slot[:, 0:D], hT[:, p, f, :],
                                     w2[:, e[0], f, :] if isinstance(e[0], int) else
                                     w2[:, bass.ds(e[0], 1), f, :].rearrange("p a n -> p (a n)"),
                                     start=f == 0, stop=f == FC - 1)
            used["hT"][p] = pe.do(m)
            dve.wait(used["hT"][p], free)
            t = dve.do(nc.vector.scalar_tensor_tensor(
                to, slot[:, 0:D], scale, b2[:, e[1], :] if isinstance(e[1], int) else
                b2[:, bass.ds(e[1], 1), :].rearrange("p a n -> p (a n)"), ALU.mult, ALU.add))
            y_ring.free(k, t)
            return t

        if kind == "selu":
            top = sb("top", [P, NT, 8])
            top_i = sb("top_i", [P, NT, 8], U32)
            topf = sb("topf", [P, 2, NT])
            sums = sb("sums", [P, NT])
            pe.wait(ld[NE].now())
            for n in range(NT):
                t = hidden(lambda c: xnT[:, c, P * n:P * n + P], 0, NE, n % 2)
                t = projected((NE, NE), n % 2, t, y[:, n % 2, :], None)
                dve.wait(t)
                dve.seq(nc.vector.max(top[:, n, :], y[:, n % 2, :]))
                dve.seq(nc.vector.max_index(top_i[:, n, :], top[:, n, :], y[:, n % 2, :]))
            dve.seq(nc.vector.tensor_copy(topf[:].rearrange("p k n -> p n k"), top_i[:, :, 0:2]))
            dve.seq(nc.vector.tensor_tensor(sums[:], top[:, :, 0], top[:, :, 1], ALU.add))
            dve.seq(nc.vector.reciprocal(sums[:], sums[:]))
            for k in range(K):
                dve.seq(nc.vector.tensor_tensor(wk[:, NT * k:NT * k + NT], top[:, :, k], sums[:], ALU.mult))
            chosen = topf[:].rearrange("p k n -> p (k n)")
        else:
            pr, red = sb("pr", [P, NT, NE]), sb("red", [P, 3, NT])
            k, slot = t_ring.take()
            lg = slot[:, 0:NT * NE].rearrange("p (n e) -> p n e", e=NE)
            for n in range(NT):
                for c in range(DC):
                    m = nc.tensor.matmul(lg[:, n, :], xnT[:, c, P * n:P * n + P], gw[:, c, :],
                                         start=c == 0, stop=c == DC - 1)
            dve.wait(pe.do(m))
            dve.seq(nc.vector.tensor_reduce(red[:, 0, :], lg, AX.X, ALU.max))
            over = lambda r: r.rearrange("p (n a) -> p n a", a=1).to_broadcast([P, NT, NE])
            t = dve.seq(nc.vector.tensor_tensor(pr[:], lg, over(red[:, 0, :]), ALU.subtract))
            t_ring.free(k, t)
            act.wait(t)
            t = act.do(nc.scalar.activation(pr[:], pr[:], ACT.Exp))
            dve.wait(t)
            dve.seq(nc.vector.tensor_reduce(red[:, 1, :], pr[:], AX.X, ALU.add))
            dve.seq(nc.vector.reciprocal(red[:, 1, :], red[:, 1, :]))
            dve.seq(nc.vector.tensor_tensor(pr[:], pr[:], over(red[:, 1, :]), ALU.mult))
            dve.seq(nc.vector.tensor_reduce(wk[:], pr[:], AX.X, ALU.max))
            dve.seq(nc.vector.tensor_tensor(pr[:], pr[:], over(wk[:]), ALU.is_lt))
            dve.seq(nc.vector.scalar_tensor_tensor(pr[:].rearrange("p n e -> p (n e)"), pr[:].rearrange("p n e -> p (n e)"), float(NE),
                                                   cst["iota_e"][:, 0:NT * NE], ALU.mult, ALU.add))
            dve.seq(nc.vector.tensor_reduce(red[:, 2, :], pr[:], AX.X, ALU.min))
            chosen = red[:, 2, :]
        iota = cst["iota_e"][:, 0:K * NT * NE].rearrange("p (n e) -> p n e", e=NE)
        overk = lambda r: r.rearrange("p (n a) -> p n a", a=1).to_broadcast([P, K * NT, NE])
        dve.seq(nc.vector.tensor_tensor(oh[:], iota, overk(chosen), ALU.is_equal))

        rank, tot = sb("rank", [P, K * NT, NE]), sb("tot", [P, 2, K * NT, NE])
        flat = oh[:].rearrange("p n e -> p (n e)")
        pe.wait(dve.done.now())
        k, slot = t_ring.take()
        k2, slot2 = t_ring.take()
        n_all = K * NT * NE
        nc.tensor.matmul(slot[:, 0:n_all], cst["tri"][:], flat, start=True, stop=True)
        dve.wait(pe.do(nc.tensor.matmul(slot2[:, 0:n_all], cst["ones"][:], flat, start=True, stop=True)))
        dve.do(nc.vector.tensor_copy(tot[:, 0, :, :].rearrange("p n e -> p (n e)"), slot2[:, 0:n_all]))
        t = dve.seq(nc.vector.tensor_copy(rank[:].rearrange("p n e -> p (n e)"), slot[:, 0:n_all]))
        t_ring.free(k, t)
        t_ring.free(k2, t)
        a, step = 0, 1
        while step < K * NT:
            dve.do(nc.vector.tensor_copy(tot[:, 1 - a, 0:step, :], tot[:, a, 0:step, :]))
            dve.seq(nc.vector.tensor_tensor(tot[:, 1 - a, step:, :], tot[:, a, step:, :], tot[:, a, 0:K * NT - step, :], ALU.add))
            a, step = 1 - a, 2 * step
        dve.seq(nc.vector.tensor_tensor(rank[:, 1:, :], rank[:, 1:, :], tot[:, a, 0:K * NT - 1, :], ALU.add))
        base = sb("base", [P, 2, NE])
        ends = sb("ends", [P, NE])
        if kind == "gelu":
            dve.do(nc.vector.tensor_scalar(base[:, 0, :], cst["iota_e"][:, 0:NE], float(CAP), None, ALU.mult))
            dve.seq(nc.vector.tensor_scalar(ends[:], cst["iota_e"][:, 0:NE], float(CAP), float(CAP), ALU.mult, ALU.add))
        else:
            cnt = sb("cnt", [P, NE], I32)
            dve.seq(nc.vector.tensor_scalar(ends[:], tot[:, a, K * NT - 1, :], float(P - 1), None, ALU.add))
            dve.seq(nc.vector.tensor_copy(cnt[:], ends[:]))
            dve.seq(nc.vector.tensor_scalar(cnt[:], cnt[:], 7, 7, ALU.arith_shift_right, ALU.arith_shift_left))
            dve.seq(nc.vector.tensor_copy(ends[:], cnt[:]))
            dve.seq(nc.vector.tensor_copy(base[:, 0, :], ends[:]))
            c0, step = 0, 1
            while step < NE:
                dve.do(nc.vector.tensor_copy(base[:, 1 - c0, 0:step], base[:, c0, 0:step]))
                dve.seq(nc.vector.tensor_tensor(base[:, 1 - c0, step:], base[:, c0, step:], base[:, c0, 0:NE - step], ALU.add))
                c0, step = 1 - c0, 2 * step
            dve.seq(nc.vector.tensor_tensor(base[:, 1 - c0, :], base[:, c0, :], ends[:], ALU.subtract))
            dve.seq(nc.vector.tensor_copy(ends[:], base[:, c0, :]))
            if c0 == 0:
                dve.seq(nc.vector.tensor_copy(base[:, 0, :], base[:, 1, :]))
        if kind == "gelu":
            dve.seq(nc.vector.tensor_scalar(tot[:, 0, :, :], rank[:], float(CAP), None, ALU.is_le))
            dve.seq(nc.vector.tensor_tensor(oh[:], oh[:], tot[:, 0, :, :], ALU.mult))
        bb = base[:, 0:1, :].to_broadcast([P, K * NT, NE])
        dve.seq(nc.vector.tensor_tensor(rank[:], rank[:], bb, ALU.add))
        dve.seq(nc.vector.tensor_scalar(rank[:], rank[:], -1.0, None, ALU.add))
        dve.seq(nc.vector.tensor_tensor(rank[:], rank[:], oh[:], ALU.mult))
        dve.seq(nc.vector.tensor_reduce(slot_f[:], rank[:], AX.X, ALU.add))
        dve.seq(nc.vector.tensor_copy(slot_u[:], slot_f[:]))
        dve.seq(nc.vector.tensor_reduce(valid[:], oh[:], AX.X, ALU.add))
        dve.seq(nc.vector.tensor_tensor(wk[:], wk[:], valid[:], ALU.mult))
        dve.seq(nc.vector.tensor_scalar(valid[:], valid[:], -1.0, 1.0, ALU.mult, ALU.add))
        dve.seq(nc.vector.tensor_tensor(valid[:], valid[:], cst["aside"][:, 0:K * NT], ALU.mult))
        dve.seq(nc.vector.tensor_tensor(slot_f[:], slot_f[:], valid[:], ALU.add))
        dve.seq(nc.vector.tensor_copy(to_u[:], slot_f[:]))
        dve.seq(nc.vector.tensor_scalar(wk[:], wk[:], gate, None, ALU.mult))
        te = sb("te", [1, 2, 64])
        dve.seq(nc.vector.tensor_scalar(te[:, 0, :], cst["starts"][0:1, :], ends[0:1, 0:1], None, ALU.is_ge))
        for e in range(1, NE - 1):
            dve.seq(nc.vector.scalar_tensor_tensor(te[:, e % 2, :], cst["starts"][0:1, :], ends[0:1, e:e + 1],
                                                   te[:, 1 - e % 2, :], ALU.is_ge, ALU.add))
        routed = dve.seq(nc.vector.tensor_copy(tile_e[:], te[:, (NE - 2) % 2, :]))

        xn = sb("xn", [P, 2, D])
        sent = [None, None]
        sc_s = [pg.stream("sc0"), pg.stream("sc1")]
        pool.wait(dram["zeroed"], routed)
        for n in range(NT):
            p = n % 2
            dve.wait(sent[p])
            t = dve.do(nc.vector.tensor_scalar(xn[:, p, :], x[:, n, :], cst["mv"][:, n, 0:1], cst["rstd"][:, n:n + 1],
                                               ALU.subtract, ALU.mult))
            pool.wait(t)
            for k in range(K):
                sc_s[p].after(nc.gpsimd.indirect_dma_start(
                    out=xs, out_offset=bass.IndirectOffsetOnAxis(ap=to_u[:, k * NT + n:k * NT + n + 1], axis=0),
                    in_=xn[:, p, :], in_offset=None))
            sent[p] = sc_s[p].now()
        sp.wait(*sent)

        wl = [pg.stream("wl0"), pg.stream("wl1")]
        xl, yl = [pg.stream("xl0"), pg.stream("xl1")], [pg.stream("yl0"), pg.stream("yl1")]
        for e in range(NE):
            pe.wait(ld[e].now())
        pool.wait(*sent, routed)
        pe.wait(routed)
        act.wait(routed)
        dve.wait(routed)
        st = dict(w1=[None, None], arrived=[None, None], xT=[None, None], xTt=[None, None], h=[None, None])

        def load(m, p):
            sp.wait(used["x"][p])
            st["arrived"][p] = sp.dma(xl[p], xt[:, p, :], xs[bass.ds(m * P, P), :])

        def turn(p):
            act.wait(used["xT"][p])
            st["xTt"][p] = transposed(pg, t_ring, xtT[:, p, :, :], xt[:, p, :], cst, st["arrived"][p])
            used["x"][p] = pe.done.now()

        def expert_of(eng, m):
            return eng.eng.value_load(tile_e[0:1, bass.ds(m, 1)], min_val=0, max_val=NE - 1)

        def weights(m, p):
            e = expert_of(pool, m)
            pool.wait(used["w1"][p])
            st["w1"][p] = wl[p].after(nc.gpsimd.dma_start(
                w1[:, p, :, :], w["w1"][bass.ds(e, 1), :, :].rearrange("a (c p) f -> p (a c) f", p=P)))

        def up(m, p):
            e = expert_of(act, m)
            pe.wait(st["xTt"][p], st["w1"][p])
            st["h"][p] = hidden(lambda c: xtT[:, p, c, :], p, e, p)
            used["xT"][p] = used["w1"][p] = pe.done.now()

        def down(m, p):
            e = (expert_of(pe, m), expert_of(dve, m))
            t = projected(e, p, st["h"][p], y[:, p, :], used["y"][p])
            sp.wait(t)
            used["y"][p] = sp.dma(yl[p], ys[bass.ds(m * P, P), :], y[:, p, :])

        dve.wait(dve.done.now())
        sp.wait(dve.do(nc.vector.memset(y[:], 0.0)))
        for p in range(2):
            used["y"][p] = sp.dma(yl[p], ys[(MOST + p) * P:(MOST + p + 1) * P, :], y[:, p, :])
            used["w1"][p] = pe.done.now()
            weights(p, p)
        load(0, 0)
        load(1, 1)
        turn(0)
        up(0, 0)
        weights(2, 0)
        load(2, 0)
        turn(1)
        uid = pg.n_names
        rounds = (M - 1) // 2
        kept = [("used", k) for k in ("hT", "x", "xT", "y", "w1")] + [("st", k) for k in ("w1", "arrived", "xTt", "h")]
        where = {"used": used, "st": st}
        for e in pg.engines:
            e.wait(*[where[a][k][p] for a, k in kept for p in range(2)], used["z"])
        with pg.loop(rounds) as i:
            for a, k in kept:
                for p in range(2):
                    where[a][k][p] = pg.last_round(f"{a}{k}{p}@{uid}")
            used["z"] = pg.last_round(f"z@{uid}")
            for p in (1, 0):
                m = i * 2 + (1 if p else 2)
                up(m, p)
                weights(m + 2, p)
                load(m + 2, p)
                turn(1 - p)
                down(m - 1, 1 - p)
            for a, k in kept:
                for p in range(2):
                    if where[a][k][p] is not None and not isinstance(where[a][k][p], LastRound):
                        pg.keep(f"{a}{k}{p}@{uid}", where[a][k][p])
            if used["z"] is not None and not isinstance(used["z"], LastRound):
                pg.keep(f"z@{uid}", used["z"])
        m = 2 * rounds + 1
        if m < M:
            up(m, 1)
            down(m - 1, 0)
            down(m, 1)
        else:
            down(m - 1, 0)
        yg = sb("yg", [P, 2, D])
        got = [pg.stream("got0"), pg.stream("got1")]
        pool.wait(*used["y"])
        taken = [None, None]
        q = 0
        for n in range(NT):
            for k in range(K):
                p = q % 2
                q += 1
                pool.wait(taken[p])
                t = got[p].after(nc.gpsimd.indirect_dma_start(
                    out=yg[:, p, :], out_offset=None, in_=ys,
                    in_offset=bass.IndirectOffsetOnAxis(ap=slot_u[:, k * NT + n:k * NT + n + 1], axis=0)))
                dve.wait(t, dve.done.now())
                taken[p] = dve.do(nc.vector.scalar_tensor_tensor(
                    x[:, n, :], yg[:, p, :], wk[:, k * NT + n:k * NT + n + 1], x[:, n, :], ALU.mult, ALU.add))
        for r in (h_ring, t_ring, y_ring):
            pg.rings.remove(r)


def masked_keys(pg, cst, mask, maskrow, live):
    nc, pe, dve, sp = pg.nc, pg.pe, pg.dve, pg.sp
    with ExitStack() as ctx:
        mi = pg.sbuf(ctx, "mi", [B, S2], I32)
        off, any_, dg = pg.sbuf(ctx, "off", [B, S2]), pg.sbuf(ctx, "any", [B, 1]), pg.sbuf(ctx, "dg", [B, B])
        row = pg.sbuf(ctx, "row", [B, S2], BF16)
        ps = pg.psum(ctx, "ps", [P, B])
        ld = pg.stream("mask")
        sp.dma(ld, mi[:], mask.rearrange("b x y k -> (b x y) k"))
        dve.wait(ld.now())
        dve.seq(nc.vector.tensor_copy(off[:], mi[:]))
        dve.seq(nc.vector.tensor_scalar(off[:], off[:], 0.0, None, ALU.is_equal))
        dve.seq(nc.vector.tensor_reduce(any_[:], off[:], AX.X, ALU.min))
        dve.seq(nc.vector.tensor_scalar(any_[:], any_[:], -1.0, 1.0, ALU.mult, ALU.add))
        dve.seq(nc.vector.tensor_scalar(off[:], off[:], any_[:, 0:1], -1e30, ALU.mult, ALU.mult))
        t = dve.seq(nc.vector.tensor_copy(row[:], off[:]))
        sp.wait(t)
        st = pg.stream("maskrow")
        out = sp.dma(st, maskrow, row[:])
        t = dve.seq(nc.vector.tensor_scalar(dg[:], cst["ident"][0:B, 0:B], any_[:, 0:1], None, ALU.mult))
        pe.wait(t)
        t = pe.do(nc.tensor.matmul(ps[:], cst["ones"][0:B, :], dg[:], start=True, stop=True))
        dve.wait(t)
        dve.seq(nc.vector.tensor_copy(live[:], ps[:]))
        sp.wait(out)
        return out


def build(nc, a, loops):
    with ExitStack() as ctx:
        pg = Program(nc, ctx, loops)
        pe, act, dve, pool, sp = pg.pe, pg.act, pg.dve, pg.pool, pg.sp
        x, xnT = pg.sbuf(ctx, "x", [P, NT, D]), pg.sbuf(ctx, "xnT", [P, DC, N])
        cst = {n: pg.sbuf(ctx, n, s) for n, s in (
            ("ident", [P, P]), ("sel", [P, P]), ("tri", [P, P]), ("ones", [P, P]), ("mhalf", [P, NT]),
            ("iota_e", [P, 2 * NT * NE]), ("aside", [P, 2 * NT]), ("starts", [1, 64]), ("mv", [P, NT, 2]), ("rstd", [P, NT]))}
        cst["identb"] = pg.sbuf(ctx, "identb", [P, P], BF16)
        zero = pg.sbuf(ctx, "zero", [P, D])
        gates, live = pg.sbuf(ctx, "gates", [P, 8]), pg.sbuf(ctx, "live", [P, B])
        dram = {}
        for n, s, dt in (("xs", [(MOST + 2) * P + 2 * N, D], F32), ("ys", [(MOST + 2) * P, D], F32), ("kparts", [3, D, S2], BF16),
                         ("qparts", [3, D, T], BF16), ("maskrow", [B, S2], BF16)):
            dram[n] = nc.dram_tensor(n, s, dt).ap()

        ld = pg.stream("constants")
        for n in ("ident", "sel", "tri", "iota_e", "aside", "starts"):
            sp.dma(ld, cst[n][:], a[n])
        sp.dma(ld, x[:], a["x"].rearrange("b (t p) d -> p (b t) d", p=P))
        with nc.allow_non_contiguous_dma("8 numbers"):
            for k, n in enumerate(("g_xattn", "g_ffn")):
                sp.dma(ld, gates[:, 4 * k:4 * k + 4], a[n].rearrange("(a n) -> a n", a=1).to_broadcast([P, 4]))
        for e in (dve, act, pe, pool):
            e.wait(ld.now())
        dve.do(nc.vector.memset(cst["ones"][:], 1.0))
        dve.do(nc.vector.memset(cst["mhalf"][:], -0.5))
        dve.do(nc.vector.tensor_copy(cst["identb"][:], cst["ident"][:]))
        dve.wait(act.do(nc.scalar.activation(gates[:], gates[:], ACT.Tanh)))
        for e in (dve, act, pe, pool):
            e.wait(dve.done.now())

        with ExitStack() as c:
            dve.do(nc.vector.memset(zero[:], 0.0))
            masked = masked_keys(pg, cst, a["mask"], dram["maskrow"], live)
            for e in pg.engines:
                e.wait(dve.done.now(), masked)

        def norm(psum=None, stats=None, xn=None):
            with ExitStack() as c:
                if psum is None:
                    pg.barrier()
                    psum = [pg.psum(c, f"t{i}", [P, 512])[:] for i in range(3)]
                    stats, xn = pg.sbuf(c, "stats", [P, NT, 6]), pg.sbuf(c, "xn", [P, 4, D])
                yield from normalised(pg, x, xnT, cst, psum, stats, xn)

        for layer in range(4):
            w = {n: a[f"L{layer}_{n}"] for n in ("wq", "bq", "wk", "bk", "wv", "bv", "wo", "bo")}
            if layer == 1:
                w |= {n: a[f"L1_{n}"] for n in ("wqr", "bqr", "wkr", "bkr")}
            w |= dict(ctxT=a["ctxT"], kparts=dram["kparts"], qparts=dram["qparts"])
            g_x, g_f = gates[:, layer:layer + 1], gates[:, 4 + layer:5 + layer]
            if layer < 3:
                head_attention(pg, x, xnT, cst, w, g_x, 1 / 16 if layer == 2 else 1 / 4, norm,
                               a["rope"] if layer == 1 else None, (dram["maskrow"], live) if layer else None)
            else:
                drain(norm())
                wide_attention(pg, x, xnT, cst, w, g_x)
            drain(norm())
            if layer == 0:
                zs = pg.stream("zeroed")
                for n in range(MOST + 2):
                    for m in ("xs", "ys"):
                        sp.dma(zs, dram[m][P * n:P * n + P, :], zero[:])
                dram["zeroed"] = zs.now()
                quantised_linear(pg, x, xnT, cst, a["L0_weight"], a["hadamard"], g_f)
            else:
                names = ("gate", "w1", "b1", "w2", "b2") if layer < 3 else ("gw1", "gb1", "gw2", "gb2", "w1", "b1", "w2", "b2")
                experts(pg, x, xnT, cst, {n: a[f"L{layer}_{n}"] for n in names}, g_f,
                        (None, "relu", "gelu", "selu")[layer], dram)
        pg.barrier()
        o = pg.stream("out")
        sp.dma(o, a["out"].rearrange("b (t p) d -> p (b t) d", p=P), x[:])
        sp.wait(o.now())
        sp.flush()
        return pg.measured


def constants():
    f = np.float32
    c = {"ident": np.eye(P, dtype=f)}
    p = np.arange(P)
    c["sel"] = (p[:, None] == 32 * (p[None, :] // 32) + HD).astype(f)
    c["tri"] = (p[:, None] <= p[None, :]).astype(f)
    c["iota_e"] = np.tile(np.arange(NE, dtype=f), (P, 2 * NT))
    c["aside"] = ((MOST + 2) * P + P * np.arange(2 * NT)[None, :] + p[:, None]).astype(f)
    c["starts"] = (P * np.arange(64, dtype=f))[None, :]
    inv = f(1.0) / f(10000.0) ** (np.arange(0, HD, 2, dtype=f) / f(HD))
    emb = np.arange(S2, dtype=f)[:, None] * inv[None, :]
    emb = np.concatenate([emb, emb], axis=-1).T
    sign = np.where(np.arange(HD) < HD // 2, -1, 1).astype(f)[:, None]
    c["rope"] = np.ascontiguousarray(np.tile(np.stack([np.cos(emb), np.sin(emb) * sign], 1), (P // HD, 1, 1)))
    h = np.array([[1.0]])
    while h.shape[0] < D:
        h = np.block([[h, h], [h, -h]])
    c["hadamard"] = (h / np.sqrt(D)).astype(f)
    return c


def laid_out(i):
    out = dict(x=i["x"], ctxT=i["ctx_1024"].transpose(0, 2, 1), mask=i["mask_Bx1x1xS2_if1"], g_xattn=i["g_xattn"],
               g_ffn=i["g_ffn"], L0_weight=i["L0_ffn_weight"])
    for n in range(4):
        for m in "qkvo":
            w = i[f"L{n}_xattn_W{m}"]
            out[f"L{n}_w{m}"] = w.T if n in (0, 2) else w
            out[f"L{n}_b{m}"] = i[f"L{n}_xattn_b{m}"]
    halves = (HD * np.arange(H)[:, None] + np.roll(np.arange(HD), HD // 2)[None, :]).reshape(-1)
    for m in "qk":
        out[f"L1_w{m}r"], out[f"L1_b{m}r"] = out[f"L1_w{m}"][:, halves], out[f"L1_b{m}"][halves]
    out["L1_gate"], out["L2_gate"] = i["L1_ffn_gate_w"].T, i["L2_ffn_wg"]
    for n in (1, 2):
        for m in ("w1", "b1", "w2", "b2"):
            out[f"L{n}_{m}"] = i[f"L{n}_ffn_{m}"]
    for k, m in (("w1", "wi"), ("b1", "bi"), ("w2", "wo"), ("b2", "bo")):
        out[f"L3_g{k}"], out[f"L3_{k}"] = i[f"L3_ffn_gate_{m}"], i[f"L3_ffn_exp_{m}"]
    return {n: np.ascontiguousarray(a) for n, a in out.items()}


def kernel(**inputs):
    import concourse.bacc as bacc
    from concourse.bass_utils import run_bass_kernel_spmd

    arrays = laid_out({n: np.asarray(v) for n, v in inputs.items()}) | constants()

    def program(loops):
        nc = bacc.Bacc("TRN2", target_bir_lowering=False, num_devices=1)
        a = {n: nc.dram_tensor(f"in_{n}", v.shape, mybir.dt.from_np(v.dtype), kind="ExternalInput").ap()
             for n, v in arrays.items()}
        a["out"] = nc.dram_tensor("out_x", (B, T, D), F32, kind="ExternalOutput").ap()
        return nc, build(nc, a, loops)

    _, loops = program([])
    nc, _ = program(loops)
    r = run_bass_kernel_spmd(nc, [{f"in_{n}": v for n, v in arrays.items()}], core_ids=[0])
    return r.results[0]["out_x"]
```

```python
from contextlib import ExitStack, contextmanager

import numpy as np

import concourse.bass as bass
import concourse.mybir as mybir

F32, BF16, I32 = mybir.dt.float32, mybir.dt.bfloat16, mybir.dt.int32
U32 = mybir.dt.uint32
ALU, ACT, AX = mybir.AluOpType, mybir.ActivationFunctionType, mybir.AxisListType

B, T, D, S2 = 4, 512, 256, 1601
N = B * T
H, HD = 16, 16
NE, FF = 8, 1024
P = 128
TT = T // P
NT = N // P
DC = D // P
FC = FF // P
KT = -(-S2 // P)
KW = [min(P, S2 - P * k) for k in range(KT)]
MOST = 2 * N // P + NE - 1
XTILES = MOST + 3
EPS = 1e-5


class Tick:

    def __init__(self, stream, scope, base, local):
        self.stream, self.scope, self.base, self.local = stream, scope, base, local


class LastRound(Tick):
    pass


class Scope:

    def __init__(self, index, count, per):
        self.index, self.count, self.per = index, count, per


class Stream:

    def __init__(self, prog, name, step=1):
        self.prog, self.name, self.step = prog, name, step
        self.sem = prog.ctx.enter_context(prog.nc.semaphore(name))
        self.base, self.local = 0, 0
        prog.streams.append(self)

    def now(self):
        return Tick(self, self.prog.scope, self.base, self.local)

    def after(self, instruction):
        instruction.then_inc(self.sem, self.step)
        self.local += self.step
        return self.now()


class Engine:

    def __init__(self, prog, name, eng):
        self.prog, self.eng = prog, eng
        self.done = Stream(prog, f"{name}_done")
        self.seen, self.pending = {}, []

    def wait(self, *ticks):
        todo = [w for w in map(self.value, ticks) if w is not None]
        if self is self.prog.sp:
            self.pending += todo
            return
        for sem, v in todo:
            self.eng.wait_ge(sem, v)

    def flush(self):
        todo = [(sem, v if isinstance(v, int) else self.eng.to_reg(v)) for sem, v in self.pending]
        self.pending = []
        for sem, v in todo:
            self.eng.wait_ge(sem, v)

    def dma(self, stream, out, in_):
        self.flush()
        return stream.after(self.eng.dma_start(out, in_))

    def value(self, t):
        if t is None:
            return None
        scope, s = self.prog.scope, t.stream
        if isinstance(t, LastRound):
            per = scope.per.get(s.name, 1)
            back = t.local - per
            if t.base + back <= 0:
                back = 0
            assert t.base > 0 and back <= 0, (s.name, t.base, t.local, per)
            return s.sem, scope.index * per + (t.base + back)
        if t.scope is not None and scope is None:
            total = t.base + (t.scope.count - 1) * t.scope.per.get(s.name, 1) + t.local
        else:
            assert t.scope is None or t.scope is scope
            total = t.base + t.local
        key = (s.name, scope, t.scope)
        if self.seen.get(key, 0) >= total:
            return None
        self.seen[key] = total
        if t.scope is not None and scope is not None:
            return s.sem, scope.index * scope.per.get(s.name, 1) + total
        return s.sem, total

    def do(self, instruction):
        return self.done.after(instruction)

    def seq(self, instruction):
        t = self.do(instruction)
        self.wait(t)
        return t


class Program:
    def __init__(self, nc, ctx, loops):
        self.nc, self.ctx, self.loops = nc, ctx, loops
        self.scope, self.streams, self.n_loops, self.measured = None, [], 0, []
        self.pe = Engine(self, "pe", nc.tensor)
        self.act = Engine(self, "act", nc.scalar)
        self.dve = Engine(self, "dve", nc.vector)
        self.pool = Engine(self, "pool", nc.gpsimd)
        self.sp = Engine(self, "sp", nc.sync)
        self.engines = [self.pe, self.act, self.dve, self.pool, self.sp]
        self.n_names = 0
        self.rings, self.kept = [], {}

    def sbuf(self, ctx, name, shape, dt=F32):
        self.n_names += 1
        return ctx.enter_context(self.nc.sbuf_tensor(f"{name}_{self.n_names}", shape, dt))

    def psum(self, ctx, name, shape, dt=F32):
        self.n_names += 1
        return ctx.enter_context(self.nc.psum_tensor(f"{name}_{self.n_names}", shape, dt))

    def stream(self, name, step=16):
        self.n_names += 1
        return Stream(self, f"{name}_{self.n_names}", step)

    @contextmanager
    def loop(self, count):
        n = self.n_loops
        self.n_loops += 1
        per = self.loops[n] if n < len(self.loops) else {}
        for s in self.streams:
            s.base, s.local = s.base + s.local, 0
        made = len(self.streams)
        for r in self.rings:
            r.enter(per)
        self.sp.flush()
        self.kept = {}
        with self.nc.Fori(0, count) as index:
            self.scope = Scope(index, count, per)
            yield index
            for r in self.rings:
                r.leave()
            assert not self.sp.pending
        self.scope = None
        assert made == len(self.streams)
        self.measured.append({s.name: s.local for s in self.streams if s.local} | self.kept)
        for s in self.streams:
            s.base, s.local = s.base + count * s.local, 0

    def keep(self, name, tick):
        self.kept["@" + name] = (tick.stream.name, tick.local)

    def last_round(self, name):
        if "@" + name not in self.scope.per:
            return None
        where, local = self.scope.per["@" + name]
        s = next(s for s in self.streams if s.name == where)
        return LastRound(s, self.scope, s.base, local)

    def barrier(self):
        for e in self.engines:
            if e.done.base + e.done.local:
                for other in self.engines:
                    other.wait(e.done.now())


def drain(*generators):
    for g in generators:
        for _ in g:
            pass


class Ring:

    def __init__(self, prog, name, slots):
        self.prog, self.name, self.slots = prog, name, slots
        self.n, self.freed = 0, [None] * len(slots)
        prog.rings.append(self)

    def take(self):
        i = self.n % len(self.slots)
        self.n += 1
        self.prog.pe.wait(self.freed[i])
        return i, self.slots[i]

    def free(self, i, tick):
        self.freed[i] = tick

    def enter(self, per):
        self.prog.pe.wait(*self.freed)
        self.n, self.freed = 0, [None] * len(self.slots)
        for i in range(len(self.slots)):
            if f"@{self.name}{i}" in per:
                where, local = per[f"@{self.name}{i}"]
                s = next(s for s in self.prog.streams if s.name == where)
                self.freed[i] = LastRound(s, None, s.base, local)

    def leave(self):
        for i, t in enumerate(self.freed):
            if t is not None and not isinstance(t, LastRound):
                self.prog.keep(f"{self.name}{i}", t)


def normalised(pg, x, xnT, cst, psum, stats, xn):
    nc, pe, act, dve, pool = pg.nc, pg.pe, pg.act, pg.dve, pg.pool
    G = 4
    with ExitStack() as ctx:
        mv, rstd = cst["mv"], cst["rstd"]
        for n in range(NT):
            dve.do(nc.vector.bn_stats(stats[:, n, :], x[:, n, :]))
        dve.wait(dve.done.now())
        for n in range(NT):
            dve.do(nc.vector.bn_aggr(mv[:, n, :], stats[:, n, :]))
        dve.wait(dve.done.now())
        t = dve.do(nc.vector.tensor_scalar(rstd[:], mv[:, :, 1], EPS, None, ALU.add))
        pool.wait(t)
        t = pool.do(nc.gpsimd.tensor_tensor(rstd[:], rstd[:], cst["mhalf"][:, 0:NT], ALU.pow))
        dve.wait(t)
        yield
        uid = pg.n_names
        ring = Ring(pg, f"t_ring{uid}", psum)
        used = None
        with pg.loop(NT // G) as i:
            for g in range(G):
                dve.wait(pg.last_round(f"xn{g}@{uid}"))
                n = bass.ds(i * G + g, 1)
                t = dve.do(nc.vector.tensor_scalar(
                    xn[:, g, :], x[:, n, :].rearrange("p a n -> p (a n)"), mv[:, n, 0:1].rearrange("p a n -> p (a n)"),
                    rstd[:, n], ALU.subtract, ALU.mult))
                pe.wait(t)
                k, slot = ring.take()
                for c in range(DC):
                    m = nc.tensor.transpose(slot[:, P * c:P * c + P], xn[:, g, P * c:P * c + P], cst["ident"][:])
                used = pe.do(m)
                act.wait(used)
                pg.keep(f"xn{g}@{uid}", used)
                t = act.do(nc.scalar.copy(xnT[:, :, bass.ds((i * G + g) * P, P)],
                                          slot[:, 0:D].rearrange("p (c n) -> p c n", c=DC)))
                ring.free(k, t)
        done = act.done.now()
        pe.wait(done)
        dve.wait(done, pe.done.now())
        pg.rings.remove(ring)


RUNS = ((0, 0, 3), (3, 1, 2), (5, 2, 1))
R_MASK = 16 * 6
R_MAX = R_MASK + 1
R_ALL = R_MAX + 3
HG = 4
NG = H // HG
QC = T // P
VW = HD + 1
VG = HG * VW + 32 - VW
PIECE = 400
CHUNKS = [(c, min(512, S2 - c)) for c in range(0, S2, 512)]


def split3(e, one, rest, src, parts, have=0):
    if not have:
        e.seq(e.eng.tensor_tensor(parts[0], src, one, ALU.mult))
    e.seq(e.eng.tensor_tensor(rest, src, parts[0], ALU.subtract))
    e.seq(e.eng.tensor_tensor(parts[1], rest, one, ALU.mult))
    return e.do(e.eng.tensor_tensor(parts[2], rest, parts[1], ALU.subtract))


def head_attention(pg, x, xnT, cst, w, gate, scale, norm, rope=None, mask=None):
    nc, pe, act, dve, pool, sp = pg.nc, pg.pe, pg.act, pg.dve, pg.pool, pg.sp
    pg.barrier()
    with ExitStack() as ctx:
        sb = lambda name, shape, dt=F32: pg.sbuf(ctx, name, shape, dt)
        wq, wk, wv = (sb(n, [P, DC, D]) for n in ("wq", "wk", "wv"))
        bq, bk = sb("bq", [P, DC]), sb("bk", [P, DC])
        if rope:
            wqr, wkr = sb("wqr", [P, DC, D]), sb("wkr", [P, DC, D])
            bqr, bkr = sb("bqr", [P, DC]), sb("bkr", [P, DC])
            turn = sb("turn", [P, 2, 2, 512])
        woa = sb("woa", [P, NG, D])
        bva = sb("bva", [P, NG])
        bob = sb("bob", [P, D])
        ctxb = sb("ctxb", [P, 2, DC, 512])
        kf = sb("kf", [P, 2, 512])
        kr = sb("kr", [P, 2, 512])
        ks = sb("ks", [P, 2, 3, 512], BF16)
        kaug = sb("kaug", [P, NG, HG, S2], BF16)
        qaug = sb("qaug", [P, NG, HG, T], BF16)
        v = sb("v", [P, KT, NG, VG])
        vn = sb("vn", [P, KT, NG, HG, HD])
        e_t = sb("e_t", [P, 2, HG, T])
        mxp = sb("mxp", [P, 2, 2, HG * QC])
        mx = sb("mx", [P, 2, HG * QC])
        nm = sb("nm", [P, P // (HG * QC), HG * QC], BF16)
        tm = sb("tm", [P, P], BF16)
        z, r = sb("z", [P, T]), sb("r", [P, T])
        bvr = z[:].rearrange("p (g n) -> p g n", g=NG)
        rc = sb("rc", [P, HG * QC])
        one_sum = cst["sel"][:].rearrange("p (j n) -> p j n", n=P // HG)[:, :, 0]
        ot = sb("ot", [P, NG, T])
        live_now = sb("live_now", [P, 1])

        s_ring = Ring(pg, f"s_ring{pg.n_names}", [pg.psum(ctx, f"s{i}", [P, 512]) for i in range(3)])
        m_ring = Ring(pg, f"m_ring{pg.n_names}", [pg.psum(ctx, f"m{i}", [P, 1024]) for i in range(2)])
        pv = pg.psum(ctx, "pv", [P, T])

        cd = [pg.stream(f"ctx{n}") for n in range(len(CHUNKS))]
        kd = [pg.stream(f"kd{g}") for g in range(NG)]
        td = pg.stream("td")
        stored = [pg.stream(f"stored{n}") for n in range(3)]
        rd = [pg.stream("turn0"), pg.stream("turn1")]
        st = dict(kf=[None] * 3, ctx=[None] * 4, put=[None] * 3, turn=[None, None], e=[None, None],
                  k_free=[None] * NG, v_free=[None] * NG, arrived=[None] * NG, v=[None] * NG, td=[None] * NG,
                  z=[None], ot=[None], nm=[None], norm=[None], vn=[None], taken=[None],
                  peaks=[None] * 2, live=[None], live_now=[None], r_read=[None], r_used=[None])
        count = dict(kf=0, e=0)

        def context(nb, n_c, f=None):
            c0, n = CHUNKS[n_c]
            f = (n_c + 1) % 2 if f is None else f
            chunk = ctx_buffers[f][:, :, 0:n]
            sp.wait(st["ctx"][f])
            return chunk, sp.dma(cd[f], chunk,
                          w["ctxT"][bass.ds(nb, 1), :, c0:c0 + n].rearrange("a (c p) n -> p (a c) n", p=P))

        ctx_buffers = [ctxb[:, 0, :, :], ctxb[:, 1, :, :], e_t[:, 1, 0:2, :], e_t[:, 1, 2:4, :]]
        buffers = [(kf[:, f, :], kr[:, f, :], ks[:, f, :, :]) for f in range(2)]
        fill = vn[:].rearrange("p k g j d -> p (k g j d)").bitcast(BF16)
        more_buffers = [(e_t[:, 0, 0, :], e_t[:, 0, 1, :], fill[:, 2 * S2:2 * S2 + 3 * 512].rearrange("p (a n) -> p a n", a=3))]

        row = lambda a: a.rearrange("(c p) n -> p c n", p=P)
        ld_k, ld, rows = pg.stream("ld_k"), pg.stream("ld"), pg.stream("rows")
        for t, n in ((wk, "wk"), (wkr, "wkr")) if rope else ((wk, "wk"),):
            sp.dma(ld_k, t[:], row(w[n]))
        for t, n in ((bk, "bk"), (bkr, "bkr")) if rope else ((bk, "bk"),):
            sp.dma(ld_k, t[:], w[n])
        early = [context(0, n, n) for n in range(2)]
        for t, n in ((wq, "wq"), (wqr, "wqr")) if rope else ((wq, "wq"),):
            sp.dma(ld, t[:], row(w[n]))
        for t, n in ((bq, "bq"), (bqr, "bqr")) if rope else ((bq, "bq"),):
            sp.dma(ld, t[:], w[n])
        sp.dma(ld, wv[:], row(w["wv"]))
        sp.dma(ld, woa[:], w["woa"])
        sp.dma(ld, bva[:], w["bva"])
        sp.dma(ld, bob[:], w["bo"].rearrange("(a n) -> a n", a=1).to_broadcast([P, D]))
        loaded = ld.now()
        early += [context(0, n, n) for n in range(2, 4)]

        pool.do(nc.gpsimd.memset(fill[0:R_ALL - R_MASK, 0:S2], 1.0))
        sp.wait(pool.do(nc.gpsimd.memset(fill[0:1, S2:2 * S2], 0.0)))
        v_ones = v[:, :, :, 0:HG * VW].rearrange("p k g (j c) -> p k g j c", c=VW)
        pool.do(nc.gpsimd.memset(v[:, :, :, HG * VW:VG], 0.0))
        for g in range(NG):
            pool.do(nc.gpsimd.memset(v_ones[:, :, g, :, HD:VW], 1.0))
        pool.do(nc.gpsimd.memset(vn[:, KT - 1, :, :, :], 0.0))
        ready = pool.seq(nc.gpsimd.memset(nm[:], 0.0))
        spread = lambda a: a.rearrange("p (a n) -> p a n", a=1).to_broadcast([a.shape[0], H, a.shape[1]])
        for t, n in ((kaug, S2), (qaug, T)):
            sp.dma(rows, t[R_MASK:R_ALL, :, :, :].rearrange("p g j n -> p (g j) n"), spread(fill[0:R_ALL - R_MASK, 0:n]))
        sp.wait(rows.now())
        if mask is None:
            sp.dma(rows, kaug[R_MASK:R_MASK + 1, :, :, :].rearrange("p g j n -> p (g j) n"), spread(fill[0:1, S2:2 * S2]))
        norm = norm([s[:] for s in s_ring.slots], z[:, 0:6 * NT].rearrange("p (n k) -> p n k", k=6),
                    ot[:].rearrange("p g (a d) -> p (g a) d", d=D)[:, 0:4, :])
        next(norm)

        def biases():
            for g in range(NG):
                t = dve.do(nc.vector.tensor_scalar(bvr[:, g, :], cst["ones"][:], bva[:, g:g + 1], None, ALU.mult))
            pe.wait(t)
            i, slot = m_ring.take()
            for g in range(NG):
                m = nc.tensor.matmul(slot[:, 0:D], bvr[:, g, :], woa[:, g, :], start=g == 0, stop=g == NG - 1)
            dve.wait(pe.do(m))
            t = dve.seq(nc.vector.tensor_tensor(bob[:], slot[:, 0:D], bob[:], ALU.add))
            m_ring.free(i, t)
            dve.seq(nc.vector.tensor_scalar(bob[:], bob[:], gate, None, ALU.mult))

        def project(nb, engines, what="kvq", on_their_way=None):
            live = None
            if mask and "q" in what:
                live = live_now[:, 0:1]
                act.wait(*st["live"])
                st["live_now"] = [act.do(nc.scalar.copy(live, mask[1][:, bass.ds(nb, 1)]))]

            def one(wt, wr, rhs, n, c, mul, b0, b1, pos, turn_in, dst, live):
                f = count["kf"] % len(buffers)
                kf, kr, ks = buffers[f]
                e = engines[count["kf"] % len(engines)]
                count["kf"] += 1
                direct = not rope and live is None
                act.wait(st["kf"][f])
                for t, wm, b_ in ((kf, wt, b0), (kr, wr, b1)) if rope else ((kf, wt, b0),):
                    i, slot = s_ring.take()
                    for kc in range(DC):
                        m = nc.tensor.matmul(slot[:, 0:n], wm[:, kc, P * c:P * c + P], rhs(kc),
                                             start=kc == 0, stop=kc == DC - 1)
                    act.wait(pe.do(m))
                    a = act.do(nc.scalar.activation(t[:, 0:n], slot[:, 0:n], ACT.Identity, bias=b_[:, c:c + 1],
                                                    scale=mul))
                    if direct:
                        act.wait(st["put"][f])
                        a = act.do(nc.scalar.activation(ks[:, 0, 0:n], slot[:, 0:n], ACT.Identity,
                                                        bias=b_[:, c:c + 1], scale=mul))
                    s_ring.free(i, a)
                src = kf[:, 0:n]
                e.wait(a)
                if rope:
                    o = kr[:, 0:n]
                    e.wait(turn_in)
                    e.do(e.eng.tensor_tensor(src, src, turn[:, pos, 0, 0:n], ALU.mult))
                    e.seq(e.eng.tensor_tensor(o, o, turn[:, pos, 1, 0:n], ALU.mult))
                    e.seq(e.eng.tensor_tensor(src, src, o, ALU.add))
                if live is not None:
                    e.wait(*st["live_now"])
                    st["live"] = [e.seq(e.eng.tensor_tensor(src, src, live.to_broadcast([P, n]), ALU.mult))]
                e.wait(st["put"][f])
                t = split3(e, cst["ones"][:, 0:1].to_broadcast([P, n]), kr[:, 0:n], src,
                           [ks[:, k, 0:n] for k in range(3)], direct)
                e.wait(t)
                st["kf"][f] = st["turn"][pos] = t
                sp.wait(t)
                st["put"][f] = sp.dma(stored[f], dst[:, P * c:P * c + P, :].rearrange("a p k -> p a k"), ks[:, :, 0:n])

            def turns(f, c0, n):
                if not rope:
                    return None
                sp.wait(st["turn"][f])
                return sp.dma(rd[f], turn[:, f, :, 0:n], rope[:, :, c0:c0 + n])

            in_chunks = what != "q"
            q_turn = 1 if "k" in what else 0
            to_turn = [((n + 1) % 2, *c) for n, c in enumerate(CHUNKS) if "k" in what]
            to_turn += [(q_turn, 0, T)] if "q" in what else []
            turned = []

            def next_turn():
                if to_turn:
                    turned.append(turns(*to_turn.pop(0)))
            next_turn()
            arrived = (on_their_way or [context(nb, n) for n in range(2)]) if in_chunks else []
            sp.wait(*st["arrived"])
            for n_c, (c0, n) in enumerate(CHUNKS if in_chunks else ()):
                f = (n_c + 1) % 2
                if "k" in what:
                    t_in = turned.pop()
                    next_turn()
                chunk, tick = arrived[n_c]
                pe.wait(tick)
                for c in range(DC if "k" in what else 0):
                    one(wk, wkr if rope else None, lambda kc: chunk[:, kc, 0:n], n, c, 1.0, bk,
                        bkr if rope else None, f, t_in, w["kparts"][:, :, c0:c0 + n], None)
                    yield
                for k in range(c0 // P, -(-(c0 + n) // P)) if "v" in what else ():
                    i, slot = s_ring.take()
                    for kc in range(DC):
                        m = nc.tensor.matmul(slot[0:KW[k], 0:D], chunk[:, kc, k * P - c0:k * P - c0 + KW[k]],
                                             wv[:, kc, :], start=kc == 0, stop=kc == DC - 1)
                    act.wait(pe.do(m), st["taken"][0])
                    t = act.do(nc.scalar.copy(vn[0:KW[k], k, :, :, :].rearrange("p g j d -> p (g j d)"),
                                              slot[0:KW[k], 0:D]))
                    s_ring.free(i, t)
                    yield
                st["ctx"][f] = pe.done.now()
                if n_c + 2 < len(CHUNKS) and not on_their_way:
                    arrived.append(context(nb, n_c + 2))
            if "v" in what:
                st["vn"] = [t]
            t_in = turned.pop() if "q" in what else None
            for c in range(DC if "q" in what else 0):
                one(wq, wqr if rope else None, lambda kc: xnT[:, kc, bass.ds(nb * T, T)], T, c, scale, bq,
                    bqr if rope else None, q_turn, t_in, w["qparts"], live)
                yield

        def fetch(g, nb, what="kq", n_g=1, by=None):
            by = by or kd[g]
            sp.wait(*st["put"], st["k_free"][g])
            h0, h1 = HG * HD * g, HG * HD * (g + n_g)
            for s, pq, n in RUNS:
                for k in range(n):
                    r0 = HD * (s + k)
                    for it, to, src, part in (("q", qaug, "qparts", pq), ("k", kaug, "kparts", k)):
                        if it in what:
                            sp.dma(by, to[r0:r0 + HD, g:g + n_g, :, :].rearrange("p g j k -> p (g j) k"),
                                   w[src][part, h0:h1, :].rearrange("(h d) k -> d h k", d=HD))
            if mask and "k" in what:
                for j in range(HG * n_g):
                    sp.dma(by, kaug[R_MASK:R_MASK + 1, g + j // HG, j % HG, :], mask[0][bass.ds(nb, 1), :])
            for n in range(n_g):
                st["arrived"][g + n] = by.now()

        def values_of(g):
            act.wait(*st["vn"], st["v_free"][g])
            st["v"][g] = st["taken"][0] = act.do(nc.scalar.copy(v_ones[:, :, g, :, 0:HD], vn[:, :, g, :, :]))

        def maxima(g, begin=0, end=None):
            u = g % 2
            pe.wait(st["arrived"][g])
            t = None
            for j in range(HG):
                for qc in range(QC):
                    for half in range(2):
                        step = 2 * (j * QC + qc) + half
                        if step < begin:
                            continue
                        if end is not None and step >= end:
                            return
                        i, slot = m_ring.take()
                        for k in range(2):
                            k0 = PIECE * (2 * half + k)
                            m = nc.tensor.matmul(slot[:, 512 * k:512 * k + PIECE + 1],
                                                 qaug[0:R_MAX, g, j, P * qc:P * qc + P],
                                                 kaug[0:R_MAX, g, j, k0:k0 + PIECE + 1], start=True, stop=True)
                        dve.wait(pe.do(m))
                        n = j * QC + qc
                        t = dve.do(nc.vector.tensor_reduce(
                            mxp[:, u, half, n:n + 1], slot[:].rearrange("p (a n) -> p a n", a=2)[:, :, 0:PIECE + 1],
                            AX.XY, ALU.max))
                        m_ring.free(i, t)
                        st["peaks"][u] = t
                        yield
            dve.wait(t, st["peaks"][g % 2], *st["nm"])
            dve.seq(nc.vector.tensor_tensor(mx[:, 0, :], mxp[:, u, 0, :], mxp[:, u, 1, :], ALU.max))
            dve.seq(nc.vector.tensor_scalar(mx[:, 0, :], mx[:, 0, :], -1.0, None, ALU.mult))
            t = split3(dve, cst["ones"][:, 0:HG * QC], mx[:, 1, :], mx[:, 0, :], [nm[:, k, :] for k in range(3)])
            yield
            i, slot = m_ring.take()
            o = slot[:].bitcast(BF16)[:, 0:P]
            pe.wait(t)
            tick = pe.do(nc.tensor.transpose(o, nm[:].rearrange("p a n -> p (a n)"), cst["identb"][:]))
            st["nm"] = [tick]
            dve.wait(tick, st["td"][(g - 1) % NG])
            t = dve.do(nc.vector.tensor_copy(tm[:], o))
            m_ring.free(i, t)
            sp.wait(t)
            for k in range(3):
                sp.dma(td, qaug[R_MAX + k:R_MAX + k + 1, g, :, :].rearrange("a j (c q) -> a (j c) q", q=P),
                       tm[16 * k:16 * k + 16, :])
            st["td"][g] = td.now()
            yield

        MAX_STEPS = 2 * HG * QC + 2

        def normalise(g):
            i, slot = m_ring.take()
            pe.wait(*st["z"])
            for c in range(QC):
                m = nc.tensor.matmul(slot[:, HG * c:HG * c + HG], z[:, P * c:P * c + P], one_sum, start=True, stop=True)
            dve.wait(pe.do(m), *st["r_read"])
            t = dve.do(nc.vector.reciprocal(rc[:], slot[:, 0:HG * QC]))
            m_ring.free(i, t)
            pool.wait(t, *st["r_used"])
            t = pool.do(nc.gpsimd.tensor_tensor(
                r[:].rearrange("p (k n) -> p k n", n=P // HG),
                cst["ones"][:, 0:1].to_broadcast([P, T]).rearrange("p (k n) -> p k n", n=P // HG),
                rc[:].rearrange("p (k a) -> p k a", a=1).to_broadcast([P, HG * QC, P // HG]), ALU.mult))
            st["r_read"] = [t]
            yield
            i, slot = m_ring.take()
            pe.wait(t)
            for c in range(QC):
                part = slice(P * c, P * c + P)
                m = nc.tensor.matmul(slot[:, part], r[:, part], cst["ident"][:], start=True, stop=True)
            st["r_used"] = [pe.do(m)]
            dve.wait(*st["r_used"], *st["ot"])
            st["norm"] = [dve.do(nc.vector.tensor_tensor(ot[:, g, :], z[:], slot[:, 0:T], ALU.mult))]
            m_ring.free(i, st["norm"][0])
            yield

        def output(b):
            for tt in range(TT):
                i, slot = m_ring.take()
                if tt == 0:
                    pe.wait(*st["norm"])
                for g in range(NG):
                    m = nc.tensor.matmul(slot[:, 0:D], ot[:, g, P * tt:P * tt + P], woa[:, g, :],
                                         start=g == 0, stop=g == NG - 1)
                xt = x[:, bass.ds(b * TT + tt, 1), :].rearrange("p a n -> p (a n)")
                dve.wait(pe.do(m))
                t = dve.seq(nc.vector.scalar_tensor_tensor(xt, slot[:, 0:D], gate, xt, ALU.mult, ALU.add))
                m_ring.free(i, t)
                dve.do(nc.vector.tensor_tensor(xt, xt, bob[:], ALU.add))
                yield
            st["ot"] = [pe.done.now()]

        waiting = []

        def attend(g, *work):
            pe.wait(st["td"][g])

            def values(k, jobs):
                e = count["e"] % 2
                count["e"] += 1
                pe.wait(*jobs, *((st["v"][g], *st["z"]) if k == 0 else ()))
                for j in range(HG):
                    m = nc.tensor.matmul(pv[32 * j:32 * j + 32, :], v[0:KW[k], k, g, VW * j:VW * j + 32],
                                         e_t[0:KW[k], e, j, :], start=k == 0, stop=k == KT - 1)
                st["e"][e] = pe.do(m)
                if k == KT - 1:
                    st["v_free"][g] = st["e"][e]
                    act.wait(st["e"][e], *st["norm"])
                    st["z"] = [act.do(nc.scalar.copy(z[:], pv[:]))]
            given = [0] * len(work)
            for k in range(KT):
                jobs = []
                for j in range(HG):
                    i, slot = s_ring.take()
                    mm = pe.do(nc.tensor.matmul(slot[0:KW[k], :], kaug[0:R_ALL, g, j, P * k:P * k + KW[k]],
                                                qaug[0:R_ALL, g, j, :], start=True, stop=True))
                    e = (count["e"] + len(waiting)) % 2
                    act.wait(mm, st["e"][e] if j == 0 else None)
                    t = act.do(nc.scalar.activation(e_t[0:KW[k], e, j, :], slot[0:KW[k], :], ACT.Exp))
                    s_ring.free(i, t)
                    jobs.append(t)
                    n = HG * k + j
                    for a, (gen, steps, first, last) in enumerate(work):
                        while n >= first and given[a] * (last - first + 1) < steps * (n - first + 1):
                            given[a] += 1
                            next(gen, None)
                if waiting:
                    waiting.pop()()
                waiting.append(lambda k=k, jobs=jobs: values(k, jobs))
            st["k_free"][g] = pe.done.now()

        def finish():
            if waiting:
                waiting.pop()()

        def then(f, *a):
            f(*a)
            yield

        def chain(*gens):
            for gen in gens:
                yield from gen

        JOBS = HG * KT
        LEAD = 8 if mask else 12

        pe.wait(*s_ring.freed)
        drain(norm)
        dve.wait(loaded, ready)
        for b_ in (bq, bqr) if rope else (bq,):
            t = dve.do(nc.vector.tensor_scalar(b_[:], b_[:], scale, None, ALU.mult))
        for e in (pe, act):
            e.wait(ld_k.now(), loaded, ready, t)
        buffers += more_buffers
        drain(project(0, (dve,), "q"))
        projected = project(0, (pool, dve, dve), "k", early)
        for _ in range(4):
            next(projected)
        fetch(0, 0, "q", NG, kd[3])
        drain(projected)
        fetch(0, 0, "k")
        pe.wait(rows.now(), kd[3].now())
        del buffers[2:]
        projected = project(0, (), "v", early)
        for n, _ in enumerate(maxima(0)):
            if n % 2:
                next(projected, None)
            if n == 3:
                sp.wait(pe.done.now())
                fetch(1, 0, "k")
                fetch(2, 0, "k", 2)
        drain(projected)
        biases()
        for g in range(NG):
            values_of(g)
        drain(maxima(1, 0, LEAD))
        attend(0, (chain(maxima(1, LEAD), maxima(2, 0, LEAD)), MAX_STEPS, 0, JOBS - 1))
        finish()

        def all_ticks():
            for name, ticks in st.items():
                for i, t in enumerate(ticks):
                    yield f"{name}{i}", (lambda t, name=name, i=i: st[name].__setitem__(i, t)), t

        uid = pg.n_names
        for e in pg.engines:
            e.wait(*[t for _, _, t in all_ticks() if t is not None])
        with pg.loop(B - 1) as b:
            count["kf"] = count["e"] = 0
            for n, put, _ in list(all_ticks()):
                put(pg.last_round(f"{n}@{uid}"))
            peaks = (chain(maxima(2, LEAD), maxima(3), maxima(0), maxima(1), maxima(2, 0, LEAD)), MAX_STEPS, 0, JOBS - 1)
            projected = chain(project(b + 1, (pool,)), *(then(fetch, g, b + 1) for g in (0, 1)))
            attend(1, peaks, (projected, 16, 6, JOBS - 1), (normalise(0), 2, 2 * HG, JOBS - 1))
            attend(2, peaks, (projected, 10, 0, 20), (normalise(1), 2, 2 * HG, JOBS - 1))
            attend(3, peaks, (chain(then(fetch, 2, b + 1), *(then(values_of, g) for g in range(3))), 4, 8, 24),
                   (normalise(2), 2, 2 * HG, JOBS - 1))
            attend(0, peaks, (chain(then(fetch, 3, b + 1), then(values_of, 3)), 2, 8, 24),
                   (chain(normalise(3), output(b)), 2 + TT + 1, 2 * HG, JOBS - 1))
            finish()
            for n, _, t in all_ticks():
                if t is not None and not isinstance(t, LastRound):
                    pg.keep(f"{n}@{uid}", t)
        peaks = (chain(maxima(2, LEAD), maxima(3)), MAX_STEPS, 0, JOBS - 1)
        for g in range(1, NG):
            attend(g, peaks, (normalise(g - 1), 2, 2 * HG, JOBS - 1))
        finish()
        drain(normalise(NG - 1), output(B - 1))
        for ring in (s_ring, m_ring):
            pg.rings.remove(ring)


def wide_attention(pg, x, xnT, cst, w, gate, norm):
    nc, pe, act, dve, pool, sp = pg.nc, pg.pe, pg.act, pg.dve, pg.pool, pg.sp
    pg.barrier()
    scale = 1.0 / D ** 0.5
    with ExitStack() as ctx:
        sb = lambda name, shape, dt=F32: pg.sbuf(ctx, name, shape, dt)
        wq, wk, wv, wo = (sb(n, [P, DC, D]) for n in ("wq", "wk", "wv", "wo"))
        bq, bk = sb("bq", [P, DC]), sb("bk", [P, DC])
        bvb, bob = sb("bvb", [P, D]), sb("bob", [P, D])
        ctxb = sb("ctxb", [P, 2, DC, 512])
        kT = sb("kT", [P, DC, S2])
        v = sb("v", [P, KT, D])
        qT = sb("qT", [P, DC, T])
        e_t = sb("e_t", [P, 2, S2])
        eT = sb("eT", [P, 2, KT, P])
        stat = sb("stat", [P, 2, 4])
        o, oT = sb("o", [P, 2, D]), sb("oT", [P, 2, DC, P])
        s_ps = pg.psum(ctx, "s", [P, 4 * 512])
        t_ring = Ring(pg, f"t{pg.n_names}", [pg.psum(ctx, f"t{i}", [P, 512]) for i in range(3)])
        y_ring = Ring(pg, f"y{pg.n_names}", [pg.psum(ctx, f"y{i}", [P, 512]) for i in range(1)])
        ld = pg.stream("ld")
        with nc.allow_non_contiguous_dma("biases: small"):
            for t, n in ((wq, "wq"), (wk, "wk"), (wv, "wv"), (wo, "wo")):
                sp.dma(ld, t[:], w[n].rearrange("(c p) n -> p c n", p=P))
            for t, n in ((bq, "bq"), (bk, "bk")):
                sp.dma(ld, t[:], w[n])
            for t, n in ((bvb, "bv"), (bob, "bo")):
                sp.dma(ld, t[:], w[n].rearrange("(a n) -> a n", a=1).to_broadcast([P, D]))
        drain(norm([s[:] for s in t_ring.slots], e_t[:, 0, 0:6 * NT].rearrange("p (n k) -> p n k", k=6),
                   eT[:, 0, 0:8, :].rearrange("p k n -> p (k n)").rearrange("p (g d) -> p g d", d=D)))
        for e in (pe, act, dve):
            e.wait(ld.now())
        dve.do(nc.vector.tensor_scalar(bob[:], bob[:], gate, None, ALU.mult))
        act.wait(dve.seq(nc.vector.tensor_scalar(bq[:], bq[:], scale, None, ALU.mult)))
        cd = [pg.stream("c0"), pg.stream("c1")]
        st = dict(ctx=[None] * 2, e=[None] * 2, eT=[None] * 2, oT=[None] * 2, o=[None] * 2, s=[None])

        def project(b):
            def one(dst, wt, c, bias, mul, n, rhs):
                k, slot = t_ring.take()
                for kc in range(DC):
                    m = nc.tensor.matmul(slot[:, 0:n], wt[:, kc, P * c:P * c + P], rhs(kc),
                                         start=kc == 0, stop=kc == DC - 1)
                act.wait(pe.do(m))
                t_ring.free(k, act.do(nc.scalar.activation(dst, slot[:, 0:n], ACT.Identity, bias=bias[:, c:c + 1],
                                                           scale=mul)))
            for c in range(DC):
                one(qT[:, c, :], wq, c, bq, scale, T, lambda kc: xnT[:, kc, bass.ds(b * T, T)])
            for n_c, (c0, n) in enumerate(CHUNKS):
                f = n_c % 2
                pool.wait(st["ctx"][f])
                pe.wait(cd[f].after(nc.gpsimd.dma_start(
                    ctxb[:, f, :, 0:n], w["ctxT"][bass.ds(b, 1), :, c0:c0 + n].rearrange("a (c p) n -> p (a c) n", p=P))))
                for c in range(DC):
                    one(kT[:, c, c0:c0 + n], wk, c, bk, 1.0, n, lambda kc: ctxb[:, f, kc, 0:n])
                for k_ in range(c0 // P, -(-(c0 + n) // P)):
                    k, slot = t_ring.take()
                    for kc in range(DC):
                        m = nc.tensor.matmul(slot[0:KW[k_], 0:D], ctxb[:, f, kc, P * k_ - c0:P * k_ - c0 + KW[k_]],
                                             wv[:, kc, :], start=kc == 0, stop=kc == DC - 1)
                    act.wait(pe.do(m))
                    t_ring.free(k, act.do(nc.scalar.copy(v[0:KW[k_], k_, :], slot[0:KW[k_], 0:D])))
                st["ctx"][f] = pe.done.now()
            return act.done.now()

        def scores(qc):
            u = qc % 2
            pe.wait(*st["s"])
            for c0, n in CHUNKS:
                for c in range(DC):
                    m = nc.tensor.matmul(s_ps[:, c0:c0 + n], qT[:, c, P * qc:P * qc + P], kT[:, c, c0:c0 + n],
                                         start=c == 0, stop=c == DC - 1)
            mm = pe.do(m)
            dve.wait(mm, st["e"][u], st["o"][u])
            dve.seq(nc.vector.tensor_reduce(stat[:, u, 0:1], s_ps[:, 0:S2], AX.X, ALU.max))
            return dve.do(nc.vector.tensor_scalar(stat[:, u, 1:2], stat[:, u, 0:1], -1.0, None, ALU.mult))

        def exp_of(qc, after):
            u = qc % 2
            act.wait(after, st["e"][u])
            t = act.do(nc.scalar.activation(e_t[:, u, :], s_ps[:, 0:S2], ACT.Exp, bias=stat[:, u, 1:2],
                                            accum_out=stat[:, u, 2:3]))
            st["s"] = [t]
            return t

        def values(qc, exped, between):
            u = qc % 2
            dve.wait(exped)
            dve.do(nc.vector.reciprocal(stat[:, u, 3:4], stat[:, u, 2:3]))
            pe.wait(exped)
            act.wait(st["eT"][u])
            ky, y_slot = y_ring.take()

            def product(tick, tiles):
                pe.wait(tick)
                for n in tiles:
                    m = nc.tensor.matmul(y_slot[:, 0:D], eT[0:KW[n], u, n, :], v[0:KW[n], n, :],
                                         start=n == 0, stop=n == KT - 1)
                return m
            before = None
            for k0 in range(0, KT, 4):
                k, slot = t_ring.take()
                tiles = range(k0, min(KT, k0 + 4))
                for n in tiles:
                    m = nc.tensor.transpose(slot[0:KW[n], P * (n - k0):P * (n - k0) + P],
                                            e_t[:, u, P * n:P * n + KW[n]], cst["ident"][:])
                act.wait(pe.do(m))
                h = KW[tiles[-1]]
                t = act.do(nc.scalar.copy(eT[0:h, u, k0:k0 + len(tiles), :],
                                          slot[0:h, 0:P * len(tiles)].rearrange("p (k n) -> p k n", n=P)))
                t_ring.free(k, t)
                if k0 == 4:
                    between()
                if before:
                    product(*before)
                before = (t, tiles)
            st["e"][u] = pe.done.now()
            st["eT"][u] = pe.do(product(*before))
            dve.wait(st["eT"][u], st["o"][u], dve.done.now())
            t = dve.do(nc.vector.scalar_tensor_tensor(o[:, u, :], y_slot[:, 0:D], stat[:, u, 3:4], bvb[:], ALU.mult, ALU.add))
            y_ring.free(ky, t)
            return t

        def output(b, qc, after):
            u = qc % 2
            act.wait(st["oT"][u])
            t = transposed(pg, t_ring, oT[:, u, :, :], o[:, u, :], cst, after)
            st["o"][u] = pe.done.now()
            pe.wait(t)
            k, slot = y_ring.take()
            for c in range(DC):
                m = nc.tensor.matmul(slot[:, 0:D], oT[:, u, c, :], wo[:, c, :], start=c == 0, stop=c == DC - 1)
            st["oT"][u] = pe.do(m)
            xt = x[:, bass.ds(b * TT + qc, 1), :].rearrange("p a n -> p (a n)")
            dve.wait(st["oT"][u])
            t = dve.seq(nc.vector.scalar_tensor_tensor(xt, slot[:, 0:D], gate, xt, ALU.mult, ALU.add))
            y_ring.free(k, t)
            dve.do(nc.vector.tensor_tensor(xt, xt, bob[:], ALU.add))

        names = ("ctx", "e", "eT", "oT", "o", "s")
        with pg.loop(B) as b:
            for name in names:
                for p in range(len(st[name])):
                    st[name][p] = pg.last_round(f"{name}{p}@wide")
            pe.wait(project(b))
            exped, got = exp_of(0, scores(0)), None
            for qc in range(QC):
                after = scores(qc + 1) if qc + 1 < QC else None
                if got:
                    output(b, qc - 1, got)
                coming = []
                got = values(qc, exped, lambda: coming.append(exp_of(qc + 1, after) if after else None))
                exped = coming[0]
            output(b, QC - 1, got)
            for name in names:
                for p, t in enumerate(st[name]):
                    pg.keep(f"{name}{p}@wide", t)
        for r in (t_ring, y_ring):
            pg.rings.remove(r)


LAMBDA, ALPHA = 1.0507009873554804934193349852946, 1.6732632423543772848170429916717


def transposed(pg, ring, out, src, cst, after, nr=2):
    nc, pe, act = pg.nc, pg.pe, pg.act
    pe.wait(after)
    k, slot = ring.take()
    for c in range(nr):
        m = nc.tensor.transpose(slot[:, P * c:P * c + P], src[:, P * c:P * c + P], cst["ident"][:])
    act.wait(pe.do(m))
    t = act.do(nc.scalar.copy(out, slot[:, 0:P * nr].rearrange("p (c n) -> p c n", c=nr)))
    ring.free(k, t)
    return t


def quantised_linear(pg, x, xnT, cst, weight, hadamard, gate, norm, clear):
    nc, pe, act, dve, pool, sp = pg.nc, pg.pe, pg.act, pg.dve, pg.pool, pg.sp
    pg.barrier()
    POS, NEG, ROUND = 7.0, 8.0, 1.5 * 2.0 ** 23
    G = 4
    with ExitStack() as ctx:
        sb = lambda name, shape, dt=F32: pg.sbuf(ctx, name, shape, dt)
        wt, hd = sb("wt", [P, DC, D]), sb("hd", [P, DC, D])
        wsc, wn, wa, wb = sb("wsc", [P, 3, DC]), sb("wn", [P, DC, D]), sb("wa", [P, DC, D]), sb("wb", [P, DC, D])
        wqT = sb("wqT", [P, DC, D])
        xc = sb("xc", [P, 2, DC, G * P])
        xh, t1, xq = (sb(n, [P, 2, G, D]) for n in ("xh", "t1", "xq"))
        xqT = sb("xqT", [P, 2, G, DC, P])
        sc = sb("sc", [P, 2, 4, G])
        h_ring = Ring(pg, f"h{pg.n_names}", [pg.psum(ctx, f"h{i}", [P, G * D]) for i in range(2)])
        t_ring = Ring(pg, f"t{pg.n_names}", [pg.psum(ctx, f"t{i}", [P, 2 * D]) for i in range(2)])
        y_ring = Ring(pg, f"y{pg.n_names}", [pg.psum(ctx, f"y{i}", [P, 2 * D]) for i in range(2)])
        ld = pg.stream("ld")
        sp.dma(ld, wt[:], weight.rearrange("(c p) n -> p c n", p=P))
        sp.dma(ld, hd[:], hadamard.rearrange("(c p) n -> p c n", p=P))
        clear()
        norm = norm([s[:] for r in (t_ring, y_ring) for s in r.slots],
                    sb("stats", [P, NT, 6]), xq[:, 0, :, :])
        drain(norm)
        dve.wait(ld.now())
        pe.wait(ld.now())
        flat = lambda a: a.rearrange("p g n -> p (g n)")
        each = lambda s, k: s.rearrange("p (n a) -> p n a", a=1).to_broadcast([P, k, D])
        dve.seq(nc.vector.tensor_scalar(wn[:], wt[:], -1.0, None, ALU.mult))
        dve.seq(nc.vector.tensor_tensor(wa[:], wn[:], wt[:], ALU.max))
        dve.seq(nc.vector.tensor_reduce(wsc[:, 0, :], wa[:], AX.X, ALU.add))
        dve.seq(nc.vector.tensor_scalar(wsc[:, 1, :], wsc[:, 0, :], 1.0 / D, 1e-5, ALU.mult, ALU.max))
        dve.seq(nc.vector.reciprocal(wsc[:, 2, :], wsc[:, 1, :]))
        dve.seq(nc.vector.tensor_tensor(wn[:], wt[:], each(wsc[:, 2, :], DC), ALU.mult))
        dve.do(nc.vector.tensor_scalar(wa[:], wn[:], 0.5, None, ALU.is_gt))
        dve.seq(nc.vector.tensor_scalar(wb[:], wn[:], -0.5, None, ALU.is_lt))
        dve.seq(nc.vector.tensor_tensor(wa[:], wa[:], wb[:], ALU.subtract))
        dve.seq(nc.vector.tensor_tensor(wa[:], wa[:], each(wsc[:, 1, :], DC), ALU.mult))
        dve.seq(nc.vector.tensor_tensor(wb[:], wa[:], wt[:], ALU.subtract))
        t = dve.seq(nc.vector.tensor_tensor(wn[:], wb[:], wt[:], ALU.add))
        for c in range(DC):
            turned = transposed(pg, t_ring, wqT[:, :, P * c:P * c + P], wn[:, c, :], cst, t)
        pe.wait(turned)
        uid = pg.n_names

        def rotated(i, u):
            act.wait(st["xc"][u])
            pe.wait(act.do(nc.scalar.copy(xc[:, u, :, :], xnT[:, :, bass.ds(i * (G * P), G * P)])))
            k, slot = h_ring.take()
            for g in range(G):
                for c in range(DC):
                    m = nc.tensor.matmul(slot[:, D * g:D * g + D], xc[:, u, c, P * g:P * g + P], hd[:, c, :],
                                         start=c == 0, stop=c == DC - 1)
            st["xc"][u] = pe.do(m)
            act.wait(st["xc"][u], st["xh"][u])
            t = act.do(nc.scalar.copy(flat(xh[:, u, :, :]), slot[:]))
            h_ring.free(k, t)
            return t

        def quantised(u, after):
            s, h, q = sc[:, u, :, :], xh[:, u, :, :], t1[:, u, :, :]
            dve.wait(after, st["xh"][u])
            dve.do(nc.vector.tensor_reduce(s[:, 0, :], h, AX.X, ALU.max))
            dve.seq(nc.vector.tensor_reduce(s[:, 1, :], h, AX.X, ALU.min))
            dve.seq(nc.vector.scalar_tensor_tensor(s[:, 2, :], s[:, 1, :], -1.0, s[:, 0, :], ALU.mult, ALU.max))
            dve.seq(nc.vector.tensor_scalar(s[:, 2, :], s[:, 2, :], 1e-5, 1.0 / POS, ALU.max, ALU.mult))
            dve.seq(nc.vector.reciprocal(s[:, 3, :], s[:, 2, :]))
            dve.seq(nc.vector.tensor_tensor(q, h, each(s[:, 3, :], G), ALU.mult))
            dve.seq(nc.vector.tensor_scalar(q, q, ROUND, None, ALU.add))
            dve.seq(nc.vector.tensor_scalar(q, q, ROUND, POS, ALU.subtract, ALU.min))
            dve.seq(nc.vector.tensor_scalar(q, q, -NEG, None, ALU.max))
            t = dve.seq(nc.vector.tensor_tensor(q, q, each(s[:, 2, :], G), ALU.mult))
            pool.wait(t, st["xq"][u])
            pool.seq(nc.gpsimd.tensor_tensor(q, q, h, ALU.subtract))
            t = pool.do(nc.gpsimd.tensor_tensor(xq[:, u, :, :], q, h, ALU.add))
            st["xh"][u] = t
            return t

        def product(i, u, after):
            pe.wait(after)
            act.wait(st["xqT"][u])
            ready = []
            for h in range(G // 2):
                k, slot = t_ring.take()
                for g in range(2 * DC):
                    m = nc.tensor.transpose(slot[:, P * g:P * g + P],
                                            xq[:, u, 2 * h + g // DC, P * (g % DC):P * (g % DC) + P], cst["ident"][:])
                act.wait(pe.do(m))
                t = act.do(nc.scalar.copy(xqT[:, u, 2 * h:2 * h + 2, :, :].rearrange("p g c n -> p (g c n)"), slot[:]))
                t_ring.free(k, t)
                ready.append(t)
            st["xq"][u] = pe.done.now()
            for h in range(G // 2):
                pe.wait(ready[h])
                k, slot = y_ring.take()
                for g in range(2):
                    for c in range(DC):
                        m = nc.tensor.matmul(slot[:, D * g:D * g + D], xqT[:, u, 2 * h + g, c, :], wqT[:, c, :],
                                             start=c == 0, stop=c == DC - 1)
                t = pe.do(m)
                xt = x[:, bass.ds(i * G + 2 * h, 2), :]
                dve.wait(t)
                t = dve.do(nc.vector.scalar_tensor_tensor(xt, slot[:].rearrange("p (g n) -> p g n", n=D), gate, xt,
                                                          ALU.mult, ALU.add))
                y_ring.free(k, t)
            st["xqT"][u] = pe.done.now()

        st = {n: [None, None] for n in ("xc", "xh", "xq", "xqT")}
        after = rotated(0, 0)
        got = quantised(0, after)
        for i in range(NT // G):
            u = i % 2
            if i + 1 < NT // G:
                ahead = quantised(1 - u, rotated(i + 1, 1 - u))
            product(i, u, got)
            got = ahead
        for r in (h_ring, t_ring, y_ring):
            pg.rings.remove(r)


def experts(pg, x, xnT, cst, w, gate, kind, dram, norm):
    nc, pe, act, dve, pool, sp = pg.nc, pg.pe, pg.act, pg.dve, pg.pool, pg.sp
    pg.barrier()
    K = 2 if kind == "selu" else 1
    CAP = N // NE
    M = N // P if kind == "gelu" else K * N // P + NE - 1
    NX = NE + (kind == "selu")
    xs, ys = dram["xs"], dram["ys"]
    with ExitStack() as ctx:
        sb = lambda name, shape, dt=F32: pg.sbuf(ctx, name, shape, dt)
        w1, w2 = sb("w1", [P, 2, DC, FF]), sb("w2", [P, NX, FC, D])
        b1, b2 = sb("b1", [P, NX, FC]), sb("b2", [P, NX, D])
        oh = sb("oh", [P, K * NT, NE])
        wk = sb("wk", [P, K * NT])
        slot_u = sb("slot_u", [P, K * NT], U32)
        to_u = sb("to_u", [P, K * NT], U32)
        slot_f = sb("slot_f", [P, K * NT])
        valid = sb("valid", [P, K * NT])
        tile_e = sb("tile_e", [1, 64], I32)
        xt = sb("xt", [P, 2, D])
        xtT = sb("xtT", [P, 2, DC, P])
        hT = sb("hT", [P, 2, FC, P])
        y = sb("y", [P, 2, D])
        bank = [pg.psum(ctx, f"b{i}", [P, 512]) for i in range(2)]
        h_ring = Ring(pg, f"h{pg.n_names}", [pg.psum(ctx, f"h{i}", [P, FC * P]) for i in range(2)])
        y_ring = Ring(pg, f"y{pg.n_names}", [pg.psum(ctx, f"y{i}", [P, 512]) for i in range(2)])
        t_ring = Ring(pg, f"t{pg.n_names}", bank)

        ld = [pg.stream(f"ldw{e}") for e in range(NX)]
        order = ([NE] if kind == "selu" else []) + list(range(NE))
        small = pg.stream("lds")
        with nc.allow_non_contiguous_dma("biases: small"):
            sp.dma(small, b1[:, 0:NE, :], w["b1"])
            if kind == "selu":
                sp.dma(small, b1[:, NE, :], w["gb1"])
            else:
                gw = sb("gw", [P, DC, NE])
                sp.dma(small, gw[:], w["gate"])
        sp.dma(small, b2[:, 0:NE, :].rearrange("p e n -> p (e n)"),
               w["b2"].rearrange("e n -> (e n)").rearrange("(a m) -> a m", a=1).to_broadcast([P, NE * D]))
        if kind == "selu":
            sp.dma(small, b2[:, NE, :], w["gb2"].rearrange("(a n) -> a n", a=1).to_broadcast([P, D]))
        for e in order:
            s2 = w["w2"][e] if e < NE else w["gw2"]
            if e == NE:
                sp.dma(ld[e], w1[:, 0, :, :], w["gw1"].rearrange("(c p) f -> p c f", p=P))
            sp.dma(ld[e], w2[:, e, :, :], s2.rearrange("(f p) n -> p f n", p=P))
        drain(norm([s[:] for r in (t_ring, y_ring) for s in r.slots], y[:, 0, 0:6 * NT].rearrange("p (n k) -> p n k", k=6),
                   hT[:, 0, :, :].rearrange("p f n -> p (f n)").rearrange("p (g d) -> p g d", d=D)))
        pe.wait(small.now())
        act.wait(small.now())
        dve.wait(small.now())
        scale = LAMBDA if kind == "selu" else 1.0
        used = dict(w1=[None, None], hT=[None, None], x=[None, None], xT=[None, None], y=[None, None])
        if kind == "selu":
            z, ez = ([sb(f"{n}{p}", [P, FC * P]) for p in range(2)] for n in ("z", "ez"))

        def hidden(xT, w1_at, e, p):
            k, slot = h_ring.take()
            for f in range(FC):
                for c in range(DC):
                    m = nc.tensor.matmul(slot[:, P * f:P * f + P], w1[:, w1_at, c, P * f:P * f + P], xT(c),
                                         start=c == 0, stop=c == DC - 1)
            mm = pe.do(m)
            act.wait(mm, used["hT"][p])
            bias = lambda f: (b1[:, e, f:f + 1] if isinstance(e, int) else
                              b1[:, bass.ds(e, 1), f:f + 1].rearrange("p a n -> p (a n)"))
            if kind != "selu":
                func = ACT.Relu if kind == "relu" else ACT.Gelu_apprx_tanh
                for f in range(FC):
                    t = act.do(nc.scalar.activation(hT[:, p, f, :], slot[:, P * f:P * f + P], func, bias=bias(f)))
                h_ring.free(k, t)
                return t
            for to, func in ((ez[p], ACT.Exp), (z[p], ACT.Relu)):
                for f in range(FC):
                    t = act.do(nc.scalar.activation(to[:, P * f:P * f + P], slot[:, P * f:P * f + P], func, bias=bias(f)))
            h_ring.free(k, t)
            dve.wait(t)
            dve.seq(nc.vector.tensor_scalar(ez[p][:], ez[p][:], ALPHA, ALPHA, ALU.mult, ALU.subtract))
            return dve.seq(nc.vector.scalar_tensor_tensor(hT[:, p, :, :].rearrange("p f n -> p (f n)"), ez[p][:], 0.0,
                                                          z[p][:], ALU.min, ALU.add))

        def projected(e, p, after, to, free):
            pe.wait(after)
            k, slot = y_ring.take()
            for f in range(FC):
                m = nc.tensor.matmul(slot[:, 0:D], hT[:, p, f, :],
                                     w2[:, e[0], f, :] if isinstance(e[0], int) else
                                     w2[:, bass.ds(e[0], 1), f, :].rearrange("p a n -> p (a n)"),
                                     start=f == 0, stop=f == FC - 1)
            used["hT"][p] = pe.do(m)
            dve.wait(used["hT"][p], free)
            t = dve.do(nc.vector.scalar_tensor_tensor(
                to, slot[:, 0:D], scale, b2[:, e[1], :] if isinstance(e[1], int) else
                b2[:, bass.ds(e[1], 1), :].rearrange("p a n -> p (a n)"), ALU.mult, ALU.add))
            y_ring.free(k, t)
            return t

        xn = sb("xn", [P, NT, D])
        for n in range(NT):
            xn_made = dve.do(nc.vector.tensor_scalar(xn[:, n, :], x[:, n, :], cst["mv"][:, n, 0:1],
                                                     cst["rstd"][:, n:n + 1], ALU.subtract, ALU.mult))

        if kind == "selu":
            top = sb("top", [P, NT, 8])
            top_i = sb("top_i", [P, NT, 8], U32)
            topf = sb("topf", [P, 2, NT])
            sums = sb("sums", [P, NT])
            pe.wait(ld[NE].now())
            best, best_i = sb("best", [P, 2, 8]), sb("best_i", [P, 2, 8], U32)

            def gate_up(n, p):
                return hidden(lambda c: xnT[:, c, bass.ds(n * P, P)], 0, NE, p)

            idle = sb("idle", [P, 2])
            dve.seq(nc.vector.memset(idle[:], 0.0))

            def take_wait():
                dve.do(nc.vector.tensor_copy(idle[:, 0:1], idle[:, 1:2]))

            def gate_down(n, p, after):
                dve.wait(projected((NE, NE), p, after, y[:, p, :], None))
                take_wait()
                dve.seq(nc.vector.max(best[:, p, :], y[:, p, :]))
                take_wait()
                dve.seq(nc.vector.max_index(best_i[:, p, :], best[:, p, :], y[:, p, :]))
                at = lambda t: t[:, bass.ds(n, 1), :].rearrange("p a k -> p (a k)")
                dve.do(nc.vector.tensor_copy(at(top), best[:, p, :]))
                dve.seq(nc.vector.tensor_copy(at(top_i), best_i[:, p, :]))

            h = gate_up(0, 0)
            pe.wait(h)
            uid = pg.n_names
            with pg.loop(NT // 2 - 1) as i:
                for p in range(2):
                    used["hT"][p] = pg.last_round(f"gate_hT{p}@{uid}")
                h0 = pg.last_round(f"gate_h0@{uid}")
                h1 = gate_up(i * 2 + 1, 1)
                gate_down(i * 2, 0, h0)
                h0 = gate_up(i * 2 + 2, 0)
                gate_down(i * 2 + 1, 1, h1)
                pg.keep(f"gate_h0@{uid}", h0)
                for p in range(2):
                    pg.keep(f"gate_hT{p}@{uid}", used["hT"][p])
            h1 = gate_up(NT - 1, 1)
            gate_down(NT - 2, 0, h0)
            gate_down(NT - 1, 1, h1)
            dve.seq(nc.vector.tensor_copy(topf[:].rearrange("p k n -> p n k"), top_i[:, :, 0:2]))
            dve.seq(nc.vector.tensor_tensor(sums[:], top[:, :, 0], top[:, :, 1], ALU.add))
            dve.seq(nc.vector.reciprocal(sums[:], sums[:]))
            for k in range(K):
                dve.seq(nc.vector.tensor_tensor(wk[:, NT * k:NT * k + NT], top[:, :, k], sums[:], ALU.mult))
            chosen = topf[:].rearrange("p k n -> p (k n)")
        else:
            pr, red = sb("pr", [P, NT, NE]), sb("red", [P, 3, NT])
            k, slot = t_ring.take()
            lg = slot[:, 0:NT * NE].rearrange("p (n e) -> p n e", e=NE)
            for n in range(NT):
                for c in range(DC):
                    m = nc.tensor.matmul(lg[:, n, :], xnT[:, c, P * n:P * n + P], gw[:, c, :],
                                         start=c == 0, stop=c == DC - 1)
            dve.wait(pe.do(m))
            dve.seq(nc.vector.tensor_reduce(red[:, 0, :], lg, AX.X, ALU.max))
            over = lambda r: r.rearrange("p (n a) -> p n a", a=1).to_broadcast([P, NT, NE])
            t = dve.seq(nc.vector.tensor_tensor(pr[:], lg, over(red[:, 0, :]), ALU.subtract))
            t_ring.free(k, t)
            act.wait(t)
            t = act.do(nc.scalar.activation(pr[:], pr[:], ACT.Exp))
            dve.wait(t)
            dve.seq(nc.vector.tensor_reduce(red[:, 1, :], pr[:], AX.X, ALU.add))
            dve.seq(nc.vector.reciprocal(red[:, 1, :], red[:, 1, :]))
            dve.seq(nc.vector.tensor_tensor(pr[:], pr[:], over(red[:, 1, :]), ALU.mult))
            dve.seq(nc.vector.tensor_reduce(wk[:], pr[:], AX.X, ALU.max))
            dve.seq(nc.vector.tensor_tensor(pr[:], pr[:], over(wk[:]), ALU.is_lt))
            dve.seq(nc.vector.scalar_tensor_tensor(pr[:].rearrange("p n e -> p (n e)"), pr[:].rearrange("p n e -> p (n e)"), float(NE),
                                                   cst["iota_e"][:, 0:NT * NE], ALU.mult, ALU.add))
            dve.seq(nc.vector.tensor_reduce(red[:, 2, :], pr[:], AX.X, ALU.min))
            chosen = red[:, 2, :]
        iota = cst["iota_e"][:, 0:K * NT * NE].rearrange("p (n e) -> p n e", e=NE)
        overk = lambda r: r.rearrange("p (n a) -> p n a", a=1).to_broadcast([P, K * NT, NE])
        dve.seq(nc.vector.tensor_tensor(oh[:], iota, overk(chosen), ALU.is_equal))

        rank, tot = sb("rank", [P, K * NT, NE]), sb("tot", [P, 2, K * NT, NE])
        flat = oh[:].rearrange("p n e -> p (n e)")
        pe.wait(dve.done.now())
        k, slot = t_ring.take()
        k2, slot2 = t_ring.take()
        n_all = K * NT * NE
        nc.tensor.matmul(slot[:, 0:n_all], cst["tri"][:], flat, start=True, stop=True)
        dve.wait(pe.do(nc.tensor.matmul(slot2[:, 0:n_all], cst["ones"][:], flat, start=True, stop=True)))
        dve.do(nc.vector.tensor_copy(tot[:, 0, :, :].rearrange("p n e -> p (n e)"), slot2[:, 0:n_all]))
        t = dve.seq(nc.vector.tensor_copy(rank[:].rearrange("p n e -> p (n e)"), slot[:, 0:n_all]))
        t_ring.free(k, t)
        t_ring.free(k2, t)
        a, step = 0, 1
        while step < K * NT:
            dve.do(nc.vector.tensor_copy(tot[:, 1 - a, 0:step, :], tot[:, a, 0:step, :]))
            dve.seq(nc.vector.tensor_tensor(tot[:, 1 - a, step:, :], tot[:, a, step:, :], tot[:, a, 0:K * NT - step, :], ALU.add))
            a, step = 1 - a, 2 * step
        dve.seq(nc.vector.tensor_tensor(rank[:, 1:, :], rank[:, 1:, :], tot[:, a, 0:K * NT - 1, :], ALU.add))
        base = sb("base", [P, 2, NE])
        ends = sb("ends", [P, NE])
        if kind == "gelu":
            dve.do(nc.vector.tensor_scalar(base[:, 0, :], cst["iota_e"][:, 0:NE], float(CAP), None, ALU.mult))
            dve.seq(nc.vector.tensor_scalar(ends[:], cst["iota_e"][:, 0:NE], float(CAP), float(CAP), ALU.mult, ALU.add))
        else:
            cnt = sb("cnt", [P, NE], I32)
            dve.seq(nc.vector.tensor_scalar(ends[:], tot[:, a, K * NT - 1, :], float(P - 1), None, ALU.add))
            dve.seq(nc.vector.tensor_copy(cnt[:], ends[:]))
            dve.seq(nc.vector.tensor_scalar(cnt[:], cnt[:], 7, 7, ALU.arith_shift_right, ALU.arith_shift_left))
            dve.seq(nc.vector.tensor_copy(ends[:], cnt[:]))
            dve.seq(nc.vector.tensor_copy(base[:, 0, :], ends[:]))
            c0, step = 0, 1
            while step < NE:
                dve.do(nc.vector.tensor_copy(base[:, 1 - c0, 0:step], base[:, c0, 0:step]))
                dve.seq(nc.vector.tensor_tensor(base[:, 1 - c0, step:], base[:, c0, step:], base[:, c0, 0:NE - step], ALU.add))
                c0, step = 1 - c0, 2 * step
            dve.seq(nc.vector.tensor_tensor(base[:, 1 - c0, :], base[:, c0, :], ends[:], ALU.subtract))
            dve.seq(nc.vector.tensor_copy(ends[:], base[:, c0, :]))
            if c0 == 0:
                dve.seq(nc.vector.tensor_copy(base[:, 0, :], base[:, 1, :]))
        if kind == "gelu":
            dve.seq(nc.vector.tensor_scalar(tot[:, 0, :, :], rank[:], float(CAP), None, ALU.is_le))
            dve.seq(nc.vector.tensor_tensor(oh[:], oh[:], tot[:, 0, :, :], ALU.mult))
        bb = base[:, 0:1, :].to_broadcast([P, K * NT, NE])
        dve.seq(nc.vector.tensor_tensor(rank[:], rank[:], bb, ALU.add))
        dve.seq(nc.vector.tensor_scalar(rank[:], rank[:], -1.0, None, ALU.add))
        dve.seq(nc.vector.tensor_tensor(rank[:], rank[:], oh[:], ALU.mult))
        dve.seq(nc.vector.tensor_reduce(slot_f[:], rank[:], AX.X, ALU.add))
        dve.seq(nc.vector.tensor_reduce(valid[:], oh[:], AX.X, ALU.add))
        dve.do(nc.vector.tensor_copy(slot_u[:], slot_f[:]))
        dve.do(nc.vector.tensor_tensor(wk[:], wk[:], valid[:], ALU.mult))
        dve.seq(nc.vector.tensor_scalar(valid[:], valid[:], -1.0, 1.0, ALU.mult, ALU.add))
        dve.seq(nc.vector.tensor_tensor(valid[:], valid[:], cst["aside"][:, 0:K * NT], ALU.mult))
        dve.seq(nc.vector.tensor_tensor(slot_f[:], slot_f[:], valid[:], ALU.add))
        placed = dve.seq(nc.vector.tensor_copy(to_u[:], slot_f[:]))
        dve.seq(nc.vector.tensor_scalar(wk[:], wk[:], gate, None, ALU.mult))
        sc_s = pg.stream("scatter")
        pool.wait(dram["zeroed"], placed, xn_made)
        for n in range(NT):
            for k in range(K):
                sc_s.after(nc.gpsimd.indirect_dma_start(
                    out=xs, out_offset=bass.IndirectOffsetOnAxis(ap=to_u[:, k * NT + n:k * NT + n + 1], axis=0),
                    in_=xn[:, n, :], in_offset=None))
        sent = sc_s.now()
        sp.wait(sent)

        te = sb("te", [1, 2, 64])
        dve.seq(nc.vector.tensor_scalar(te[:, 0, :], cst["starts"][0:1, :], ends[0:1, 0:1], None, ALU.is_ge))
        for e in range(1, NE - 1):
            dve.seq(nc.vector.scalar_tensor_tensor(te[:, e % 2, :], cst["starts"][0:1, :], ends[0:1, e:e + 1],
                                                   te[:, 1 - e % 2, :], ALU.is_ge, ALU.add))
        routed = dve.seq(nc.vector.tensor_copy(tile_e[:], te[:, (NE - 2) % 2, :]))

        wl = [pg.stream("wl0"), pg.stream("wl1")]
        xl, yl = [pg.stream("xl0"), pg.stream("xl1")], [pg.stream("yl0"), pg.stream("yl1")]
        for e in range(NE):
            pe.wait(ld[e].now())
        pool.wait(sent, routed)
        pe.wait(routed)
        act.wait(routed)
        dve.wait(routed)
        st = dict(w1=[None, None], arrived=[None, None], xT=[None, None], xTt=[None, None], h=[None, None])

        def load(m, p):
            sp.wait(used["x"][p])
            st["arrived"][p] = sp.dma(xl[p], xt[:, p, :], xs[bass.ds(m * P, P), :])

        def turn(p):
            act.wait(used["xT"][p])
            st["xTt"][p] = transposed(pg, t_ring, xtT[:, p, :, :], xt[:, p, :], cst, st["arrived"][p])
            used["x"][p] = pe.done.now()

        def expert_of(eng, m):
            return eng.eng.value_load(tile_e[0:1, bass.ds(m, 1)], min_val=0, max_val=NE - 1)

        def weights(m, p):
            e = expert_of(pool, m)
            pool.wait(used["w1"][p])
            st["w1"][p] = wl[p].after(nc.gpsimd.dma_start(
                w1[:, p, :, :], w["w1"][bass.ds(e, 1), :, :].rearrange("a (c p) f -> p (a c) f", p=P)))

        def up(m, p):
            e = expert_of(act, m)
            pe.wait(st["xTt"][p], st["w1"][p])
            st["h"][p] = hidden(lambda c: xtT[:, p, c, :], p, e, p)
            used["xT"][p] = used["w1"][p] = pe.done.now()

        def down(m, p):
            e = (expert_of(pe, m), expert_of(dve, m))
            t = projected(e, p, st["h"][p], y[:, p, :], used["y"][p])
            sp.wait(t)
            used["y"][p] = sp.dma(yl[p], ys[bass.ds(m * P, P), :], y[:, p, :])

        dve.wait(dve.done.now())
        sp.wait(dve.do(nc.vector.memset(y[:], 0.0)))
        for p in range(2):
            used["y"][p] = sp.dma(yl[p], ys[(MOST + p) * P:(MOST + p + 1) * P, :], y[:, p, :])
            used["w1"][p] = pe.done.now()
            weights(p, p)
        load(0, 0)
        load(1, 1)
        turn(0)
        load(2, 0)
        turn(1)
        up(0, 0)
        weights(2, 0)
        load(3, 1)
        uid = pg.n_names
        rounds = (M - 1) // 2
        kept = [("used", k) for k in ("hT", "x", "xT", "y", "w1")] + [("st", k) for k in ("w1", "arrived", "xTt", "h")]
        where = {"used": used, "st": st}
        for e in pg.engines:
            e.wait(*[where[a][k][p] for a, k in kept for p in range(2)])
        with pg.loop(rounds) as i:
            for a, k in kept:
                for p in range(2):
                    where[a][k][p] = pg.last_round(f"{a}{k}{p}@{uid}")
            for p in (1, 0):
                m = i * 2 + (1 if p else 2)
                turn(1 - p)
                up(m, p)
                weights(m + 2, p)
                load(m + 3, 1 - p)
                down(m - 1, 1 - p)
            for a, k in kept:
                for p in range(2):
                    if where[a][k][p] is not None and not isinstance(where[a][k][p], LastRound):
                        pg.keep(f"{a}{k}{p}@{uid}", where[a][k][p])
        m = 2 * rounds + 1
        if m < M:
            up(m, 1)
            down(m - 1, 0)
            down(m, 1)
        else:
            down(m - 1, 0)
        AHEAD = 8
        yg = xn
        got = [pg.stream(f"got{p}") for p in range(AHEAD)]
        pool.wait(*used["y"])
        taken = [None] * AHEAD
        q = 0
        for n in range(NT):
            for k in range(K):
                p = q % AHEAD
                q += 1
                pool.wait(taken[p])
                t = got[p].after(nc.gpsimd.indirect_dma_start(
                    out=yg[:, p, :], out_offset=None, in_=ys[0:M * P, :],
                    in_offset=bass.IndirectOffsetOnAxis(ap=slot_u[:, k * NT + n:k * NT + n + 1], axis=0)))
                dve.wait(t, dve.done.now())
                taken[p] = dve.do(nc.vector.scalar_tensor_tensor(
                    x[:, n, :], yg[:, p, :], wk[:, k * NT + n:k * NT + n + 1], x[:, n, :], ALU.mult, ALU.add))
        for r in (h_ring, t_ring, y_ring):
            pg.rings.remove(r)


def masked_keys(pg, cst, mask, maskrow, live):
    nc, pe, dve, sp = pg.nc, pg.pe, pg.dve, pg.sp
    with ExitStack() as ctx:
        mi = pg.sbuf(ctx, "mi", [B, S2], I32)
        off, any_, dg = pg.sbuf(ctx, "off", [B, S2]), pg.sbuf(ctx, "any", [B, 1]), pg.sbuf(ctx, "dg", [B, B])
        row = pg.sbuf(ctx, "row", [B, S2], BF16)
        ps = pg.psum(ctx, "ps", [P, B])
        ld = pg.stream("mask")
        sp.dma(ld, mi[:], mask.rearrange("b x y k -> (b x y) k"))
        dve.wait(ld.now())
        dve.seq(nc.vector.tensor_copy(off[:], mi[:]))
        dve.seq(nc.vector.tensor_scalar(off[:], off[:], 0.0, None, ALU.is_equal))
        dve.seq(nc.vector.tensor_reduce(any_[:], off[:], AX.X, ALU.min))
        dve.seq(nc.vector.tensor_scalar(any_[:], any_[:], -1.0, 1.0, ALU.mult, ALU.add))
        dve.seq(nc.vector.tensor_scalar(off[:], off[:], any_[:, 0:1], -1e30, ALU.mult, ALU.mult))
        t = dve.seq(nc.vector.tensor_copy(row[:], off[:]))
        sp.wait(t)
        st = pg.stream("maskrow")
        out = sp.dma(st, maskrow, row[:])
        t = dve.seq(nc.vector.tensor_scalar(dg[:], cst["ident"][0:B, 0:B], any_[:, 0:1], None, ALU.mult))
        pe.wait(t)
        t = pe.do(nc.tensor.matmul(ps[:], cst["ones"][0:B, :], dg[:], start=True, stop=True))
        dve.wait(t)
        dve.seq(nc.vector.tensor_copy(live[:], ps[:]))
        sp.wait(out)
        return out


def build(nc, a, loops):
    with ExitStack() as ctx:
        pg = Program(nc, ctx, loops)
        pe, act, dve, pool, sp = pg.pe, pg.act, pg.dve, pg.pool, pg.sp
        x, xnT = pg.sbuf(ctx, "x", [P, NT, D]), pg.sbuf(ctx, "xnT", [P, DC, N])
        cst = {n: pg.sbuf(ctx, n, s) for n, s in (
            ("ident", [P, P]), ("sel", [P, P]), ("tri", [P, P]), ("ones", [P, P]), ("mhalf", [P, NT]),
            ("iota_e", [P, 2 * NT * NE]), ("aside", [P, 2 * NT]), ("starts", [1, 64]), ("mv", [P, NT, 2]), ("rstd", [P, NT]))}
        cst["identb"] = pg.sbuf(ctx, "identb", [P, P], BF16)
        zero = pg.sbuf(ctx, "zero", [P, D])
        gates, live = pg.sbuf(ctx, "gates", [P, 8]), pg.sbuf(ctx, "live", [P, B])
        dram = {}
        for n, s, dt in (("xs", [XTILES * P + 2 * N, D], F32), ("ys", [XTILES * P, D], F32), ("kparts", [3, D, S2], BF16),
                         ("qparts", [3, D, T], BF16), ("maskrow", [B, S2], BF16)):
            dram[n] = nc.dram_tensor(n, s, dt).ap()

        ld = pg.stream("constants")
        for n in ("ident", "sel", "tri", "iota_e", "aside", "starts"):
            sp.dma(ld, cst[n][:], a[n])
        sp.dma(ld, x[:], a["x"].rearrange("b (t p) d -> p (b t) d", p=P))
        with nc.allow_non_contiguous_dma("8 numbers"):
            for k, n in enumerate(("g_xattn", "g_ffn")):
                sp.dma(ld, gates[:, 4 * k:4 * k + 4], a[n].rearrange("(a n) -> a n", a=1).to_broadcast([P, 4]))
        for e in (dve, act, pe, pool):
            e.wait(ld.now())
        dve.do(nc.vector.memset(cst["ones"][:], 1.0))
        dve.do(nc.vector.memset(cst["mhalf"][:], -0.5))
        dve.do(nc.vector.tensor_copy(cst["identb"][:], cst["ident"][:]))
        dve.wait(act.do(nc.scalar.activation(gates[:], gates[:], ACT.Tanh)))
        for e in (dve, act, pe, pool):
            e.wait(dve.done.now())

        with ExitStack() as c:
            dve.do(nc.vector.memset(zero[:], 0.0))
            masked = masked_keys(pg, cst, a["mask"], dram["maskrow"], live)
            for e in pg.engines:
                e.wait(dve.done.now(), masked)

        def norm(psum, stats, xn):
            return normalised(pg, x, xnT, cst, psum, stats, xn)

        def clear():
            zs = pg.stream("zeroed")
            for n in range(XTILES):
                sp.dma(zs, dram["xs"][P * n:P * n + P, :], zero[:])
            dram["zeroed"] = zs.now()

        for layer in range(4):
            w = {n: a[f"L{layer}_{n}"] for n in ("wq", "bq", "wk", "bk", "wv", "bo") + (("woa", "bva") if layer < 3 else ("wo", "bv"))}
            if layer == 1:
                w |= {n: a[f"L1_{n}"] for n in ("wqr", "bqr", "wkr", "bkr")}
            w |= dict(ctxT=a["ctxT"], kparts=dram["kparts"], qparts=dram["qparts"])
            g_x, g_f = gates[:, layer:layer + 1], gates[:, 4 + layer:5 + layer]
            if layer < 3:
                head_attention(pg, x, xnT, cst, w, g_x, 1 / 16 if layer == 2 else 1 / 4, norm,
                               a["rope"] if layer == 1 else None, (dram["maskrow"], live) if layer else None)
            else:
                wide_attention(pg, x, xnT, cst, w, g_x, norm)
            if layer == 0:
                quantised_linear(pg, x, xnT, cst, a["L0_weight"], a["hadamard"], g_f, norm, clear)
            else:
                names = ("gate", "w1", "b1", "w2", "b2") if layer < 3 else ("gw1", "gb1", "gw2", "gb2", "w1", "b1", "w2", "b2")
                experts(pg, x, xnT, cst, {n: a[f"L{layer}_{n}"] for n in names}, g_f,
                        (None, "relu", "gelu", "selu")[layer], dram, norm)
        pg.barrier()
        o = pg.stream("out")
        sp.dma(o, a["out"].rearrange("b (t p) d -> p (b t) d", p=P), x[:])
        sp.wait(o.now())
        sp.flush()
        return pg.measured


def constants():
    f = np.float32
    c = {"ident": np.eye(P, dtype=f)}
    p = np.arange(P)
    c["sel"] = (p[:, None] == 32 * (p[None, :] // 32) + HD).astype(f)
    c["tri"] = (p[:, None] <= p[None, :]).astype(f)
    c["iota_e"] = np.tile(np.arange(NE, dtype=f), (P, 2 * NT))
    c["aside"] = (XTILES * P + P * np.arange(2 * NT)[None, :] + p[:, None]).astype(f)
    c["starts"] = (P * np.arange(64, dtype=f))[None, :]
    inv = f(1.0) / f(10000.0) ** (np.arange(0, HD, 2, dtype=f) / f(HD))
    emb = np.arange(S2, dtype=f)[:, None] * inv[None, :]
    emb = np.concatenate([emb, emb], axis=-1).T
    sign = np.where(np.arange(HD) < HD // 2, -1, 1).astype(f)[:, None]
    c["rope"] = np.ascontiguousarray(np.tile(np.stack([np.cos(emb), np.sin(emb) * sign], 1), (P // HD, 1, 1)))
    h = np.array([[1.0]])
    while h.shape[0] < D:
        h = np.block([[h, h], [h, -h]])
    c["hadamard"] = (h / np.sqrt(D)).astype(f)
    return c


def laid_out(i):
    out = dict(x=i["x"], ctxT=i["ctx_1024"].transpose(0, 2, 1), mask=i["mask_Bx1x1xS2_if1"], g_xattn=i["g_xattn"],
               g_ffn=i["g_ffn"], L0_weight=i["L0_ffn_weight"])
    for n in range(4):
        for m in "qkvo":
            w = i[f"L{n}_xattn_W{m}"]
            out[f"L{n}_w{m}"] = w.T if n in (0, 2) else w
            out[f"L{n}_b{m}"] = i[f"L{n}_xattn_b{m}"]
        if n < 3:
            wide = np.zeros((P, H // HG, D), np.float32)
            wide.reshape(HG, P // HG, H // HG, D)[:, 0:HD] = out[f"L{n}_wo"].reshape(-1, HG, HD, D).transpose(1, 2, 0, 3)
            out[f"L{n}_woa"] = wide
            wide = np.zeros((P, H // HG), np.float32)
            wide.reshape(HG, P // HG, H // HG)[:, 0:HD] = out[f"L{n}_bv"].reshape(-1, HG, HD).transpose(1, 2, 0)
            out[f"L{n}_bva"] = wide
    halves = (HD * np.arange(H)[:, None] + np.roll(np.arange(HD), HD // 2)[None, :]).reshape(-1)
    for m in "qk":
        out[f"L1_w{m}r"], out[f"L1_b{m}r"] = out[f"L1_w{m}"][:, halves], out[f"L1_b{m}"][halves]
    out["L1_gate"], out["L2_gate"] = i["L1_ffn_gate_w"].T, i["L2_ffn_wg"]
    for n in (1, 2):
        for m in ("w1", "b1", "w2", "b2"):
            out[f"L{n}_{m}"] = i[f"L{n}_ffn_{m}"]
    for k, m in (("w1", "wi"), ("b1", "bi"), ("w2", "wo"), ("b2", "bo")):
        out[f"L3_g{k}"], out[f"L3_{k}"] = i[f"L3_ffn_gate_{m}"], i[f"L3_ffn_exp_{m}"]
    for n in [n for n in out if n[3:] in ("bq", "bk", "bqr", "bkr")]:
        out[n] = out[n].reshape(DC, P).T
    for n in ("L1_b1", "L2_b1", "L3_b1"):
        out[n] = out[n].reshape(NE, FC, P).transpose(2, 0, 1)
    out["L3_gb1"] = out["L3_gb1"].reshape(FC, P).T
    for n in ("L1_gate", "L2_gate"):
        out[n] = out[n].reshape(DC, P, NE).transpose(1, 0, 2)
    return {n: np.ascontiguousarray(a) for n, a in out.items()}


def kernel(**inputs):
    import concourse.bacc as bacc
    from concourse.bass_utils import run_bass_kernel_spmd

    arrays = laid_out({n: np.asarray(v) for n, v in inputs.items()}) | constants()

    def program(loops):
        nc = bacc.Bacc("TRN2", target_bir_lowering=False, num_devices=1)
        a = {n: nc.dram_tensor(f"in_{n}", v.shape, mybir.dt.from_np(v.dtype), kind="ExternalInput").ap()
             for n, v in arrays.items()}
        a["out"] = nc.dram_tensor("out_x", (B, T, D), F32, kind="ExternalOutput").ap()
        return nc, build(nc, a, loops)

    _, loops = program([])
    nc, _ = program(loops)
    r = run_bass_kernel_spmd(nc, [{f"in_{n}": v for n, v in arrays.items()}], core_ids=[0])
    return r.results[0]["out_x"]
```
